# Optimizing a Trainium2 kernel written in Bass

```python
import numpy as np
import jax
import jax.numpy as jnp

def _softmax(x, axis=-1):
    return jax.nn.softmax(x, axis=axis)

def _gelu(x):
    return jax.nn.gelu(x, approximate=True)

def _silu(x):
    return jax.nn.silu(x)

def _sigmoid(x):
    return jax.nn.sigmoid(x)

def _layernorm(x, axis=-1, eps=1e-05):
    m = jnp.mean(x, axis=axis, keepdims=True)
    v = jnp.var(x, axis=axis, keepdims=True)
    return (x - m) / jnp.sqrt(v + eps)

def _scatter_add(tgt, idx, src, axis=0):
    return tgt.at[idx].add(src)

def _segment_sum(src, seg, n):
    return jax.ops.segment_sum(src, seg, n)
kernel_name = 'mk_decoder_postln_d1_seqx_r4_eaffb5'

def setup_inputs(seed: int=0):
    np.random.seed(seed)
    _w = jnp.asarray

    def _rec_inputs():
        import jax
        import jax.numpy as jnp
        _rk = jax.random.key(seed)
        x = 7.22e-05 + 1 * jax.random.normal(jax.random.fold_in(_rk, 1), (8, 512, 256), jnp.float32)
        _lenS = 512 - jax.random.randint(jax.random.fold_in(_rk, 7), (8,), 0, max(1, 512 // 4) + 1, jnp.int32)
        _lenS2 = 512 - jax.random.randint(jax.random.fold_in(_rk, 8), (8,), 0, max(1, 512 // 4) + 1, jnp.int32)
        _ctx_1024P = jax.random.normal(jax.random.fold_in(_rk, 11), (8, 16, 256), jnp.float32)
        _ctx_1024c = jax.random.dirichlet(jax.random.fold_in(_rk, 511), 0.3 * jnp.ones((16,), jnp.float32), (8, 512))
        _ctx_1024t = jnp.einsum('bsk,bkd->bsd', _ctx_1024c, _ctx_1024P)
        _ctx_1024t = _ctx_1024t * jax.lax.rsqrt(jnp.mean(jnp.square(_ctx_1024t)) + 1e-12) * 0.953939
        ctx_1024 = 4.13588e-05 + 0.999923 * (_ctx_1024t + 0.3 * jax.random.normal(jax.random.fold_in(_rk, 611), (8, 512, 256), jnp.float32))
        _validS = jnp.arange(512)[None, :] < _lenS[:, None]
        _validS2 = jnp.arange(512)[None, :] < _lenS2[:, None]
        _causal = jnp.tril(jnp.ones((512, 512), dtype=bool))
        mask_BxS2_bf1 = jnp.ones((8, 512), dtype=bool)
        return (x, ctx_1024, mask_BxS2_bf1)
    x, ctx_1024, mask_BxS2_bf1 = _rec_inputs()

    def _L0_attn_setup():
        import jax, jax.numpy as jnp
        import numpy as np
        CHUNK = 32
        key = jax.random.key(seed)
        ks = jax.random.split(key, 7)
        B, T, D = (4, 2048, 256)
        s = 1.0 / np.sqrt(D)
        return {'x': jax.random.normal(ks[0], (B, T, D), jnp.float32), 'W_q': jax.random.normal(ks[1], (D, D), jnp.float32) * s, 'W_k': jax.random.normal(ks[2], (D, D), jnp.float32) * s, 'W_v': jax.random.normal(ks[3], (D, D), jnp.float32) * s, 'W_g': jax.random.normal(ks[4], (D, D), jnp.float32) * s, 'W_o': jax.random.normal(ks[5], (D, D), jnp.float32) * s, 'log_decay': jax.random.normal(ks[6], (D,), jnp.float32) * 0.1}
    _L0_attn_all = _L0_attn_setup()
    _L0_attn_in = {k: v for k, v in _L0_attn_all.items() if k in ('W_q', 'W_k', 'W_v', 'W_g', 'W_o', 'log_decay')}
    del _L0_attn_all

    def _L0_xattn_setup():
        import jax, jax.numpy as jnp
        import numpy as np
        HEADS, QSIZE, KSIZE = (16, 64, 64)
        key = jax.random.key(seed)
        ks = jax.random.split(key, 8)
        B, S, D = (4, 512, 256)
        sd = 1.0 / np.sqrt(D)
        return {'q_in': jax.random.normal(ks[0], (B, S, D), jnp.float32), 'k_in': jax.random.normal(ks[1], (B, S, D), jnp.float32), 'v_in': jax.random.normal(ks[2], (B, S, D), jnp.float32), 'key_mask': jnp.ones((B, S), dtype=bool), 'Wq': jax.random.normal(ks[3], (D, HEADS * QSIZE), jnp.float32) * sd, 'bq': jnp.zeros((HEADS * QSIZE,), jnp.float32), 'Wk': jax.random.normal(ks[4], (D, HEADS * QSIZE), jnp.float32) * sd, 'bk': jnp.zeros((HEADS * QSIZE,), jnp.float32), 'Wv': jax.random.normal(ks[5], (D, HEADS * KSIZE), jnp.float32) * sd, 'bv': jnp.zeros((HEADS * KSIZE,), jnp.float32), 'Wo': jax.random.normal(ks[6], (HEADS * KSIZE, D), jnp.float32) * sd, 'bo': jnp.zeros((D,), jnp.float32)}
    _L0_xattn_all = _L0_xattn_setup()
    _L0_xattn_in = {k: v for k, v in _L0_xattn_all.items() if k in ('Wq', 'bq', 'Wk', 'bk', 'Wv', 'bv', 'Wo', 'bo')}
    del _L0_xattn_all

    def _L0_ffn_setup():
        import jax, jax.numpy as jnp
        import numpy as np

        def _bitlinear(x, w_latent):
            scale = jax.lax.stop_gradient(jnp.clip(jnp.mean(jnp.abs(w_latent), axis=1, keepdims=True), 1e-05, None))
            tern = jnp.clip(jnp.round(w_latent / scale), -1.0, 1.0)
            w = w_latent + jax.lax.stop_gradient(tern - w_latent)
            return x @ (w * scale).T
        key = jax.random.key(seed)
        ks = jax.random.split(key, 6)
        dim, hidden, rank = (256, 1024, 16)
        B, S = (4, 1024)
        x = jax.random.normal(ks[0], (B, S, dim), dtype=jnp.float32)
        w_fc = 0.02 * jax.random.normal(ks[1], (hidden, dim), dtype=jnp.float32)
        w_proj = 0.02 * jax.random.normal(ks[2], (dim, hidden), dtype=jnp.float32)
        u = 0.02 * jax.random.normal(ks[3], (hidden, rank), dtype=jnp.float32)
        v = 0.02 * jax.random.normal(ks[4], (rank, dim), dtype=jnp.float32)
        fast_b = jax.random.normal(ks[5], (rank, rank), dtype=jnp.float32)
        gate = jnp.float32(0.05)
        return {'x': x, 'fast_b': fast_b, 'w_fc': w_fc, 'w_proj': w_proj, 'u': u, 'v': v, 'gate': gate}
    _L0_ffn_all = _L0_ffn_setup()
    _L0_ffn_in = {k: v for k, v in _L0_ffn_all.items() if k in ('fast_b', 'w_fc', 'w_proj', 'u', 'v', 'gate')}
    del _L0_ffn_all
    return {'x': x, 'ctx_1024': ctx_1024, 'mask_BxS2_bf1': mask_BxS2_bf1, 'L0_attn_W_q': _L0_attn_in['W_q'], 'L0_attn_W_k': _L0_attn_in['W_k'], 'L0_attn_W_v': _L0_attn_in['W_v'], 'L0_attn_W_g': _L0_attn_in['W_g'], 'L0_attn_W_o': _L0_attn_in['W_o'], 'L0_attn_log_decay': _L0_attn_in['log_decay'], 'L0_xattn_Wq': _L0_xattn_in['Wq'], 'L0_xattn_bq': _L0_xattn_in['bq'], 'L0_xattn_Wk': _L0_xattn_in['Wk'], 'L0_xattn_bk': _L0_xattn_in['bk'], 'L0_xattn_Wv': _L0_xattn_in['Wv'], 'L0_xattn_bv': _L0_xattn_in['bv'], 'L0_xattn_Wo': _L0_xattn_in['Wo'], 'L0_xattn_bo': _L0_xattn_in['bo'], 'L0_ffn_fast_b': _L0_ffn_in['fast_b'], 'L0_ffn_w_fc': _L0_ffn_in['w_fc'], 'L0_ffn_w_proj': _L0_ffn_in['w_proj'], 'L0_ffn_u': _L0_ffn_in['u'], 'L0_ffn_v': _L0_ffn_in['v'], 'L0_ffn_gate': _L0_ffn_in['gate']}

def reference(x, ctx_1024, mask_BxS2_bf1, L0_attn_W_q, L0_attn_W_k, L0_attn_W_v, L0_attn_W_g, L0_attn_W_o, L0_attn_log_decay, L0_xattn_Wq, L0_xattn_bq, L0_xattn_Wk, L0_xattn_bk, L0_xattn_Wv, L0_xattn_bv, L0_xattn_Wo, L0_xattn_bo, L0_ffn_fast_b, L0_ffn_w_fc, L0_ffn_w_proj, L0_ffn_u, L0_ffn_v, L0_ffn_gate):
    import jax
    import jax.numpy as jnp

    def _L0_attn_ref(x, W_q, W_k, W_v, W_g, W_o, log_decay):
        import jax, jax.numpy as jnp
        import numpy as np
        CHUNK = 32
        B, T, D = x.shape
        C = CHUNK
        nc = T // C
        Q = x @ W_q.T
        K = x @ W_k.T
        V = x @ W_v.T
        decay = jax.lax.stop_gradient(jax.nn.sigmoid(log_decay[0]))
        pos = jnp.arange(C, dtype=x.dtype)
        diff = pos[:, None] - pos[None, :]
        mask = jnp.where(diff >= 0, decay ** diff, jnp.zeros((), x.dtype))
        Qc = Q.reshape(B, nc, C, D)
        Kc = K.reshape(B, nc, C, D)
        Vc = V.reshape(B, nc, C, D)
        S = jnp.einsum('bncd,bnkd->bnck', Qc, Kc) * mask
        O = jnp.einsum('bnck,bnkd->bncd', S, Vc).reshape(B, T, D)
        gate = jax.nn.sigmoid(x @ W_g.T)
        out = gate * O @ W_o.T + x
        return out

    def _L0_xattn_ref(q_in, k_in, v_in, key_mask, Wq, bq, Wk, bk, Wv, bv, Wo, bo):
        import jax, jax.numpy as jnp
        import numpy as np
        HEADS, QSIZE, KSIZE = (16, 64, 64)
        B, M, _ = q_in.shape
        N = k_in.shape[1]
        qw = (q_in @ Wq + bq).reshape(B, M, HEADS, QSIZE)
        kw = (k_in @ Wk + bk).reshape(B, N, HEADS, QSIZE)
        vw = (v_in @ Wv + bv).reshape(B, N, HEADS, KSIZE)
        a = jnp.einsum('bmhd,bnhd->bhmn', qw, kw) / jnp.sqrt(jnp.float32(QSIZE))
        a = jnp.where(key_mask[:, None, None, :], a, -jnp.inf)
        a = jax.nn.softmax(a, axis=-1)
        o = jnp.einsum('bhmn,bnhd->bmhd', a, vw).reshape(B, M, HEADS * KSIZE)
        return o @ Wo + bo

    def _L0_ffn_ref(x, fast_b, w_fc, w_proj, u, v, gate):
        import jax, jax.numpy as jnp
        import numpy as np

        def _bitlinear(x, w_latent):
            scale = jax.lax.stop_gradient(jnp.clip(jnp.mean(jnp.abs(w_latent), axis=1, keepdims=True), 1e-05, None))
            tern = jnp.clip(jnp.round(w_latent / scale), -1.0, 1.0)
            w = w_latent + jax.lax.stop_gradient(tern - w_latent)
            return x @ (w * scale).T
        h = _bitlinear(x, w_fc) + gate * (x @ v.T @ fast_b.T @ u.T)
        r = jnp.maximum(h, 0.0)
        return _bitlinear(r * r, w_proj)
    x = _layernorm(x + _L0_attn_ref(x, L0_attn_W_q, L0_attn_W_k, L0_attn_W_v, L0_attn_W_g, L0_attn_W_o, L0_attn_log_decay), axis=-1)
    x = _layernorm(x + _L0_xattn_ref(x, ctx_1024, ctx_1024, mask_BxS2_bf1, L0_xattn_Wq, L0_xattn_bq, L0_xattn_Wk, L0_xattn_bk, L0_xattn_Wv, L0_xattn_bv, L0_xattn_Wo, L0_xattn_bo), axis=-1)
    x = _layernorm(x + _L0_ffn_ref(x, L0_ffn_fast_b, L0_ffn_w_fc, L0_ffn_w_proj, L0_ffn_u, L0_ffn_v, L0_ffn_gate), axis=-1)
    return x

_drawn_inputs = setup_inputs


def setup_inputs(seed=0):
    import zlib

    import numpy as np

    out = dict(_drawn_inputs(seed))
    spreads = {'L0_xattn_bq': (0.0, 0.1),
     'L0_xattn_bk': (0.0, 0.8),
     'L0_xattn_bv': (0.0, 0.1),
     'L0_xattn_bo': (0.0, 0.1)}
    factors = {'L0_ffn_fast_b': 8.0, 'L0_ffn_u': 8.0, 'L0_ffn_v': 8.0}
    for name, (base, spread) in spreads.items():
        noise = np.random.default_rng([zlib.crc32(name.encode()), seed]).standard_normal(out[name].shape)
        drawn = base * np.exp(spread * noise) if base else spread * noise
        out[name] = jnp.asarray(drawn.astype(out[name].dtype))
    for name, factor in factors.items():
        out[name] = (out[name] * factor).astype(out[name].dtype)
    return out
```

```python
from contextlib import ExitStack

import concourse.bass as bass
from concourse import mybir

ACT = mybir.ActivationFunctionType
ALU = mybir.AluOpType
AX = mybir.AxisListType
F32 = mybir.dt.float32
F32R = mybir.dt.float32r
BF16 = mybir.dt.bfloat16
U8 = mybir.dt.uint8

P = 128
B, T, D = 8, 512, 256
DK = D // P
NT = T // P
CHUNK = 32
HEADS, DH = 16, 64
HD = HEADS * DH
PAIRS = HEADS // 2
HID = 1024
HK = HID // P
RANK = 16
EPS = 1e-5
MASKED = -1e30
LOWEST = -3e38
SCALE = DH ** -0.5


def split_matmul(pe, out, terms):
    n = len(terms)
    for i, (lh, ll, rh, rl) in enumerate(terms):
        pe.matmul(out, lh, rh, start=(i == 0), stop=False)
        pe.matmul(out, lh, rl, start=False, stop=False)
        mm = pe.matmul(out, ll, rh, start=False, stop=(i == n - 1))
    return mm


def full_matmul(pe, out, terms):
    for i, (l, r) in enumerate(terms):
        mm = pe.matmul(out, l, r, start=(i == 0), stop=(i == len(terms) - 1))
    return mm


def f32(ap):
    return ap.bitcast(F32)


def batch_cols(dram, b):
    v = dram.rearrange("(k p) (b t) -> b p k t", p=P, t=T)
    if isinstance(b, int):
        return v[b]
    return v[bass.ds(b, 1)].rearrange("b p k t -> (b p) k t")


def row_of(dram, b):
    return dram[b:b + 1, :] if isinstance(b, int) else dram[bass.ds(b, 1), :]


def decoder_layer(nc, a, out):
    x1_dram = nc.dram_tensor("x1_scratch", [D, B * T], F32, kind="Internal").ap()
    y2_dram = nc.dram_tensor("y2_scratch", [D, B * T], F32, kind="Internal").ap()
    with ExitStack() as whole:
        def sb(ctx, name, shape, dt):
            return ctx.enter_context(nc.sbuf_tensor(name, shape, dt))

        c = {}
        c["mean_w"] = sb(whole, "mean_w", [P, P], F32)
        c["ones_w"] = sb(whole, "ones_w", [P, P], F32)
        c["ident"] = sb(whole, "ident", [P, P], BF16)
        c["eps"] = sb(whole, "eps", [P, 1], F32)
        for w in ("wq", "wk", "wv"):
            c[w + "_hi"] = sb(whole, w + "_hi", [P, DK, HD], F32R)
            c[w + "_lo"] = sb(whole, w + "_lo", [P, DK, HD], F32R)
        c["wo"] = sb(whole, "wo", [P, PAIRS, D], F32)
        c["bq"] = sb(whole, "bq", [P, PAIRS], F32)
        c["bk"] = sb(whole, "bk", [P, PAIRS], F32)
        c["bo"] = sb(whole, "bo", [P, DK], F32)
        c["bv"] = sb(whole, "bv", [P, HD], F32)
        ps = whole.enter_context(nc.psum_tensor("ps", [P, 8, T], F32))
        with ExitStack() as ctx:
            linear_attention_phase(nc, ctx, sb, a, c, ps, x1_dram)
        with ExitStack() as ctx:
            cross_attention_phase(nc, ctx, sb, a, c, ps, x1_dram, y2_dram)
        with ExitStack() as ctx:
            ffn_phase(nc, ctx, sb, a, c, ps, y2_dram, out)


def linear_attention_phase(nc, ctx, sb, a, c, ps, x1_dram):
    def sem(name):
        return ctx.enter_context(nc.semaphore("a_" + name))

    ident_f = sb(ctx, "ident_f", [P, P], F32)
    bits = sb(ctx, "bits", [P, 6, P], F32)
    nbits = sb(ctx, "nbits", [P, 5, P], F32)
    decay = sb(ctx, "decay", [P, 6], F32)
    factor = sb(ctx, "factor", [P, P], F32)
    dmask = sb(ctx, "dmask", [P, P], F32)
    raw = {w: sb(ctx, w + "_l0", [P, DK, D], F32) for w in ("Wq", "Wk", "WvT", "WgT", "WoT")}
    wv = raw["WvT"]
    w_hi = {w: sb(ctx, w + "_l0_hi", [P, DK, D], F32R) for w in ("M", "WgT", "WoT")}
    w_lo = {w: sb(ctx, w + "_l0_lo", [P, DK, D], F32R) for w in ("M", "WgT", "WoT")}
    stage = sb(ctx, "stage", [P, DK, HD], F32)
    x = sb(ctx, "x_in", [P, 2, DK, T], F32)
    x_hi = sb(ctx, "x_hi", [P, DK, T], F32R)
    x_lo = sb(ctx, "x_lo", [P, DK, T], F32R)
    qm = sb(ctx, "qm", [P, DK, T], F32)
    gate = sb(ctx, "gate", [P, DK, T], F32)
    v = sb(ctx, "v_tok", [P, NT, D], F32)
    s = sb(ctx, "s_masked", [P, NT, P], F32)
    og = sb(ctx, "og", [P, DK, T], F32)
    og_hi = sb(ctx, "og_hi", [P, DK, T], F32R)
    og_lo = sb(ctx, "og_lo", [P, DK, T], F32R)
    y = sb(ctx, "y_a", [P, DK, T], F32)
    dev = sb(ctx, "dev_a", [P, DK, T], F32)
    sq = sb(ctx, "sq_a", [P, DK, T], F32)
    sd = sb(ctx, "sd_a", [P, T], F32)
    rs = sb(ctx, "rs_a", [P, T], F32)
    x1 = sb(ctx, "x1_a", [P, DK, T], F32)

    consts_in, w_in, vec_in, stage_in = sem("consts_in"), sem("w_in"), sem("vec_in"), sem("stage_in")
    setup, decay_in, sig_done = sem("setup"), sem("decay_in"), sem("sig_done")
    pow_step, m_ps, w_split = sem("pow_step"), sem("m_ps"), sem("w_split")
    stage_split = sem("stage_split")
    x_in, x_split = [sem("x_in_even"), sem("x_in_odd")], sem("x_split")
    qm_ps, qm_out, g_ps, g_out = sem("qm_ps"), sem("qm_out"), sem("g_ps"), sem("g_out")
    v_ps, v_out, s_ps, s_out = sem("v_ps"), sem("v_out"), sem("s_ps"), sem("s_out")
    o_ps, og_done, y_ps, y_out = sem("o_ps"), sem("og_done"), sem("y_ps"), sem("y_out")
    mean_ps, dev_out, sq_out, var_ps = sem("mean_ps"), sem("dev_out"), sem("sq_out"), sem("var_ps")
    sd_out, rs_out, x1_out, stored = sem("sd_out"), sem("rs_out"), sem("x1_out"), sem("stored")
    STAGED = ("Wq", "Wk", "Wv")

    QO, G, VY, S, ST = ps[:, 0:2, :], ps[:, 2:4, :], ps[:, 4:6, :], ps[:, 6, :], ps[:, 7, :]

    with nc.Block() as block:
        @block.sync
        def _(sp):
            sp.dma_start(ident_f[:], a["ident"]).then_inc(consts_in, 16)
            sp.dma_start(bits[:], a["bits"]).then_inc(consts_in, 16)
            sp.dma_start(decay[:, 5:6], a["log_decay"][:, 0:1].partition_broadcast(P)).then_inc(decay_in, 16)
            for w in ("Wq", "Wk", "WgT", "WoT", "WvT"):
                sp.dma_start(raw[w][:], a["l0_" + w].rearrange("(k p) n -> p k n", p=P)).then_inc(w_in, 16)
            for b in range(2):
                sp.dma_start(x[:, b], batch_cols(a["xT"], b)).then_inc(x_in[b], 16)
            sp.dma_start(c["wo"][:], a["Wo"].rearrange("(k p) n -> p k n", p=P)).then_inc(vec_in, 16)
            sp.dma_start(c["bq"][:], a["bq"]).then_inc(vec_in, 16)
            sp.dma_start(c["bk"][:], a["bk"]).then_inc(vec_in, 16)
            sp.dma_start(c["bo"][:], a["bo"]).then_inc(vec_in, 16)
            sp.dma_start(c["bv"][:], a["bv"].partition_broadcast(P)).then_inc(vec_in, 16)
            for i, w in enumerate(STAGED):
                if i:
                    sp.wait_ge(stage_split, 2 * i)
                sp.dma_start(stage[:], a[w].rearrange("(k p) n -> p k n", p=P)).then_inc(stage_in, 16)

            def load_and_store(b, par):
                sp.wait_ge(y_out, 2 * b - 2)
                sp.dma_start(x[:, par], batch_cols(a["xT"], b)).then_inc(x_in[par], 16)
                sp.wait_ge(x1_out, b - 1)
                sp.dma_start(batch_cols(x1_dram, b - 2), x1[:]).then_inc(stored, 16)

            with sp.Fori(2, B - 1, 2) as b:
                load_and_store(b, 0)
                load_and_store(b + 1, 1)
            for b in (B - 2, B - 1):
                sp.wait_ge(x1_out, b + 1)
                sp.dma_start(batch_cols(x1_dram, b), x1[:]).then_inc(stored, 16)
            sp.wait_ge(stored, 16 * B)
            sp.wait_ge(vec_in, 16 * 5)

        @block.gpsimd
        def _(pool):
            for i, w in enumerate(("wq", "wk", "wv")):
                pool.wait_ge(stage_in, 16 * (i + 1))
                pool.tensor_copy(c[w + "_hi"][:], stage[:]).then_inc(stage_split, 1)
                pool.wait_ge(stage_split, 2 * i + 1)
                pool.tensor_tensor(c[w + "_lo"][:], stage[:], f32(c[w + "_hi"][:]),
                                   ALU.subtract).then_inc(stage_split, 1)

        @block.scalar
        def _(act):
            act.wait_ge(decay_in, 16)
            act.activation(decay[:, 0:1], decay[:, 5:6], ACT.Sigmoid).then_inc(sig_done, 1)

            def front(b):
                for m in range(DK):
                    act.wait_ge(qm_ps, 2 * b + m + 1)
                    if m == 0 and not (isinstance(b, int) and b == 0):
                        act.wait_ge(s_ps, b)
                    act.activation(qm[:, m], QO[:, m], ACT.Copy).then_inc(qm_out, 1)
                act.wait_ge(g_ps, b + 1)
                if not (isinstance(b, int) and b == 0):
                    act.wait_ge(og_done, 3 * b)
                act.activation(gate[:], G, ACT.Sigmoid).then_inc(g_out, 1)

            def square(b):
                act.wait_ge(dev_out, b + 1)
                act.activation(sq[:], dev[:], ACT.Square).then_inc(sq_out, 1)

            def values(b):
                act.wait_ge(v_ps, b + 1)
                act.activation(v[:], VY.rearrange("p a (t n) -> p (a t) n", n=D), ACT.Copy).then_inc(v_out, 1)

            def deviation(b):
                act.wait_ge(var_ps, b + 1)
                act.activation(sd[:], ST, ACT.Sqrt, bias=c["eps"][:, 0:1]).then_inc(sd_out, 1)

            front(0)
            values(0)
            front(1)
            square(0)
            values(1)
            deviation(0)
            with act.Fori(2, B - 1, 2) as i:
                for b in (i, i + 1):
                    front(b)
                    square(b - 1)
                    values(b)
                    deviation(b - 1)
            square(B - 1)
            deviation(B - 1)

        @block.vector
        def _(dve):
            dve.memset(c["mean_w"][:], 1.0 / D).then_inc(setup, 1)
            dve.memset(c["ones_w"][:], 1.0).then_inc(setup, 1)
            dve.memset(c["eps"][:], EPS).then_inc(setup, 1)

            def split_x(b, par):
                dve.wait_ge(x_in[par], 8 * (b - par) + 16)
                if not (isinstance(b, int) and b == 0):
                    dve.wait_ge(g_ps, b)
                dve.tensor_copy(x_hi[:], x[:, par]).then_inc(x_split, 1)
                dve.wait_ge(x_split, 2 * b + 1)
                dve.tensor_tensor(x_lo[:], x[:, par], f32(x_hi[:]), ALU.subtract).then_inc(x_split, 1)

            split_x(0, 0)
            for i, w in enumerate(("M", "WgT", "WoT")):
                if w == "M":
                    dve.wait_ge(m_ps, 1)
                    src = ps[:, 0, :].rearrange("p (k n) -> p k n", k=DK)
                else:
                    dve.wait_ge(w_in, 16 * 5)
                    src = raw[w][:]
                dve.tensor_copy(w_hi[w][:], src).then_inc(w_split, 1)
                dve.wait_ge(w_split, 2 * i + 1)
                dve.tensor_tensor(w_lo[w][:], src, f32(w_hi[w][:]), ALU.subtract).then_inc(w_split, 1)
            dve.wait_ge(consts_in, 32)
            dve.wait_ge(sig_done, 1)
            dve.tensor_copy(c["ident"][:], ident_f[:]).then_inc(setup, 1)
            dve.tensor_scalar(nbits[:], bits[:, 0:5, :], -1.0, 1.0, ALU.mult, ALU.add).then_inc(pow_step, 1)
            dve.tensor_copy(dmask[:], bits[:, 5, :]).then_inc(pow_step, 1)
            n = 2
            for j in range(5):
                dve.wait_ge(pow_step, n)
                dve.scalar_tensor_tensor(out=factor[:], in0=bits[:, j, :], scalar=decay[:, j:j + 1],
                                         in1=nbits[:, j, :], op0=ALU.mult, op1=ALU.add).then_inc(pow_step, 1)
                dve.wait_ge(pow_step, n + 1)
                dve.tensor_tensor(dmask[:], dmask[:], factor[:], ALU.mult).then_inc(pow_step, 1)
                n += 2
                if j < 4:
                    dve.tensor_tensor(decay[:, j + 1:j + 2], decay[:, j:j + 1], decay[:, j:j + 1],
                                      ALU.mult).then_inc(pow_step, 1)
                    n += 1
            dve.wait_ge(pow_step, n)

            def finish_y(b, par):
                for m in range(DK):
                    dve.wait_ge(y_ps, 2 * b + m + 1)
                    if m == 0 and not (isinstance(b, int) and b == 0):
                        dve.wait_ge(dev_out, b)
                    dve.scalar_tensor_tensor(out=y[:, m], in0=x[:, par, m], scalar=2.0, in1=VY[:, m],
                                             op0=ALU.mult, op1=ALU.add).then_inc(y_out, 1)

            def subtract_mean(b):
                dve.wait_ge(mean_ps, b + 1)
                dve.wait_ge(y_out, 2 * b + 2)
                if not (isinstance(b, int) and b == 0):
                    dve.wait_ge(x1_out, b)
                mean = ST.rearrange("p (o t) -> p o t", o=1).to_broadcast([P, DK, T])
                dve.tensor_tensor(dev[:], y[:], mean, ALU.subtract).then_inc(dev_out, 1)

            def mask_scores(b):
                dve.wait_ge(s_ps, b + 1)
                if not (isinstance(b, int) and b == 0):
                    dve.wait_ge(o_ps, 2 * b)
                dve.tensor_tensor(s[:], S.rearrange("p (t n) -> p t n", n=P),
                                  dmask[:].rearrange("p (o n) -> p o n", o=1).to_broadcast([P, NT, P]),
                                  ALU.mult).then_inc(s_out, 1)

            def normalise(b):
                dve.wait_ge(sd_out, b + 1)
                dve.reciprocal(rs[:], sd[:]).then_inc(rs_out, 1)
                dve.wait_ge(rs_out, b + 1)
                if not (isinstance(b, int) and b == 0):
                    dve.wait_ge(stored, 16 * b)
                dve.tensor_tensor(x1[:], dev[:], rs[:].rearrange("p (o t) -> p o t", o=1).to_broadcast([P, DK, T]),
                                  ALU.mult).then_inc(x1_out, 1)

            def gated(b):
                dve.wait_ge(o_ps, 2 * b + 2)
                dve.wait_ge(g_out, b + 1)
                dve.tensor_tensor(og[:], QO, gate[:], ALU.mult).then_inc(og_done, 1)
                dve.wait_ge(og_done, 3 * b + 1)
                if not (isinstance(b, int) and b == 0):
                    dve.wait_ge(y_ps, 2 * b)
                dve.tensor_copy(og_hi[:], og[:]).then_inc(og_done, 1)
                dve.wait_ge(og_done, 3 * b + 2)
                dve.tensor_tensor(og_lo[:], og[:], f32(og_hi[:]), ALU.subtract).then_inc(og_done, 1)

            mask_scores(0)
            split_x(1, 1)
            gated(0)
            finish_y(0, 0)
            subtract_mean(0)
            mask_scores(1)
            normalise(0)
            with dve.Fori(2, B - 1, 2) as i:
                for b, par in ((i, 0), (i + 1, 1)):
                    split_x(b, par)
                    gated(b - 1)
                    finish_y(b - 1, 1 - par)
                    subtract_mean(b - 1)
                    mask_scores(b)
                    normalise(b - 1)
            gated(B - 1)
            finish_y(B - 1, 1)
            subtract_mean(B - 1)
            normalise(B - 1)

        @block.tensor
        def _(pe):
            pe.wait_ge(w_in, 16 * 5)
            for m in range(DK):
                mm = full_matmul(pe, ps[:, 0, m * D:(m + 1) * D],
                                 [(raw["Wq"][:, k, m * P:(m + 1) * P], raw["Wk"][:, k, :]) for k in range(DK)])
            mm.then_inc(m_ps, 1)
            pe.wait_ge(w_split, 6)

            def project(bank, w, r_hi, r_lo, m):
                return split_matmul(pe, bank, [(w_hi[w][:, k, m * P:(m + 1) * P], w_lo[w][:, k, m * P:(m + 1) * P],
                                                r_hi[:, k], r_lo[:, k]) for k in range(DK)])

            def queries(b):
                pe.wait_ge(x_split, 2 * b + 2)
                if not (isinstance(b, int) and b == 0):
                    pe.wait_ge(og_done, 3 * b - 2)
                for m in range(DK):
                    project(QO[:, m], "M", x_hi, x_lo, m).then_inc(qm_ps, 1)

            def outputs(b):
                pe.wait_ge(og_done, 3 * b + 3)
                pe.wait_ge(v_out, b + 1)
                for m in range(DK):
                    project(VY[:, m], "WoT", og_hi, og_lo, m).then_inc(y_ps, 1)

            def gates(b):
                if not (isinstance(b, int) and b == 0):
                    pe.wait_ge(g_out, b)
                for m in range(DK):
                    mm = project(G[:, m], "WgT", x_hi, x_lo, m)
                mm.then_inc(g_ps, 1)

            def mean(b):
                pe.wait_ge(y_out, 2 * b + 2)
                if not (isinstance(b, int) and b == 0):
                    pe.wait_ge(sd_out, b)
                full_matmul(pe, ST, [(c["mean_w"][:], y[:, k]) for k in range(DK)]).then_inc(mean_ps, 1)

            def variance(b):
                pe.wait_ge(sq_out, b + 1)
                full_matmul(pe, ST, [(c["mean_w"][:], sq[:, k]) for k in range(DK)]).then_inc(var_ps, 1)

            def values(b, par):
                if not (isinstance(b, int) and b == 0):
                    pe.wait_ge(y_out, 2 * b)
                vb = VY.rearrange("p a (t n) -> p (a t) n", n=D)
                for t in range(NT):
                    mm = full_matmul(pe, vb[:, t], [(x[:, par, k, t * P:(t + 1) * P], wv[:, k, :]) for k in range(DK)])
                mm.then_inc(v_ps, 1)

            def scores(b, par):
                pe.wait_ge(qm_out, 2 * b + 2)
                if not (isinstance(b, int) and b == 0):
                    pe.wait_ge(s_out, b)
                for t in range(NT):
                    tok = slice(t * P, (t + 1) * P)
                    mm = full_matmul(pe, S[:, tok], [(x[:, par, k, tok], qm[:, k, tok]) for k in range(DK)])
                mm.then_inc(s_ps, 1)

            def attend(b):
                pe.wait_ge(s_out, b + 1)
                pe.wait_ge(v_out, b + 1)
                for m in range(DK):
                    for t in range(NT):
                        mm = pe.matmul(QO[:, m, t * P:(t + 1) * P], v[:, t, m * P:(m + 1) * P], s[:, t],
                                       start=True, stop=True)
                    mm.then_inc(o_ps, 1)

            queries(0)
            gates(0)
            values(0, 0)
            scores(0, 0)
            attend(0)

            def step(b, par):
                queries(b)
                outputs(b - 1)
                gates(b)
                mean(b - 1)
                values(b, par)
                scores(b, par)
                variance(b - 1)
                attend(b)

            step(1, 1)
            with pe.Fori(2, B - 1, 2) as i:
                step(i, 0)
                step(i + 1, 1)
            outputs(B - 1)
            mean(B - 1)
            variance(B - 1)


def cross_attention_phase(nc, ctx, sb, a, c, ps, x1_dram, y2_dram):
    def sem(name):
        return ctx.enter_context(nc.semaphore("b_" + name))

    raw_x = sb(ctx, "raw_x", [P, DK, T], F32)
    raw_c = sb(ctx, "raw_c", [P, DK, T], F32)
    x_res = sb(ctx, "x_res", [P, DK, T], F32)
    x_hi, x_lo = (sb(ctx, "bx_" + n, [P, DK, T], F32R) for n in ("hi", "lo"))
    c_hi, c_lo = (sb(ctx, "bc_" + n, [P, DK, T], F32R) for n in ("hi", "lo"))
    mask_u8 = sb(ctx, "mask_u8", [P, T], U8)
    mask = sb(ctx, "mask", [P, T], F32)
    q1, q2, k1, k2 = (sb(ctx, n, [P, 2, 2, T], F32R) for n in ("q1", "q2", "k1", "k2"))
    v = sb(ctx, "v_b", [P, NT, HD], F32)
    prob = sb(ctx, "prob", [P, 2, NT * T], F32)
    half = sb(ctx, "half", [P, 2 * T], F32)
    acc = sb(ctx, "acc", [P, 2, T], F32)
    rden = sb(ctx, "rden", [P, T], F32)
    att = sb(ctx, "att", [P, PAIRS, T], F32)
    y2 = sb(ctx, "y2", [P, DK, T], F32)
    junk = sb(ctx, "junk", [P, NT, T], BF16)
    mx = sb(ctx, "mx", [P, 2, 2, NT], F32)
    nm_hi, nm_lo = (sb(ctx, "nm_" + n, [P, 2, 2, NT], BF16) for n in ("hi", "lo"))

    x_in, ctx_in, mask_in, res_in = sem("x_in"), sem("ctx_in"), sem("mask_in"), sem("res_in")
    consts, x_split, mask_done = sem("consts"), sem("x_split"), sem("mask_done")
    q_ps, q_hi_out, q_lo_out = sem("q_ps"), sem("q_hi_out"), sem("q_lo_out")
    k_ps, k_hi_out, k_lo_out, k_mask = sem("k_ps"), sem("k_hi_out"), sem("k_lo_out"), sem("k_mask")
    smax_ps, smax_out, nm_out = sem("smax_ps"), sem("smax_out"), sem("nm_out")
    row_ps, row_out = sem("row_ps"), sem("row_out")
    st_ps, exp_out, pv_ps, acc_out = sem("st_ps"), sem("exp_out"), sem("pv_ps"), sem("acc_out")
    den_ps, rden_out, att_out = sem("den_ps"), sem("rden_out"), sem("att_out")
    v_ps, v_out, o_ps, o_out, stored = sem("v_ps"), sem("v_out"), sem("o_ps"), sem("o_out"), sem("stored")

    PV = ps[:, 4, :]
    W0, W1, W2 = ps[:, 5, :], ps[:, 6, :], ps[:, 7, :]
    OWN = (slice(0, DH), slice(DH, P))
    OTHER = (OWN[1], OWN[0])
    MAX_ROW, MASK_ROW = (DH, 0), (DH + 32, 32)

    def per_pair(b, p):
        return b * PAIRS + p

    with nc.Block() as block:
        @block.sync
        def _(sp):
            def load(b):
                sp.dma_start(raw_x[:], batch_cols(x1_dram, b)).then_inc(x_in, 16)
                sp.dma_start(raw_c[:], batch_cols(a["cT"], b)).then_inc(ctx_in, 16)
                sp.dma_start(mask_u8[:], row_of(a["mask"], b).partition_broadcast(P)).then_inc(mask_in, 16)

            def store(b):
                sp.wait_ge(o_out, 2 * b + 2)
                sp.dma_start(batch_cols(y2_dram, b), y2[:]).then_inc(stored, 16)

            def load_residual(b):
                sp.dma_start(x_res[:], batch_cols(x1_dram, b)).then_inc(res_in, 16)

            load(0)
            load_residual(0)
            sp.wait_ge(x_split, 4)
            sp.wait_ge(mask_done, 1)
            load(1)
            with sp.Fori(1, B - 1) as b:
                store(b - 1)
                load_residual(b)
                sp.wait_ge(mask_done, b + 1)
                load(b + 1)
            store(B - 2)
            load_residual(B - 1)
            store(B - 1)
            sp.wait_ge(stored, 16 * B)

        @block.gpsimd
        def _(pool):
            def add_key_tiles(g, h, first):
                n = 4 * g + 2 * h
                pool.wait_ge(exp_out, n + 2)
                pool.tensor_tensor(half[:], prob[:, h, 0:2 * T], prob[:, h, 2 * T:4 * T],
                                   ALU.add).then_inc(acc_out, 1)
                pool.wait_ge(acc_out, n + 1)
                if not first:
                    pool.wait_ge(den_ps, g)
                pool.tensor_tensor(acc[:, h, :], half[:, 0:T], half[:, T:2 * T], ALU.add).then_inc(acc_out, 1)
                pool.wait_ge(acc_out, n + 2)

            def batch(b, first):
                for p in range(PAIRS):
                    for h in range(2):
                        add_key_tiles(per_pair(b, p), h, first and p == 0)

            batch(0, True)
            with pool.Fori(1, B) as b:
                batch(b, False)

        @block.scalar
        def _(act):
            act.wait_ge(consts, 3)

            def exps(g, h, first):
                for s in range(2):
                    act.wait_ge(st_ps, 4 * g + 2 * h + s + 1)
                    if not first and s == 0:
                        act.wait_ge(pv_ps, g)
                        act.wait_ge(acc_out, 4 * g - 2 + 2 * h)
                    act.activation(prob[:, h, s * 2 * T:(s + 1) * 2 * T], ps[:, 2 * s:2 * s + 2, :], ACT.Exp,
                                   scale=SCALE).then_inc(exp_out, 1)

            def queries_hi(g, p):
                par = p % 2
                act.wait_ge(q_ps, g + 1)
                for h in range(2):
                    act.activation(q1[OWN[h], par, h, :], W0[OWN[h], :], ACT.Identity,
                                   bias=c["bq"][OWN[h], p:p + 1]).then_inc(q_hi_out, 1)
                act.wait_ge(q_hi_out, 4 * g + 2)
                for h in range(2):
                    act.activation(q1[OTHER[h], par, h, :], f32(q1[OWN[h], par, h, :]), ACT.Copy).then_inc(q_hi_out, 1)

            def keys_hi(b, g, p):
                par = p % 2
                act.wait_ge(k_ps, g + 1)
                for h in range(2):
                    act.activation(k1[OWN[h], par, h, :], W1[OWN[h], :], ACT.Identity,
                                   bias=c["bk"][OWN[h], p:p + 1]).then_inc(k_hi_out, 1)
                act.wait_ge(k_hi_out, 4 * g + 2)
                for h in range(2):
                    act.activation(k2[OWN[h], par, h, :], f32(k1[OWN[h], par, h, :]), ACT.Copy).then_inc(k_hi_out, 1)
                if p < 2:
                    act.wait_ge(mask_done, b + 1)
                    for h in range(2):
                        r = slice(MASK_ROW[h], MASK_ROW[h] + 1)
                        act.activation(k2[r, par, h, :], mask[r, :], ACT.Copy).then_inc(k_mask, 1)

            def max_rows(g, p):
                par = p % 2
                for h in range(2):
                    r = slice(MAX_ROW[h], MAX_ROW[h] + 1)
                    act.wait_ge(row_ps, 2 * g + h + 1)
                    act.activation(q2[r, par, h, :], W2[r, :], ACT.Copy).then_inc(row_out, 1)

            def batch(b, first, last):
                for p in range(PAIRS):
                    g = per_pair(b, p)
                    nxt = not (last and p == PAIRS - 1)
                    pn, bn = (p + 1, b) if p < PAIRS - 1 else (0, b + 1)
                    exps(g, 0, first and p == 0)
                    if nxt:
                        queries_hi(g + 1, pn)
                    exps(g, 1, first and p == 0)
                    if nxt:
                        keys_hi(bn, g + 1, pn)
                        max_rows(g + 1, pn)

            queries_hi(0, 0)
            keys_hi(0, 0, 0)
            max_rows(0, 0)
            batch(0, True, False)
            with act.Fori(1, B - 1) as b:
                batch(b, False, False)
            batch(B - 1, False, True)

        @block.vector
        def _(dve):
            scores_number = dve.alloc_register("scores_number")
            dve.memset(f32(q2[:]), 0.0).then_inc(consts, 1)
            dve.memset(f32(k2[:]), 0.0).then_inc(consts, 1)
            dve.wait_ge(consts, 2)
            for h in range(2):
                dve.memset(f32(q2[MASK_ROW[h]:MASK_ROW[h] + 1, :, h, :]), 1.0)
                ones = dve.memset(f32(k2[MAX_ROW[h]:MAX_ROW[h] + 1, :, h, :]), 1.0)
            ones.then_inc(consts, 1)

            def split_inputs(b, first):
                n = 4 * b
                dve.wait_ge(x_in, 16 * b + 16)
                dve.wait_ge(ctx_in, 16 * b + 16)
                if not first:
                    dve.wait_ge(k_ps, PAIRS * b)
                dve.tensor_copy(x_hi[:], raw_x[:]).then_inc(x_split, 1)
                dve.tensor_copy(c_hi[:], raw_c[:]).then_inc(x_split, 1)
                dve.wait_ge(x_split, n + 1)
                dve.tensor_tensor(x_lo[:], raw_x[:], f32(x_hi[:]), ALU.subtract).then_inc(x_split, 1)
                dve.wait_ge(x_split, n + 2)
                dve.tensor_tensor(c_lo[:], raw_c[:], f32(c_hi[:]), ALU.subtract).then_inc(x_split, 1)
                dve.wait_ge(mask_in, 16 * b + 16)
                if not first:
                    dve.wait_ge(k_mask, 4 * b)
                dve.tensor_scalar(mask[:], mask_u8[:], 1.0, -MASKED, ALU.subtract, ALU.mult).then_inc(mask_done, 1)

            def queries_lo(g, p):
                par = p % 2
                for h in range(2):
                    dve.wait_ge(q_hi_out, 4 * g + 2)
                    dve.scalar_tensor_tensor(out=q2[OWN[h], par, h, :], in0=W0[OWN[h], :],
                                             scalar=c["bq"][OWN[h], p:p + 1], in1=f32(q1[OWN[h], par, h, :]),
                                             op0=ALU.add, op1=ALU.subtract).then_inc(q_lo_out, 1)

            def keys_lo(g, p):
                par = p % 2
                for h in range(2):
                    dve.wait_ge(k_hi_out, 4 * g + 2)
                    dve.scalar_tensor_tensor(out=k1[OTHER[h], par, h, :], in0=W1[OWN[h], :],
                                             scalar=c["bk"][OWN[h], p:p + 1], in1=f32(k1[OWN[h], par, h, :]),
                                             op0=ALU.add, op1=ALU.subtract).then_inc(k_lo_out, 1)

            def maxima(b, g, p):
                par = p % 2
                dve.wait_ge(mask_done, b + 1)
                for h in range(2):
                    for t in range(NT):
                        if isinstance(b, int):
                            dve.wait_ge(smax_ps, 8 * g + NT * h + t + 1)
                        else:
                            dve.wait_ge(smax_ps, scores_number)
                            dve.reg_add(scores_number, scores_number, 1)
                        dve.tensor_tensor_reduce(junk[:, t, :], (W0, W1)[t % 2], mask[:], 1.0, LOWEST, ALU.add, ALU.max,
                                                 mx[:, par, h, t:t + 1]).then_inc(smax_out, 1)
                    dve.wait_ge(smax_out, 8 * g + NT * (h + 1))
                    dve.tensor_scalar(nm_hi[:, par, h, :], mx[:, par, h, :], -1.0, None, ALU.mult).then_inc(nm_out, 1)
                    dve.wait_ge(nm_out, 4 * g + 2 * h + 1)
                    dve.scalar_tensor_tensor(out=nm_lo[:, par, h, :], in0=mx[:, par, h, :], scalar=-1.0,
                                             in1=nm_hi[:, par, h, :], op0=ALU.mult,
                                             op1=ALU.subtract).then_inc(nm_out, 1)

            def normalise(b, g, p, first):
                dve.wait_ge(den_ps, g + 1)
                dve.reciprocal(rden[:], W1).then_inc(rden_out, 1)
                dve.wait_ge(rden_out, g + 1)
                dve.wait_ge(pv_ps, g + 1)
                if p == 0 and not first:
                    dve.wait_ge(o_ps, 2 * b)
                dve.tensor_tensor(att[:, p, :], PV, rden[:], ALU.mult).then_inc(att_out, 1)

            def values_out(b, first):
                if not first:
                    dve.wait_ge(pv_ps, PAIRS * b)
                for i in range(2 * NT):
                    kt, n = divmod(i, 2)
                    cols = slice(n * T, (n + 1) * T)
                    dve.wait_ge(v_ps, 8 * b + i + 1)
                    dve.tensor_tensor(v[:, kt, cols], (W0, W2)[i % 2], c["bv"][:, cols], ALU.add).then_inc(v_out, 1)

            def projected_out(b, first):
                dve.wait_ge(res_in, 16 * b + 16)
                if not first:
                    dve.wait_ge(stored, 16 * b)
                for m in range(DK):
                    dve.wait_ge(o_ps, 2 * b + m + 1)
                    dve.scalar_tensor_tensor(out=y2[:, m], in0=(W0, W2)[m], scalar=c["bo"][:, m:m + 1],
                                             in1=x_res[:, m], op0=ALU.add, op1=ALU.add).then_inc(o_out, 1)

            def batch(b, first, last):
                for p in range(PAIRS):
                    g = per_pair(b, p)
                    nxt = not (last and p == PAIRS - 1)
                    pn, bn = (p + 1, b) if p < PAIRS - 1 else (0, b + 1)
                    if p > 0:
                        normalise(b, g - 1, p - 1, first)
                    elif not first:
                        normalise(b - 1, g - 1, PAIRS - 1, False)
                    if p == 0:
                        values_out(b, first)
                        if not first:
                            projected_out(b - 1, isinstance(b, int) and b == 1)
                    if nxt:
                        queries_lo(g + 1, pn)
                        keys_lo(g + 1, pn)
                        maxima(bn, g + 1, pn)
                    if p == PAIRS - 2 and not last:
                        split_inputs(b + 1, False)

            split_inputs(0, True)
            queries_lo(0, 0)
            keys_lo(0, 0)
            maxima(0, 0, 0)
            batch(0, True, False)
            batch(1, False, False)
            dve.reg_mov(scores_number, 8 * (per_pair(2, 0) + 1) + 1)
            with dve.Fori(2, B - 1) as b:
                batch(b, False, False)
            batch(B - 1, False, True)
            normalise(B - 1, PAIRS * B - 1, PAIRS - 1, False)
            projected_out(B - 1, False)

        @block.tensor
        def _(pe):
            def heads(bank, w, r_hi, r_lo, p):
                cols = slice(p * P, (p + 1) * P)
                return split_matmul(pe, bank, [(c[w + "_hi"][:, k, cols], c[w + "_lo"][:, k, cols],
                                                r_hi[:, k], r_lo[:, k]) for k in range(DK)])

            def queries(b, g, p, waits):
                if p == 0:
                    pe.wait_ge(x_split, 4 * b + 4)
                if waits == "values":
                    pe.wait_ge(v_out, 8 * b + 8)
                    if not (isinstance(b, int) and b == 0):
                        pe.wait_ge(o_out, 2 * b)
                heads(W0, "wq", x_hi, x_lo, p).then_inc(q_ps, 1)

            def keys(g, p, first):
                if not first:
                    pe.wait_ge(rden_out, g - 1)
                heads(W1, "wk", c_hi, c_lo, p).then_inc(k_ps, 1)

            def max_scores(g, p, h, t):
                par, n = p % 2, NT * h + t
                if n == 0:
                    pe.wait_ge(q_hi_out, 4 * g + 4)
                    pe.wait_ge(q_lo_out, 2 * g + 2)
                    pe.wait_ge(k_lo_out, 2 * g + 2)
                elif n > 1:
                    pe.wait_ge(smax_out, 8 * g + n - 1)
                pe.matmul((W0, W1)[t % 2], q1[:, par, h, t * P:(t + 1) * P], k1[:, par, h, :],
                          start=True, stop=True).then_inc(smax_ps, 1)

            def max_to_row(g, p, h):
                par, r = p % 2, slice(MAX_ROW[h], MAX_ROW[h] + 1)
                pe.wait_ge(nm_out, 4 * g + 2 * h + 2)
                for t in range(NT):
                    o = W2[r, t * P:(t + 1) * P]
                    pe.matmul(o, nm_hi[:, par, h, t:t + 1], c["ident"][:], start=True, stop=False)
                    mm = pe.matmul(o, nm_lo[:, par, h, t:t + 1], c["ident"][:], start=False, stop=True)
                mm.then_inc(row_ps, 1)

            def scores(b, g, p, h, first):
                par = p % 2
                pe.wait_ge(row_out, 2 * g + h + 1)
                if h == 0:
                    pe.wait_ge(k_hi_out, 4 * g + 4)
                    if p < 2:
                        pe.wait_ge(k_mask, 4 * b + 2 * p + 2)
                for s in range(2):
                    if not (first and h == 0):
                        pe.wait_ge(exp_out, 4 * g + 2 * h + s - 1)
                    for kt in (2 * s, 2 * s + 1):
                        cols = slice(kt * P, (kt + 1) * P)
                        pe.matmul(ps[:, kt, :], k1[:, par, h, cols], q1[:, par, h, :], start=True, stop=False)
                        mm = pe.matmul(ps[:, kt, :], k2[:, par, h, cols], q2[:, par, h, :], start=False, stop=True)
                    mm.then_inc(st_ps, 1)

            def weighted_values(p, h, kt):
                cols = slice((2 * p + h) * DH, (2 * p + h + 1) * DH)
                return pe.matmul(PV[OWN[h], :], v[:, kt, cols], prob[:, h, kt * T:(kt + 1) * T],
                                 start=(kt == 0), stop=(kt == NT - 1))

            def sums(g, nxt):
                pe.wait_ge(acc_out, 4 * g + 4)
                if nxt:
                    pe.wait_ge(smax_out, 8 * g + 16)
                for h in range(2):
                    mm = pe.matmul(W1[OWN[h], :], c["ones_w"][:, 0:DH], acc[:, h, :], start=True, stop=True)
                mm.then_inc(den_ps, 1)

            def values(b):
                for i in range(2 * NT):
                    kt, n = divmod(i, 2)
                    if i >= 2:
                        pe.wait_ge(v_out, 8 * b + i - 1)
                    elif i == 0:
                        pe.wait_ge(smax_out, PAIRS * 8 * b + 8)
                    else:
                        pe.wait_ge(row_out, PAIRS * 2 * b + 2)
                    split_matmul(pe, (W0, W2)[i % 2], [
                        (c_hi[:, k, kt * P:(kt + 1) * P], c_lo[:, k, kt * P:(kt + 1) * P],
                         c["wv_hi"][:, k, n * T:(n + 1) * T], c["wv_lo"][:, k, n * T:(n + 1) * T])
                        for k in range(DK)]).then_inc(v_ps, 1)

            def project(b, tail):
                pe.wait_ge(att_out, PAIRS * b + PAIRS)
                for m in range(DK):
                    if not tail:
                        pe.wait_ge(v_out, 8 * b + 15 + m)
                    full_matmul(pe, (W0, W2)[m], [(c["wo"][:, p, m * P:(m + 1) * P], att[:, p, :])
                                                  for p in range(PAIRS)]).then_inc(o_ps, 1)

            def batch(b, first, last):
                for p in range(PAIRS):
                    g = per_pair(b, p)
                    nxt = not (last and p == PAIRS - 1)
                    pn, bn = (p + 1, b) if p < PAIRS - 1 else (0, b + 1)
                    head = first and p == 0
                    scores(b, g, p, 0, head)
                    if p == 0:
                        values(b)
                        if not first:
                            project(b - 1, False)
                    if nxt:
                        queries(bn, g + 1, pn, "values" if p == 0 else "")
                    scores(b, g, p, 1, head)
                    if nxt:
                        keys(g + 1, pn, head)
                    pe.wait_ge(exp_out, 4 * g + 4)
                    if p == 0:
                        pe.wait_ge(v_out, 8 * b + 8)
                    if not head:
                        pe.wait_ge(att_out, g)
                    for kt in range(NT):
                        for h in range(2):
                            mm = weighted_values(p, h, kt)
                            if kt == NT - 1 and h == 1:
                                mm.then_inc(pv_ps, 1)
                            if nxt:
                                max_scores(g + 1, pn, *divmod(2 * kt + h, NT))
                    if nxt:
                        max_to_row(g + 1, pn, 0)
                        max_to_row(g + 1, pn, 1)
                    sums(g, nxt)

            queries(0, 0, 0, "")
            keys(0, 0, True)
            for h in range(2):
                for t in range(NT):
                    max_scores(0, 0, h, t)
            max_to_row(0, 0, 0)
            max_to_row(0, 0, 1)
            batch(0, True, False)
            with pe.Fori(1, B - 1) as b:
                batch(b, False, False)
            batch(B - 1, False, True)
            project(B - 1, True)


def ffn_phase(nc, ctx, sb, a, c, ps, y2_dram, out):
    def sem(name):
        return ctx.enter_context(nc.semaphore("c_" + name))

    w_hi = sb(ctx, "wfc_hi", [P, DK, HID], F32R)
    w_lo = sb(ctx, "wfc_lo", [P, DK, HID], F32R)
    tern = sb(ctx, "tern", [P, HK, D], F32R)
    pscale = sb(ctx, "pscale", [P, DK], F32)
    ones2 = c["ones_w"][:, 0:2]

    def sems(*names):
        return [sem(n) for n in names]

    w_in, step, w_ps, ready = sems("w_in", "step", "w_ps", "ready")
    with ExitStack() as tmp:
        wfc = sb(tmp, "wfc_raw", [P, DK, HID], F32)
        wabs = sb(tmp, "wfc_abs", [P, DK, HID], F32)
        wpr = sb(tmp, "wpr_raw", [P, HK, D], F32)
        wpabs = sb(tmp, "wpr_abs", [P, HK, D], F32)
        bT = sb(tmp, "bT", [RANK, RANK], F32)
        vr = sb(tmp, "vr", [RANK, D], F32)
        uT = sb(tmp, "uT", [RANK, HID], F32)
        bv = sb(tmp, "bv_lr", [RANK, D], F32)
        gt = sb(tmp, "gt", [P, 1], F32)
        scale = sb(tmp, "scale", [P, HID], F32)
        up = sb(tmp, "up", [P, HID], F32)
        dn = sb(tmp, "dn", [P, HID], F32)
        full = sb(tmp, "wfull", [P, DK, HID], F32)
        pup = sb(tmp, "pup", [P, D], F32)
        pdn = sb(tmp, "pdn", [P, D], F32)
        psc = sb(tmp, "psc", [P, D], F32)
        with nc.Block() as block:
            @block.sync
            def _(sp):
                sp.dma_start(wfc[:], a["wfcT"].rearrange("(k p) n -> p k n", p=P)).then_inc(w_in, 16)
                sp.dma_start(wpr[:], a["wprojT"].rearrange("(k p) n -> p k n", p=P)).then_inc(w_in, 16)
                sp.dma_start(bT[:], a["fast_bT"]).then_inc(w_in, 16)
                sp.dma_start(vr[:], a["v"]).then_inc(w_in, 16)
                sp.dma_start(uT[:], a["uT"]).then_inc(w_in, 16)
                sp.dma_start(gt[:], a["gate"].partition_broadcast(P)).then_inc(w_in, 16)

            @block.scalar
            def _(act):
                act.wait_ge(w_in, 96)
                act.activation(wabs[:], wfc[:], ACT.Abs).then_inc(ready, 1)
                act.activation(wpabs[:], wpr[:], ACT.Abs).then_inc(ready, 1)

            @block.tensor
            def _(pe):
                pe.wait_ge(w_in, 96)
                pe.matmul(ps[0:RANK, 7, 0:D], bT[:], vr[:], start=True, stop=True).then_inc(w_ps, 1)
                pe.wait_ge(ready, 2)
                for n in range(2):
                    full_matmul(pe, ps[:, n, :], [(c["mean_w"][:], wabs[:, k, n * T:(n + 1) * T])
                                                  for k in range(DK)])
                full_matmul(pe, ps[:, 2, 0:D], [(c["ones_w"][:], wpabs[:, k, :]) for k in range(HK)])
                for m in range(DK):
                    mm = full_matmul(pe, ps[:, 2, D + 2 * m:D + 2 * m + 2],
                                     [(wpabs[:, k, m * P:(m + 1) * P], ones2) for k in range(HK)])
                mm.then_inc(w_ps, 1)
                pe.wait_ge(step, 1)
                for k in range(DK):
                    for n in range(2):
                        mm = pe.matmul(ps[:, 3 + 2 * k + n, :], bv[:, k * P:(k + 1) * P],
                                       uT[:, n * T:(n + 1) * T], start=True, stop=True)
                mm.then_inc(w_ps, 1)

            @block.vector
            def _(dve):
                done = [0]

                def then(ins):
                    done[0] += 1
                    ins.then_inc(step, 1)
                    dve.wait_ge(step, done[0])

                dve.wait_ge(w_ps, 1)
                then(dve.tensor_copy(bv[:], ps[0:RANK, 7, 0:D]))
                dve.wait_ge(w_ps, 2)
                then(dve.tensor_scalar(scale[:], ps[:, 0:2, :].rearrange("p a n -> p (a n)"), 1e-5, None, ALU.max))
                then(dve.tensor_scalar(psc[:], ps[:, 2, 0:D], 1.0 / HID, 1e-5, ALU.mult, ALU.max))
                then(dve.tensor_scalar(pscale[:], ps[:, 2, D:D + 2 * DK:2], 1.0 / HID, 1e-5, ALU.mult, ALU.max))
                dve.wait_ge(w_ps, 3)
                for k in range(DK):
                    then(dve.scalar_tensor_tensor(out=up[:], in0=scale[:], scalar=0.5, in1=wfc[:, k, :],
                                                  op0=ALU.mult, op1=ALU.is_lt))
                    then(dve.scalar_tensor_tensor(out=dn[:], in0=scale[:], scalar=-0.5, in1=wfc[:, k, :],
                                                  op0=ALU.mult, op1=ALU.is_gt))
                    then(dve.tensor_tensor(up[:], up[:], dn[:], ALU.subtract))
                    then(dve.tensor_tensor(up[:], up[:], scale[:], ALU.mult))
                    then(dve.scalar_tensor_tensor(
                        out=full[:, k, :], in0=ps[:, 3 + 2 * k:5 + 2 * k, :].rearrange("p a n -> p (a n)"),
                        scalar=gt[:, 0:1], in1=up[:], op0=ALU.mult, op1=ALU.add))
                then(dve.tensor_copy(w_hi[:], full[:]))
                then(dve.tensor_tensor(w_lo[:], full[:], f32(w_hi[:]), ALU.subtract))
                for k in range(HK):
                    then(dve.scalar_tensor_tensor(out=pup[:], in0=psc[:], scalar=0.5, in1=wpr[:, k, :],
                                                  op0=ALU.mult, op1=ALU.is_lt))
                    then(dve.scalar_tensor_tensor(out=pdn[:], in0=psc[:], scalar=-0.5, in1=wpr[:, k, :],
                                                  op0=ALU.mult, op1=ALU.is_gt))
                    then(dve.tensor_tensor(tern[:, k, :], pup[:], pdn[:], ALU.subtract))

    y2 = sb(ctx, "y2_c", [P, DK, T], F32)
    dev2, sq2 = (sb(ctx, n, [P, DK, T], F32) for n in ("dev2", "sq2"))
    sd2, rs2 = (sb(ctx, n, [P, T], F32) for n in ("sd2", "rs2"))
    x2 = sb(ctx, "x2", [P, 2, DK, T], F32)
    x_hi, x_lo = (sb(ctx, "cx_" + n, [P, DK, T], F32R) for n in ("hi", "lo"))
    RH = 3
    r = sb(ctx, "relu", [P, RH, T], F32)
    rr = sb(ctx, "relu2", [P, RH, T], F32)
    h_hi, h_lo = (sb(ctx, "h_" + n, [P, HK, T], F32R) for n in ("hi", "lo"))
    y3 = sb(ctx, "y3", [P, DK, T], F32)
    dev3, sq3, x3 = (sb(ctx, n, [P, DK, T], F32) for n in ("dev3", "sq3", "x3"))
    sd3, rs3 = (sb(ctx, n, [P, T], F32) for n in ("sd3", "rs3"))

    y_in, stored = sems("y_in", "stored")
    mean2_ps, dev2_out, sq2_out, var2_ps, sd2_out, rs2_out, x2_out = sems(
        "mean2_ps", "dev2_out", "sq2_out", "var2_ps", "sd2_out", "rs2_out", "x2_out")
    mean3_ps, dev3_out, sq3_out, var3_ps, sd3_out, rs3_out, x3_out = sems(
        "mean3_ps", "dev3_out", "sq3_out", "var3_ps", "sd3_out", "rs3_out", "x3_out")
    x_split, h_ps, relu_out, hi_out, rr_out, lo_out, p_ps, y3_out = sems(
        "x_split", "h_ps", "relu_out", "hi_out", "rr_out", "lo_out", "p_ps", "y3_out")

    HB = 3
    STAT3, STAT2 = ps[:, 3, :], ps[:, 4, :]
    OUT = ps[:, 5:7, :]

    def both(tile):
        return tile[:].rearrange("p (o t) -> p o t", o=1).to_broadcast([P, DK, T])

    with nc.Block() as block:
        @block.sync
        def _(sp):
            def load(b):
                sp.dma_start(y2[:], batch_cols(y2_dram, b)).then_inc(y_in, 16)

            def store(b):
                sp.wait_ge(x3_out, b + 1)
                sp.dma_start(batch_cols(out, b), x3[:]).then_inc(stored, 16)

            load(0)
            sp.wait_ge(dev2_out, 1)
            load(1)
            sp.wait_ge(dev2_out, 2)
            load(2)
            with sp.Fori(3, B) as b:
                store(b - 3)
                sp.wait_ge(dev2_out, b)
                load(b)
            for b in (B - 3, B - 2, B - 1):
                store(b)
            sp.wait_ge(stored, 16 * B)

        @block.gpsimd
        def _(pool):
            def batch(b, first):
                for i in range(HK):
                    pool.wait_ge(relu_out, HK * b + i + 1)
                    if not (first and i < 2):
                        pool.wait_ge(lo_out, HK * b + i - 1)
                    pool.tensor_tensor(rr[:, i % 2, :], r[:, i % 2, :], r[:, i % 2, :], ALU.mult).then_inc(rr_out, 1)

            batch(0, True)
            with pool.Fori(1, B) as b:
                batch(b, False)

        @block.scalar
        def _(act):
            def norm_square(dev, sq, dev_out, sq_out, b):
                act.wait_ge(dev_out, b + 1)
                act.activation(sq[:], dev[:], ACT.Square).then_inc(sq_out, 1)

            def norm_root(stat, sd, var_ps, sd_out, b):
                act.wait_ge(var_ps, b + 1)
                act.activation(sd[:], stat, ACT.Sqrt, bias=c["eps"][:, 0:1]).then_inc(sd_out, 1)

            def hidden(b, i, first):
                n = HK * b + i
                act.wait_ge(h_ps, n + 1)
                if not (first and i < 2):
                    act.wait_ge(rr_out, n - 1)
                act.activation(r[:, i % 2, :], ps[:, i % 2, :], ACT.Relu).then_inc(relu_out, 1)
                act.wait_ge(relu_out, n + 1)
                if i == 0 and not first:
                    act.wait_ge(p_ps, 2 * b)
                act.activation(h_hi[:, i, :], r[:, i % 2, :], ACT.Square).then_inc(hi_out, 1)

            def batch(b, first, last):
                hidden(b, 0, first)
                hidden(b, 1, first)
                if not first:
                    norm_square(dev3, sq3, dev3_out, sq3_out, b - 1)
                hidden(b, 2, first)
                hidden(b, 3, first)
                if not last:
                    norm_square(dev2, sq2, dev2_out, sq2_out, b + 1)
                hidden(b, 4, first)
                hidden(b, 5, first)
                if not first:
                    norm_root(STAT3, sd3, var3_ps, sd3_out, b - 1)
                hidden(b, 6, first)
                hidden(b, 7, first)
                if not last:
                    norm_root(STAT2, sd2, var2_ps, sd2_out, b + 1)

            norm_square(dev2, sq2, dev2_out, sq2_out, 0)
            norm_root(STAT2, sd2, var2_ps, sd2_out, 0)
            batch(0, True, False)
            with act.Fori(1, B - 1) as b:
                batch(b, False, False)
            batch(B - 1, False, True)
            norm_square(dev3, sq3, dev3_out, sq3_out, B - 1)
            norm_root(STAT3, sd3, var3_ps, sd3_out, B - 1)

        @block.vector
        def _(dve):
            def deviate2(b, first):
                dve.wait_ge(mean2_ps, b + 1)
                if not first:
                    dve.wait_ge(x2_out, b)
                dve.tensor_tensor(dev2[:], y2[:], both(STAT2_T), ALU.subtract).then_inc(dev2_out, 1)

            def normalise2(b, par, first):
                dve.wait_ge(sd2_out, b + 1)
                dve.reciprocal(rs2[:], sd2[:]).then_inc(rs2_out, 1)
                dve.wait_ge(rs2_out, b + 1)
                dve.tensor_tensor(x2[:, par], dev2[:], both(rs2), ALU.mult).then_inc(x2_out, 1)
                dve.wait_ge(x2_out, b + 1)
                if not first:
                    dve.wait_ge(h_ps, HK * b)
                dve.tensor_copy(x_hi[:], x2[:, par]).then_inc(x_split, 1)
                dve.wait_ge(x_split, 2 * b + 1)
                dve.tensor_tensor(x_lo[:], x2[:, par], f32(x_hi[:]), ALU.subtract).then_inc(x_split, 1)

            def hidden_lo(b, i):
                n = HK * b + i
                dve.wait_ge(hi_out, n + 1)
                dve.wait_ge(rr_out, n + 1)
                dve.tensor_tensor(h_lo[:, i, :], rr[:, i % 2, :], f32(h_hi[:, i, :]), ALU.subtract).then_inc(lo_out, 1)

            def residual(b, par, first):
                for m in range(DK):
                    dve.wait_ge(p_ps, 2 * b + m + 1)
                    if m == 0 and not first:
                        dve.wait_ge(dev3_out, b)
                    dve.scalar_tensor_tensor(out=y3[:, m], in0=OUT[:, m], scalar=pscale[:, m:m + 1],
                                             in1=x2[:, par, m], op0=ALU.mult, op1=ALU.add).then_inc(y3_out, 1)

            def deviate3(b, first):
                dve.wait_ge(mean3_ps, b + 1)
                if not first:
                    dve.wait_ge(x3_out, b)
                dve.tensor_tensor(dev3[:], y3[:], both(STAT3_T), ALU.subtract).then_inc(dev3_out, 1)

            def normalise3(b, first):
                dve.wait_ge(sd3_out, b + 1)
                dve.reciprocal(rs3[:], sd3[:]).then_inc(rs3_out, 1)
                dve.wait_ge(rs3_out, b + 1)
                if not first:
                    dve.wait_ge(stored, 16 * b)
                dve.tensor_tensor(x3[:], dev3[:], both(rs3), ALU.mult).then_inc(x3_out, 1)

            STAT2_T, STAT3_T = ps[:, 4, :], ps[:, 3, :]

            def batch(b, par, first, second, last):
                if not first:
                    residual(b - 1, 1 - par, second)
                hidden_lo(b, 0)
                hidden_lo(b, 1)
                if not first:
                    deviate3(b - 1, second)
                hidden_lo(b, 2)
                hidden_lo(b, 3)
                if not last:
                    deviate2(b + 1, False)
                hidden_lo(b, 4)
                hidden_lo(b, 5)
                if not first:
                    normalise3(b - 1, second)
                hidden_lo(b, 6)
                hidden_lo(b, 7)
                if not last:
                    normalise2(b + 1, 1 - par, False)

            deviate2(0, True)
            normalise2(0, 0, True)
            batch(0, 0, True, False, False)
            batch(1, 1, False, True, False)
            with dve.Fori(2, B - 3, 2) as i:
                batch(i, 0, False, False, False)
                batch(i + 1, 1, False, False, False)
            batch(B - 2, 0, False, False, False)
            batch(B - 1, 1, False, False, True)
            residual(B - 1, 1, False)
            deviate3(B - 1, False)
            normalise3(B - 1, False)

        @block.tensor
        def _(pe):
            def mean2(b, first):
                pe.wait_ge(y_in, 16 * b + 16)
                if not first:
                    pe.wait_ge(sd2_out, b)
                full_matmul(pe, STAT2, [(c["mean_w"][:], y2[:, k]) for k in range(DK)]).then_inc(mean2_ps, 1)

            def var2(b):
                pe.wait_ge(sq2_out, b + 1)
                full_matmul(pe, STAT2, [(c["mean_w"][:], sq2[:, k]) for k in range(DK)]).then_inc(var2_ps, 1)

            def mean3(b, first):
                pe.wait_ge(y3_out, 2 * b + 2)
                if not first:
                    pe.wait_ge(sd3_out, b)
                full_matmul(pe, STAT3, [(c["mean_w"][:], y3[:, k]) for k in range(DK)]).then_inc(mean3_ps, 1)

            def var3(b):
                pe.wait_ge(sq3_out, b + 1)
                full_matmul(pe, STAT3, [(c["mean_w"][:], sq3[:, k]) for k in range(DK)]).then_inc(var3_ps, 1)

            def hidden(b, i, first):
                if i == 0:
                    pe.wait_ge(x_split, 2 * b + 2)
                if not (first and i < 2):
                    pe.wait_ge(relu_out, HK * b + i - 1)
                cols = slice(i * P, (i + 1) * P)
                split_matmul(pe, ps[:, i % 2, :], [(w_hi[:, k, cols], w_lo[:, k, cols], x_hi[:, k], x_lo[:, k])
                                                   for k in range(DK)]).then_inc(h_ps, 1)

            def project(b, first):
                if not first:
                    pe.wait_ge(y3_out, 2 * b)
                for m in range(DK):
                    for k in range(HK):
                        pe.wait_ge(lo_out, HK * b + k + 1)
                        w = tern[:, k, m * P:(m + 1) * P]
                        pe.matmul(OUT[:, m], w, h_hi[:, k, :], start=(k == 0), stop=False)
                        mm = pe.matmul(OUT[:, m], w, h_lo[:, k, :], start=False, stop=(k == HK - 1))
                    mm.then_inc(p_ps, 1)

            def batch(b, first, second, last):
                hidden(b, 0, first)
                hidden(b, 1, first)
                if not first:
                    mean3(b - 1, second)
                hidden(b, 2, first)
                hidden(b, 3, first)
                if not last:
                    mean2(b + 1, False)
                hidden(b, 4, first)
                hidden(b, 5, first)
                if not first:
                    var3(b - 1)
                hidden(b, 6, first)
                hidden(b, 7, first)
                if not last:
                    var2(b + 1)
                project(b, first)

            mean2(0, True)
            var2(0)
            batch(0, True, False, False)
            batch(1, False, True, False)
            with pe.Fori(2, B - 1) as b:
                batch(b, False, False, False)
            batch(B - 1, False, False, True)
            mean3(B - 1, False)
            var3(B - 1)


def kernel(**inputs):
    import numpy as np
    import concourse.bacc as bacc
    from concourse.bass_utils import run_bass_kernel_spmd

    i = {k: np.asarray(v) for k, v in inputs.items()}

    def columns(v):
        return v.reshape(-1, P).T

    key, query = np.arange(P)[:, None], np.arange(P)[None, :]
    diff = query - key
    seen = (diff >= 0) & (key // CHUNK == query // CHUNK)
    bits = np.stack([((diff >> j) & 1) * seen for j in range(5)] + [seen], 1).astype(np.float32)
    arrays = {
        "xT": i["x"].reshape(B * T, D).T, "cT": i["ctx_1024"].reshape(B * T, D).T,
        "mask": i["mask_BxS2_bf1"].view(np.uint8),
        "l0_Wq": i["L0_attn_W_q"], "l0_Wk": i["L0_attn_W_k"], "l0_WvT": i["L0_attn_W_v"].T,
        "l0_WgT": i["L0_attn_W_g"].T, "l0_WoT": i["L0_attn_W_o"].T,
        "log_decay": i["L0_attn_log_decay"].reshape(1, D),
        "Wq": i["L0_xattn_Wq"], "Wk": i["L0_xattn_Wk"], "Wv": i["L0_xattn_Wv"], "Wo": i["L0_xattn_Wo"],
        "bq": columns(i["L0_xattn_bq"]), "bk": columns(i["L0_xattn_bk"]), "bo": columns(i["L0_xattn_bo"]),
        "bv": i["L0_xattn_bv"].reshape(1, HD),
        "fast_bT": i["L0_ffn_fast_b"].T, "wfcT": i["L0_ffn_w_fc"].T, "wprojT": i["L0_ffn_w_proj"].T,
        "uT": i["L0_ffn_u"].T, "v": i["L0_ffn_v"], "gate": i["L0_ffn_gate"].reshape(1, 1),
        "ident": np.eye(P, dtype=np.float32), "bits": bits,
    }
    nc = bacc.Bacc("TRN2", target_bir_lowering=False, num_devices=1)
    sent, aps = {}, {}
    for name, v in arrays.items():
        v = np.ascontiguousarray(v)
        sent[f"in_{name}"] = v
        aps[name] = nc.dram_tensor(f"in_{name}", v.shape, mybir.dt.from_np(v.dtype), kind="ExternalInput").ap()
    out = nc.dram_tensor("outT", (D, B * T), F32, kind="ExternalOutput").ap()
    decoder_layer(nc, aps, out)
    got = run_bass_kernel_spmd(nc, [sent], core_ids=[0]).results[0]["outT"]
    return got.T.reshape(B, T, D)
```

```python
from contextlib import ExitStack

import concourse.bass as bass
from concourse import mybir

ACT = mybir.ActivationFunctionType
ALU = mybir.AluOpType
AX = mybir.AxisListType
F32 = mybir.dt.float32
F32R = mybir.dt.float32r
BF16 = mybir.dt.bfloat16
U8 = mybir.dt.uint8

P = 128
B, T, D = 8, 512, 256
DK = D // P
NT = T // P
CHUNK = 32
HEADS, DH = 16, 64
HD = HEADS * DH
PAIRS = HEADS // 2
HID = 1024
HK = HID // P
RANK = 16
EPS = 1e-5
MASKED = -1e30
LOWEST = -3e38
SCALE = DH ** -0.5


def split_matmul(pe, out, terms):
    n = len(terms)
    for i, (lh, ll, rh, rl) in enumerate(terms):
        pe.matmul(out, lh, rh, start=(i == 0), stop=False)
        pe.matmul(out, lh, rl, start=False, stop=False)
        mm = pe.matmul(out, ll, rh, start=False, stop=(i == n - 1))
    return mm


def full_matmul(pe, out, terms):
    for i, (l, r) in enumerate(terms):
        mm = pe.matmul(out, l, r, start=(i == 0), stop=(i == len(terms) - 1))
    return mm


def f32(ap):
    return ap.bitcast(F32)


def batch_cols(dram, b):
    v = dram.rearrange("(k p) (b t) -> b p k t", p=P, t=T)
    if isinstance(b, int):
        return v[b]
    return v[bass.ds(b, 1)].rearrange("b p k t -> (b p) k t")


def row_of(dram, b):
    return dram[b:b + 1, :] if isinstance(b, int) else dram[bass.ds(b, 1), :]


def decoder_layer(nc, a, out):
    x1_dram = nc.dram_tensor("x1_scratch", [D, B * T], F32, kind="Internal").ap()
    y2_dram = nc.dram_tensor("y2_scratch", [D, B * T], F32, kind="Internal").ap()
    with ExitStack() as whole:
        def sb(ctx, name, shape, dt):
            return ctx.enter_context(nc.sbuf_tensor(name, shape, dt))

        c = {}
        c["mean_w"] = sb(whole, "mean_w", [P, P], F32)
        c["ones_w"] = sb(whole, "ones_w", [P, P], F32)
        c["ident"] = sb(whole, "ident", [P, P], BF16)
        c["eps"] = sb(whole, "eps", [P, 1], F32)
        for w in ("wq", "wk", "wv"):
            c[w + "_hi"] = sb(whole, w + "_hi", [P, DK, HD], F32R)
            c[w + "_lo"] = sb(whole, w + "_lo", [P, DK, HD], F32R)
        c["wo"] = sb(whole, "wo", [P, PAIRS, D], F32)
        c["bq"] = sb(whole, "bq", [P, PAIRS], F32)
        c["bk"] = sb(whole, "bk", [P, PAIRS], F32)
        c["bo"] = sb(whole, "bo", [P, DK], F32)
        c["bv"] = sb(whole, "bv", [P, 2, PAIRS], F32)
        ps = whole.enter_context(nc.psum_tensor("ps", [P, 8, T], F32))
        with ExitStack() as ctx:
            linear_attention_phase(nc, ctx, sb, a, c, ps, x1_dram)
        with ExitStack() as ctx:
            cross_attention_phase(nc, ctx, sb, a, c, ps, x1_dram, y2_dram)
        with ExitStack() as ctx:
            ffn_phase(nc, ctx, sb, a, c, ps, y2_dram, out)


def linear_attention_phase(nc, ctx, sb, a, c, ps, x1_dram):
    def sem(name):
        return ctx.enter_context(nc.semaphore("a_" + name))

    ident_f = sb(ctx, "ident_f", [P, P], F32)
    bits = sb(ctx, "bits", [P, 6, P], F32)
    nbits = sb(ctx, "nbits", [P, 5, P], F32)
    decay = sb(ctx, "decay", [P, 6], F32)
    factor = sb(ctx, "factor", [P, P], F32)
    dmask = sb(ctx, "dmask", [P, P], F32)
    raw = {w: sb(ctx, w + "_l0", [P, DK, D], F32) for w in ("Wq", "Wk", "WvT", "WgT", "WoT")}
    wv = raw["WvT"]
    w_hi = {w: sb(ctx, w + "_l0_hi", [P, DK, D], F32R) for w in ("M", "WgT", "WoT")}
    w_lo = {w: sb(ctx, w + "_l0_lo", [P, DK, D], F32R) for w in ("M", "WgT", "WoT")}
    stage = sb(ctx, "stage", [P, DK, HD], F32)
    x = sb(ctx, "x_in", [P, 2, DK, T], F32)
    x_hi = sb(ctx, "x_hi", [P, 2, DK, T], F32R)
    x_lo = sb(ctx, "x_lo", [P, 2, DK, T], F32R)
    qm = sb(ctx, "qm", [P, DK, T], F32)
    gate = sb(ctx, "gate", [P, DK, T], F32)
    v = sb(ctx, "v_tok", [P, NT, D], F32)
    s = sb(ctx, "s_masked", [P, NT, P], F32)
    og = sb(ctx, "og", [P, DK, T], F32)
    og_hi = sb(ctx, "og_hi", [P, DK, T], F32R)
    og_lo = sb(ctx, "og_lo", [P, DK, T], F32R)
    y = sb(ctx, "y_a", [P, DK, T], F32)
    dev = sb(ctx, "dev_a", [P, DK, T], F32)
    sq = sb(ctx, "sq_a", [P, DK, T], F32)
    sd = sb(ctx, "sd_a", [P, T], F32)
    rs = sb(ctx, "rs_a", [P, T], F32)
    x1 = sb(ctx, "x1_a", [P, DK, T], F32)

    consts_in, w_in, vec_in, stage_in = sem("consts_in"), sem("w_in"), sem("vec_in"), sem("stage_in")
    setup, decay_in, sig_done = sem("setup"), sem("decay_in"), sem("sig_done")
    pow_step, m_ps, w_split = sem("pow_step"), sem("m_ps"), sem("w_split")
    stage_split = sem("stage_split")
    x_in, x_split = [sem("x_in_even"), sem("x_in_odd")], sem("x_split")
    qm_ps, qm_out, g_ps, g_out = sem("qm_ps"), sem("qm_out"), sem("g_ps"), sem("g_out")
    v_ps, v_out, s_ps, s_out = sem("v_ps"), sem("v_out"), sem("s_ps"), sem("s_out")
    o_ps, gate_used, og_split = sem("o_ps"), sem("gate_used"), sem("og_split")
    y_ps, y_out = sem("y_ps"), sem("y_out")
    mean_ps, dev_out, sq_out, var_ps = sem("mean_ps"), sem("dev_out"), sem("sq_out"), sem("var_ps")
    sd_out, rs_out, x1_out, stored = sem("sd_out"), sem("rs_out"), sem("x1_out"), sem("stored")
    STAGED = ("Wq", "Wk", "Wv")

    QO, G, VY, S, ST = ps[:, 0:2, :], ps[:, 2:4, :], ps[:, 4:6, :], ps[:, 6, :], ps[:, 7, :]

    with nc.Block() as block:
        @block.sync
        def _(sp):
            sp.dma_start(ident_f[:], a["ident"]).then_inc(consts_in, 16)
            sp.dma_start(bits[:], a["bits"]).then_inc(consts_in, 16)
            sp.dma_start(decay[:, 5:6], a["log_decay"][:, 0:1].partition_broadcast(P)).then_inc(decay_in, 16)
            for w in ("Wq", "Wk", "WgT", "WoT", "WvT"):
                sp.dma_start(raw[w][:], a["l0_" + w].rearrange("(k p) n -> p k n", p=P)).then_inc(w_in, 16)
            for b in range(2):
                sp.dma_start(x[:, b], batch_cols(a["xT"], b)).then_inc(x_in[b], 16)
            sp.dma_start(c["wo"][:], a["Wo"].rearrange("(k p) n -> p k n", p=P)).then_inc(vec_in, 16)
            sp.dma_start(c["bq"][:], a["bq"]).then_inc(vec_in, 16)
            sp.dma_start(c["bk"][:], a["bk"]).then_inc(vec_in, 16)
            sp.dma_start(c["bo"][:], a["bo"]).then_inc(vec_in, 16)
            for i in range(2):
                sp.dma_start(c["bv"][:, i, :], a["bv"]).then_inc(vec_in, 16)
            for i, w in enumerate(STAGED):
                if i:
                    sp.wait_ge(stage_split, 2 * i)
                sp.dma_start(stage[:], a[w].rearrange("(k p) n -> p k n", p=P)).then_inc(stage_in, 16)

            def load_and_store(b, par):
                sp.wait_ge(y_out, 2 * b - 2)
                sp.dma_start(x[:, par], batch_cols(a["xT"], b)).then_inc(x_in[par], 16)
                sp.wait_ge(x1_out, b - 1)
                sp.dma_start(batch_cols(x1_dram, b - 2), x1[:]).then_inc(stored, 16)

            with sp.Fori(2, B - 1, 2) as b:
                load_and_store(b, 0)
                load_and_store(b + 1, 1)
            for b in (B - 2, B - 1):
                sp.wait_ge(x1_out, b + 1)
                sp.dma_start(batch_cols(x1_dram, b), x1[:]).then_inc(stored, 16)
            sp.wait_ge(stored, 16 * B)
            sp.wait_ge(vec_in, 16 * 6)

        @block.gpsimd
        def _(pool):
            for i, w in enumerate(("wq", "wk", "wv")):
                pool.wait_ge(stage_in, 16 * (i + 1))
                pool.tensor_copy(c[w + "_hi"][:], stage[:]).then_inc(stage_split, 1)
                pool.wait_ge(stage_split, 2 * i + 1)
                pool.tensor_tensor(c[w + "_lo"][:], stage[:], f32(c[w + "_hi"][:]),
                                   ALU.subtract).then_inc(stage_split, 1)

        @block.scalar
        def _(act):
            act.wait_ge(decay_in, 16)
            act.activation(decay[:, 0:1], decay[:, 5:6], ACT.Sigmoid).then_inc(sig_done, 1)

            def front(b):
                act.wait_ge(g_ps, b + 1)
                if not (isinstance(b, int) and b == 0):
                    act.wait_ge(gate_used, b)
                act.activation(gate[:], G, ACT.Sigmoid).then_inc(g_out, 1)
                for m in range(DK):
                    act.wait_ge(qm_ps, 2 * b + m + 1)
                    if m == 0 and not (isinstance(b, int) and b == 0):
                        act.wait_ge(s_ps, b)
                    act.activation(qm[:, m], QO[:, m], ACT.Copy).then_inc(qm_out, 1)

            def square(b):
                act.wait_ge(dev_out, b + 1)
                act.activation(sq[:], dev[:], ACT.Square).then_inc(sq_out, 1)

            def values(b):
                act.wait_ge(v_ps, b + 1)
                act.activation(v[:], VY.rearrange("p a (t n) -> p (a t) n", n=D), ACT.Copy).then_inc(v_out, 1)

            def deviation(b):
                act.wait_ge(var_ps, b + 1)
                act.activation(sd[:], ST, ACT.Sqrt, bias=c["eps"][:, 0:1]).then_inc(sd_out, 1)

            front(0)
            values(0)
            front(1)
            values(1)
            square(0)
            deviation(0)
            with act.Fori(2, B - 1, 2) as i:
                for b in (i, i + 1):
                    front(b)
                    values(b)
                    square(b - 1)
                    deviation(b - 1)
            square(B - 1)
            deviation(B - 1)

        @block.vector
        def _(dve):
            dve.memset(c["mean_w"][:], 1.0 / D).then_inc(setup, 1)
            dve.memset(c["ones_w"][:], 1.0).then_inc(setup, 1)
            dve.memset(c["eps"][:], EPS).then_inc(setup, 1)

            def split_x(b, par):
                dve.wait_ge(x_in[par], 8 * (b - par) + 16)
                if not (isinstance(b, int) and b < 2):
                    dve.wait_ge(qm_ps, 2 * b - 2)
                dve.tensor_copy(x_hi[:, par], x[:, par]).then_inc(x_split, 1)
                dve.wait_ge(x_split, 2 * b + 1)
                dve.tensor_tensor(x_lo[:, par], x[:, par], f32(x_hi[:, par]), ALU.subtract).then_inc(x_split, 1)

            split_x(0, 0)
            for i, w in enumerate(("M", "WgT", "WoT")):
                if w == "M":
                    dve.wait_ge(m_ps, 1)
                    src = ps[:, 0, :].rearrange("p (k n) -> p k n", k=DK)
                else:
                    dve.wait_ge(w_in, 16 * 5)
                    src = raw[w][:]
                dve.tensor_copy(w_hi[w][:], src).then_inc(w_split, 1)
                dve.wait_ge(w_split, 2 * i + 1)
                dve.tensor_tensor(w_lo[w][:], src, f32(w_hi[w][:]), ALU.subtract).then_inc(w_split, 1)
            dve.wait_ge(consts_in, 32)
            dve.wait_ge(sig_done, 1)
            dve.tensor_copy(c["ident"][:], ident_f[:]).then_inc(setup, 1)
            dve.tensor_scalar(nbits[:], bits[:, 0:5, :], -1.0, 1.0, ALU.mult, ALU.add).then_inc(pow_step, 1)
            dve.tensor_copy(dmask[:], bits[:, 5, :]).then_inc(pow_step, 1)
            n = 2
            for j in range(5):
                dve.wait_ge(pow_step, n)
                dve.scalar_tensor_tensor(out=factor[:], in0=bits[:, j, :], scalar=decay[:, j:j + 1],
                                         in1=nbits[:, j, :], op0=ALU.mult, op1=ALU.add).then_inc(pow_step, 1)
                dve.wait_ge(pow_step, n + 1)
                dve.tensor_tensor(dmask[:], dmask[:], factor[:], ALU.mult).then_inc(pow_step, 1)
                n += 2
                if j < 4:
                    dve.tensor_tensor(decay[:, j + 1:j + 2], decay[:, j:j + 1], decay[:, j:j + 1],
                                      ALU.mult).then_inc(pow_step, 1)
                    n += 1
            dve.wait_ge(pow_step, n)

            def finish_y(b, par):
                for m in range(DK):
                    dve.wait_ge(y_ps, 2 * b + m + 1)
                    if m == 0 and not (isinstance(b, int) and b == 0):
                        dve.wait_ge(dev_out, b)
                    dve.scalar_tensor_tensor(out=y[:, m], in0=x[:, par, m], scalar=2.0, in1=VY[:, m],
                                             op0=ALU.mult, op1=ALU.add).then_inc(y_out, 1)

            def subtract_mean(b):
                dve.wait_ge(mean_ps, b + 1)
                dve.wait_ge(y_out, 2 * b + 2)
                if not (isinstance(b, int) and b == 0):
                    dve.wait_ge(x1_out, b)
                mean = ST.rearrange("p (o t) -> p o t", o=1).to_broadcast([P, DK, T])
                dve.tensor_tensor(dev[:], y[:], mean, ALU.subtract).then_inc(dev_out, 1)

            def mask_scores(b):
                dve.wait_ge(s_ps, b + 1)
                if not (isinstance(b, int) and b == 0):
                    dve.wait_ge(o_ps, 2 * b)
                dve.tensor_tensor(s[:], S.rearrange("p (t n) -> p t n", n=P),
                                  dmask[:].rearrange("p (o n) -> p o n", o=1).to_broadcast([P, NT, P]),
                                  ALU.mult).then_inc(s_out, 1)

            def normalise(b):
                dve.wait_ge(sd_out, b + 1)
                dve.reciprocal(rs[:], sd[:]).then_inc(rs_out, 1)
                dve.wait_ge(rs_out, b + 1)
                if not (isinstance(b, int) and b == 0):
                    dve.wait_ge(stored, 16 * b)
                dve.tensor_tensor(x1[:], dev[:], rs[:].rearrange("p (o t) -> p o t", o=1).to_broadcast([P, DK, T]),
                                  ALU.mult).then_inc(x1_out, 1)

            def gated(b):
                dve.wait_ge(o_ps, 2 * b + 2)
                dve.wait_ge(g_out, b + 1)
                dve.tensor_tensor(og[:], QO, gate[:], ALU.mult).then_inc(gate_used, 1)
                dve.wait_ge(gate_used, b + 1)
                if not (isinstance(b, int) and b == 0):
                    dve.wait_ge(y_ps, 2 * b)
                dve.tensor_copy(og_hi[:], og[:]).then_inc(og_split, 1)
                dve.wait_ge(og_split, 2 * b + 1)
                dve.tensor_tensor(og_lo[:], og[:], f32(og_hi[:]), ALU.subtract).then_inc(og_split, 1)

            def step(b, par, last):
                finish_y(b - 1, 1 - par)
                mask_scores(b)
                subtract_mean(b - 1)
                if not last:
                    split_x(b + 1, 1 - par)
                gated(b)
                normalise(b - 1)

            mask_scores(0)
            split_x(1, 1)
            gated(0)
            step(1, 1, False)
            with dve.Fori(2, B - 3, 2) as i:
                step(i, 0, False)
                step(i + 1, 1, False)
            step(B - 2, 0, False)
            step(B - 1, 1, True)
            finish_y(B - 1, 1)
            subtract_mean(B - 1)
            normalise(B - 1)

        @block.tensor
        def _(pe):
            pe.wait_ge(w_in, 16 * 5)
            for m in range(DK):
                mm = full_matmul(pe, ps[:, 0, m * D:(m + 1) * D],
                                 [(raw["Wq"][:, k, m * P:(m + 1) * P], raw["Wk"][:, k, :]) for k in range(DK)])
            mm.then_inc(m_ps, 1)
            pe.wait_ge(w_split, 6)

            def project(bank, w, r_hi, r_lo, m):
                return split_matmul(pe, bank, [(w_hi[w][:, k, m * P:(m + 1) * P], w_lo[w][:, k, m * P:(m + 1) * P],
                                                r_hi[:, k], r_lo[:, k]) for k in range(DK)])

            def queries(b, par):
                if not (isinstance(b, int) and b == 0):
                    pe.wait_ge(gate_used, b)
                for m in range(DK):
                    project(QO[:, m], "M", x_hi[:, par], x_lo[:, par], m).then_inc(qm_ps, 1)

            def outputs(b):
                pe.wait_ge(og_split, 2 * b + 2)
                pe.wait_ge(v_out, b + 1)
                for m in range(DK):
                    project(VY[:, m], "WoT", og_hi, og_lo, m).then_inc(y_ps, 1)

            def gates(b, par):
                pe.wait_ge(x_split, 2 * b + 2)
                if not (isinstance(b, int) and b == 0):
                    pe.wait_ge(g_out, b)
                for m in range(DK):
                    mm = project(G[:, m], "WgT", x_hi[:, par], x_lo[:, par], m)
                mm.then_inc(g_ps, 1)

            def mean(b):
                pe.wait_ge(y_out, 2 * b + 2)
                if not (isinstance(b, int) and b == 0):
                    pe.wait_ge(sd_out, b)
                full_matmul(pe, ST, [(c["mean_w"][:], y[:, k]) for k in range(DK)]).then_inc(mean_ps, 1)

            def variance(b):
                pe.wait_ge(sq_out, b + 1)
                full_matmul(pe, ST, [(c["mean_w"][:], sq[:, k]) for k in range(DK)]).then_inc(var_ps, 1)

            def values(b, par):
                if not (isinstance(b, int) and b == 0):
                    pe.wait_ge(y_out, 2 * b)
                vb = VY.rearrange("p a (t n) -> p (a t) n", n=D)
                for t in range(NT):
                    mm = full_matmul(pe, vb[:, t], [(x[:, par, k, t * P:(t + 1) * P], wv[:, k, :]) for k in range(DK)])
                mm.then_inc(v_ps, 1)

            def scores(b, par):
                pe.wait_ge(qm_out, 2 * b + 2)
                if not (isinstance(b, int) and b == 0):
                    pe.wait_ge(s_out, b)
                for t in range(NT):
                    tok = slice(t * P, (t + 1) * P)
                    mm = full_matmul(pe, S[:, tok], [(x[:, par, k, tok], qm[:, k, tok]) for k in range(DK)])
                mm.then_inc(s_ps, 1)

            def attend(b):
                pe.wait_ge(s_out, b + 1)
                pe.wait_ge(v_out, b + 1)
                for m in range(DK):
                    for t in range(NT):
                        mm = pe.matmul(QO[:, m, t * P:(t + 1) * P], v[:, t, m * P:(m + 1) * P], s[:, t],
                                       start=True, stop=True)
                    mm.then_inc(o_ps, 1)

            gates(0, 0)
            queries(0, 0)
            scores(0, 0)
            values(0, 0)
            attend(0)

            def step(b, par):
                gates(b, par)
                queries(b, par)
                outputs(b - 1)
                scores(b, par)
                values(b, par)
                mean(b - 1)
                attend(b)
                variance(b - 1)

            step(1, 1)
            with pe.Fori(2, B - 1, 2) as i:
                step(i, 0)
                step(i + 1, 1)
            outputs(B - 1)
            mean(B - 1)
            variance(B - 1)


def cross_attention_phase(nc, ctx, sb, a, c, ps, x1_dram, y2_dram):
    def sem(name):
        return ctx.enter_context(nc.semaphore("b_" + name))

    raw_x = sb(ctx, "raw_x", [P, DK, T], F32)
    raw_c = sb(ctx, "raw_c", [P, DK, T], F32)
    x_res = sb(ctx, "x_res", [P, DK, T], F32)
    x_hi, x_lo = (sb(ctx, "bx_" + n, [P, DK, T], F32R) for n in ("hi", "lo"))
    c_hi, c_lo = (sb(ctx, "bc_" + n, [P, DK, T], F32R) for n in ("hi", "lo"))
    mask_u8 = sb(ctx, "mask_u8", [P, T], U8)
    mask = sb(ctx, "mask", [P, T], F32)
    q1, q2, k1, k2 = (sb(ctx, n, [P, 2, 2, T], F32R) for n in ("q1", "q2", "k1", "k2"))
    v = sb(ctx, "v_b", [P, NT, HD], F32)
    prob = sb(ctx, "prob", [P, 2, NT * T], F32)
    half = sb(ctx, "half", [P, 2 * T], F32)
    acc = sb(ctx, "acc", [P, 2, T], F32)
    log_den = sb(ctx, "log_den", [P, T], F32)
    recip0 = sb(ctx, "recip0", [P, T], F32)
    recip = sb(ctx, "recip", [P, T], F32)
    att = sb(ctx, "att", [P, PAIRS, T], F32)
    y2 = sb(ctx, "y2", [P, DK, T], F32)
    out_bias = sb(ctx, "out_bias", [P, DK], F32)
    junk = sb(ctx, "junk", [P, NT, T], BF16)
    mx = sb(ctx, "mx", [P, 2, 2, NT], F32)
    nm_hi, nm_lo = (sb(ctx, "nm_" + n, [P, 2, 2, NT], BF16) for n in ("hi", "lo"))

    x_in, ctx_in, mask_in, res_in = sem("x_in"), sem("ctx_in"), sem("mask_in"), sem("res_in")
    consts, mask_done = sem("consts"), sem("mask_done")
    x_rounded, x_split = sem("x_rounded"), sem("x_split")
    q_ps, q_hi_out, q_lo_out = sem("q_ps"), sem("q_hi_out"), sem("q_lo_out")
    k_ps, k_hi_out, k_lo_out, k_mask = sem("k_ps"), sem("k_hi_out"), sem("k_lo_out"), sem("k_mask")
    smax_ps, smax_out, nm_out = sem("smax_ps"), sem("smax_out"), sem("nm_out")
    row_ps, row_out = sem("row_ps"), sem("row_out")
    st_ps, exp_out, pv_ps, acc_out = sem("st_ps"), sem("exp_out"), sem("pv_ps"), sem("acc_out")
    den_ps, log_out, recip0_out = sem("den_ps"), sem("log_out"), sem("recip0_out")
    bias_ps, bias_out = sem("bias_ps"), sem("bias_out")
    newton, att_out = sem("newton"), sem("att_out")
    v_ps, v_out, o_ps, o_out, stored = sem("v_ps"), sem("v_out"), sem("o_ps"), sem("o_out"), sem("stored")

    PV = ps[:, 4, :]
    W0, W1, W2 = ps[:, 5, :], ps[:, 6, :], ps[:, 7, :]
    OWN = (slice(0, DH), slice(DH, P))
    OTHER = (OWN[1], OWN[0])
    MAX_ROW, MASK_ROW = (DH, 0), (DH + 32, 32)

    def per_pair(b, p):
        return b * PAIRS + p

    with nc.Block() as block:
        @block.sync
        def _(sp):
            def load(b):
                sp.dma_start(raw_x[:], batch_cols(x1_dram, b)).then_inc(x_in, 16)
                sp.dma_start(raw_c[:], batch_cols(a["cT"], b)).then_inc(ctx_in, 16)
                sp.dma_start(mask_u8[:], row_of(a["mask"], b).partition_broadcast(P)).then_inc(mask_in, 16)

            def store(b):
                sp.wait_ge(o_out, 2 * b + 2)
                sp.dma_start(batch_cols(y2_dram, b), y2[:]).then_inc(stored, 16)

            def load_residual(b):
                sp.dma_start(x_res[:], batch_cols(x1_dram, b)).then_inc(res_in, 16)

            load(0)
            load_residual(0)
            sp.wait_ge(x_split, 2)
            sp.wait_ge(mask_done, 1)
            load(1)
            with sp.Fori(1, B - 1) as b:
                store(b - 1)
                load_residual(b)
                sp.wait_ge(mask_done, b + 1)
                load(b + 1)
            store(B - 2)
            load_residual(B - 1)
            store(B - 1)
            sp.wait_ge(stored, 16 * B)

        @block.gpsimd
        def _(pool):
            def add_key_tiles(g, h, first):
                n = 4 * g + 2 * h
                pool.wait_ge(exp_out, n + 2)
                pool.tensor_tensor(half[:], prob[:, h, 0:2 * T], prob[:, h, 2 * T:4 * T],
                                   ALU.add).then_inc(acc_out, 1)
                pool.wait_ge(acc_out, n + 1)
                if not first:
                    pool.wait_ge(den_ps, g)
                pool.tensor_tensor(acc[:, h, :], half[:, 0:T], half[:, T:2 * T], ALU.add).then_inc(acc_out, 1)
                pool.wait_ge(acc_out, n + 2)

            def split_inputs(b):
                pool.wait_ge(x_rounded, 2 * b + 1)
                pool.tensor_tensor(x_lo[:], raw_x[:], f32(x_hi[:]), ALU.subtract).then_inc(x_split, 1)
                pool.wait_ge(x_rounded, 2 * b + 2)
                pool.tensor_tensor(c_lo[:], raw_c[:], f32(c_hi[:]), ALU.subtract).then_inc(x_split, 1)

            def batch(b, first, last):
                for p in range(PAIRS):
                    for h in range(2):
                        add_key_tiles(per_pair(b, p), h, first and p == 0)
                    if p == PAIRS - 3 and not last:
                        split_inputs(b + 1)

            batch(0, True, False)
            with pool.Fori(1, B - 1) as b:
                batch(b, False, False)
            batch(B - 1, False, True)

        @block.scalar
        def _(act):
            act.preload_act_table_set("natural_log_exp_and_others")
            act.wait_ge(consts, 3)

            def exps(g, h, s, first):
                act.wait_ge(st_ps, 4 * g + 2 * h + s + 1)
                if not first and s == 0:
                    act.wait_ge(pv_ps, g)
                    act.wait_ge(acc_out, 4 * g - 2 + 2 * h)
                act.activation(prob[:, h, s * 2 * T:(s + 1) * 2 * T], ps[:, 2 * s:2 * s + 2, :], ACT.Exp,
                               scale=SCALE).then_inc(exp_out, 1)

            def reciprocal_estimate(g, first):
                act.wait_ge(den_ps, g + 1)
                if not first:
                    act.wait_ge(newton, 2 * g)
                act.activation(log_den[:], W2, ACT.Ln).then_inc(log_out, 1)
                act.wait_ge(log_out, g + 1)
                act.activation(recip0[:], log_den[:], ACT.Exp, scale=-1.0).then_inc(recip0_out, 1)

            def queries_hi(g, p):
                par = p % 2
                act.wait_ge(q_ps, g + 1)
                for h in range(2):
                    act.activation(q1[OWN[h], par, h, :], W0[OWN[h], :], ACT.Identity,
                                   bias=c["bq"][OWN[h], p:p + 1]).then_inc(q_hi_out, 1)

            def queries_twice(g, p):
                par = p % 2
                act.wait_ge(q_hi_out, 4 * g + 2)
                for h in range(2):
                    act.activation(q1[OTHER[h], par, h, :], f32(q1[OWN[h], par, h, :]), ACT.Copy).then_inc(q_hi_out, 1)

            def keys_hi(g, p):
                par = p % 2
                act.wait_ge(k_ps, g + 1)
                for h in range(2):
                    act.activation(k1[OWN[h], par, h, :], W1[OWN[h], :], ACT.Identity,
                                   bias=c["bk"][OWN[h], p:p + 1]).then_inc(k_hi_out, 1)

            def keys_twice(g, p):
                par = p % 2
                act.wait_ge(k_hi_out, 4 * g + 2)
                for h in range(2):
                    act.activation(k2[OWN[h], par, h, :], f32(k1[OWN[h], par, h, :]), ACT.Copy).then_inc(k_hi_out, 1)

            def values_out(b, first):
                if not first:
                    act.wait_ge(pv_ps, PAIRS * b)
                for i in range(2 * NT):
                    kt, n = divmod(i, 2)
                    act.wait_ge(v_ps, 8 * b + i + 1)
                    act.activation(v[:, kt, n * T:(n + 1) * T], (W0, W1)[i % 2], ACT.Copy).then_inc(v_out, 1)

            def round_inputs(b, first):
                act.wait_ge(x_in, 16 * b + 16)
                if not first:
                    act.wait_ge(k_ps, PAIRS * b)
                act.activation(x_hi[:], raw_x[:], ACT.Copy).then_inc(x_rounded, 1)
                act.wait_ge(ctx_in, 16 * b + 16)
                act.activation(c_hi[:], raw_c[:], ACT.Copy).then_inc(x_rounded, 1)

            def mask_rows(b, par):
                act.wait_ge(mask_done, b + 1)
                for h in range(2):
                    r = slice(MASK_ROW[h], MASK_ROW[h] + 1)
                    act.activation(k2[r, par, h, :], mask[r, :], ACT.Copy).then_inc(k_mask, 1)

            def max_row(g, p, h):
                r = slice(MAX_ROW[h], MAX_ROW[h] + 1)
                act.wait_ge(row_ps, 2 * g + h + 1)
                act.activation(q2[r, p % 2, h, :], W2[r, :], ACT.Copy).then_inc(row_out, 1)

            def project_pair(g, p):
                queries_hi(g, p)
                keys_hi(g, p)
                queries_twice(g, p)
                keys_twice(g, p)

            def batch(b, first, last):
                for p in range(PAIRS):
                    g = per_pair(b, p)
                    head = first and p == 0
                    nxt = not (last and p == PAIRS - 1)
                    nxt2 = not (last and p >= PAIRS - 2)
                    exps(g, 0, 0, head)
                    max_row(g, p, 1)
                    exps(g, 0, 1, head)
                    exps(g, 1, 0, head)
                    if not head:
                        reciprocal_estimate(g - 1, first and p == 1)
                    exps(g, 1, 1, head)
                    if p == 0:
                        values_out(b, first)
                        mask_rows(b, 1)
                    if nxt2:
                        project_pair(g + 2, (p + 2) % PAIRS)
                    if nxt:
                        max_row(g + 1, (p + 1) % PAIRS, 0)
                    if p == PAIRS - 3 and not last:
                        round_inputs(b + 1, False)
                    if p == PAIRS - 1 and not last:
                        mask_rows(b + 1, 0)

            round_inputs(0, True)
            project_pair(0, 0)
            project_pair(1, 1)
            mask_rows(0, 0)
            max_row(0, 0, 0)
            batch(0, True, False)
            with act.Fori(1, B - 1) as b:
                batch(b, False, False)
            batch(B - 1, False, True)
            reciprocal_estimate(PAIRS * B - 1, False)

        @block.vector
        def _(dve):
            scores_number = dve.alloc_register("scores_number")
            dve.memset(f32(q2[:]), 0.0).then_inc(consts, 1)
            dve.memset(f32(k2[:]), 0.0).then_inc(consts, 1)
            dve.wait_ge(consts, 2)
            for h in range(2):
                dve.memset(f32(q2[MASK_ROW[h]:MASK_ROW[h] + 1, :, h, :]), 1.0)
                ones = dve.memset(f32(k2[MAX_ROW[h]:MAX_ROW[h] + 1, :, h, :]), 1.0)
            ones.then_inc(consts, 1)

            def first_split():
                dve.wait_ge(x_rounded, 1)
                dve.tensor_tensor(x_lo[:], raw_x[:], f32(x_hi[:]), ALU.subtract).then_inc(x_split, 1)
                dve.wait_ge(x_rounded, 2)
                dve.tensor_tensor(c_lo[:], raw_c[:], f32(c_hi[:]), ALU.subtract).then_inc(x_split, 1)

            def prepare_mask(b, first):
                dve.wait_ge(mask_in, 16 * b + 16)
                if not first:
                    dve.wait_ge(k_mask, 4 * b)
                dve.tensor_scalar(mask[:], mask_u8[:], 1.0, -MASKED, ALU.subtract, ALU.mult).then_inc(mask_done, 1)
                dve.wait_ge(mask_done, b + 1)

            def queries_lo(g, p):
                par = p % 2
                for h in range(2):
                    dve.wait_ge(q_hi_out, 4 * g + 2)
                    dve.scalar_tensor_tensor(out=q2[OWN[h], par, h, :], in0=W0[OWN[h], :],
                                             scalar=c["bq"][OWN[h], p:p + 1], in1=f32(q1[OWN[h], par, h, :]),
                                             op0=ALU.add, op1=ALU.subtract).then_inc(q_lo_out, 1)

            def keys_lo(g, p):
                par = p % 2
                for h in range(2):
                    dve.wait_ge(k_hi_out, 4 * g + 2)
                    dve.scalar_tensor_tensor(out=k1[OTHER[h], par, h, :], in0=W1[OWN[h], :],
                                             scalar=c["bk"][OWN[h], p:p + 1], in1=f32(k1[OWN[h], par, h, :]),
                                             op0=ALU.add, op1=ALU.subtract).then_inc(k_lo_out, 1)

            def maxima(b, g, p, h, tiles):
                for t in tiles:
                    if isinstance(b, int):
                        dve.wait_ge(smax_ps, 8 * g + NT * h + t + 1)
                    else:
                        dve.wait_ge(smax_ps, scores_number)
                        dve.reg_add(scores_number, scores_number, 1)
                    dve.tensor_tensor_reduce(junk[:, t, :], (W0, W1)[t % 2], mask[:], 1.0, LOWEST, ALU.add, ALU.max,
                                             mx[:, p % 2, h, t:t + 1]).then_inc(smax_out, 1)

            def negate_maxima(g, p, h):
                par = p % 2
                dve.wait_ge(smax_out, 8 * g + NT * (h + 1))
                dve.tensor_scalar(nm_hi[:, par, h, :], mx[:, par, h, :], -1.0, None, ALU.mult).then_inc(nm_out, 1)
                dve.wait_ge(nm_out, 4 * g + 2 * h + 1)
                dve.scalar_tensor_tensor(out=nm_lo[:, par, h, :], in0=mx[:, par, h, :], scalar=-1.0,
                                         in1=nm_hi[:, par, h, :], op0=ALU.mult,
                                         op1=ALU.subtract).then_inc(nm_out, 1)

            def normalise(b, g, p, first):
                dve.wait_ge(recip0_out, g + 1)
                dve.tensor_tensor(log_den[:], W2, recip0[:], ALU.mult).then_inc(newton, 1)
                dve.wait_ge(newton, 2 * g + 1)
                dve.scalar_tensor_tensor(out=recip[:], in0=log_den[:], scalar=2.0, in1=recip0[:],
                                         op0=ALU.subtract, op1=ALU.mult).then_inc(newton, 1)
                dve.wait_ge(newton, 2 * g + 2)
                dve.wait_ge(pv_ps, g + 1)
                if p == 0 and not first:
                    dve.wait_ge(o_ps, 2 * b)
                dve.scalar_tensor_tensor(out=att[:, p, :], in0=PV, scalar=-1.0, in1=recip[:], op0=ALU.mult,
                                         op1=ALU.mult).then_inc(att_out, 1)

            def projected_out(b, first):
                if first:
                    dve.wait_ge(bias_out, 1)
                dve.wait_ge(res_in, 16 * b + 16)
                if not first:
                    dve.wait_ge(stored, 16 * b)
                for m in range(DK):
                    dve.wait_ge(o_ps, 2 * b + m + 1)
                    dve.scalar_tensor_tensor(out=y2[:, m], in0=(W0, W1)[m], scalar=out_bias[:, m:m + 1],
                                             in1=x_res[:, m], op0=ALU.add, op1=ALU.add).then_inc(o_out, 1)

            def batch(b, first, last):
                for p in range(PAIRS):
                    g = per_pair(b, p)
                    nxt = not (last and p == PAIRS - 1)
                    nxt2 = not (last and p >= PAIRS - 2)
                    pn, bn = (p + 1, b) if p < PAIRS - 1 else (0, b + 1)
                    if p == PAIRS - 1 and not last:
                        prepare_mask(b + 1, False)
                    if nxt:
                        maxima(bn, g + 1, pn, 0, range(NT))
                        negate_maxima(g + 1, pn, 0)
                    if p > 0:
                        normalise(b, g - 1, p - 1, first)
                    elif not first:
                            normalise(b - 1, g - 1, PAIRS - 1, False)
                            projected_out(b - 1, isinstance(b, int) and b == 1)
                    if nxt2:
                        queries_lo(g + 2, (p + 2) % PAIRS)
                        keys_lo(g + 2, (p + 2) % PAIRS)
                    if nxt:
                        maxima(bn, g + 1, pn, 1, range(NT))
                        negate_maxima(g + 1, pn, 1)

            first_split()
            prepare_mask(0, True)
            dve.wait_ge(bias_ps, 1)
            dve.tensor_tensor(out_bias[:], ps[:, 0:DK, 0:1].rearrange("p m o -> p (m o)"), c["bo"][:],
                              ALU.add).then_inc(bias_out, 1)
            for g in range(2):
                queries_lo(g, g)
                keys_lo(g, g)
            for h in range(2):
                maxima(0, 0, 0, h, range(NT))
                negate_maxima(0, 0, h)
            batch(0, True, False)
            batch(1, False, False)
            dve.reg_mov(scores_number, 8 * (per_pair(2, 0) + 1) + 1)
            with dve.Fori(2, B - 1) as b:
                batch(b, False, False)
            batch(B - 1, False, True)
            normalise(B - 1, PAIRS * B - 1, PAIRS - 1, False)
            projected_out(B - 1, False)

        @block.tensor
        def _(pe):
            def heads(bank, w, r_hi, r_lo, p):
                cols = slice(p * P, (p + 1) * P)
                return split_matmul(pe, bank, [(c[w + "_hi"][:, k, cols], c[w + "_lo"][:, k, cols],
                                                r_hi[:, k], r_lo[:, k]) for k in range(DK)])

            def queries(b, g, p):
                if p == 0:
                    pe.wait_ge(x_split, 2 * b + 2)
                heads(W0, "wq", x_hi, x_lo, p).then_inc(q_ps, 1)

            def keys(g, p):
                heads(W1, "wk", c_hi, c_lo, p).then_inc(k_ps, 1)

            def max_scores(g, p, h, t):
                par = p % 2
                pe.matmul((W0, W1)[t % 2], q1[:, par, h, t * P:(t + 1) * P], k1[:, par, h, :],
                          start=True, stop=True).then_inc(smax_ps, 1)

            def maxima_read(g, n):
                pe.wait_ge(smax_out, 8 * g + n)

            def operands_ready(g):
                pe.wait_ge(q_hi_out, 4 * g + 4)
                pe.wait_ge(k_lo_out, 2 * g + 2)

            def max_to_row(g, p, h):
                par, r = p % 2, slice(MAX_ROW[h], MAX_ROW[h] + 1)
                pe.wait_ge(nm_out, 4 * g + 2 * h + 2)
                for t in range(NT):
                    o = W2[r, t * P:(t + 1) * P]
                    pe.matmul(o, nm_hi[:, par, h, t:t + 1], c["ident"][:], start=True, stop=False)
                    mm = pe.matmul(o, nm_lo[:, par, h, t:t + 1], c["ident"][:], start=False, stop=True)
                mm.then_inc(row_ps, 1)

            def scores(g, p, h, s, first):
                par = p % 2
                if not (first and h == 0):
                    pe.wait_ge(exp_out, 4 * g + 2 * h + s - 1)
                for kt in (2 * s, 2 * s + 1):
                    cols = slice(kt * P, (kt + 1) * P)
                    pe.matmul(ps[:, kt, :], k1[:, par, h, cols], q1[:, par, h, :], start=True, stop=False)
                    mm = pe.matmul(ps[:, kt, :], k2[:, par, h, cols], q2[:, par, h, :], start=False, stop=True)
                mm.then_inc(st_ps, 1)

            def weighted_values(p, kt):
                for h in range(2):
                    cols = slice((2 * p + h) * DH, (2 * p + h + 1) * DH)
                    mm = pe.matmul(PV[OWN[h], :], v[:, kt, cols], prob[:, h, kt * T:(kt + 1) * T],
                                   start=(kt == 0), stop=(kt == NT - 1))
                return mm

            def sums(g):
                pe.wait_ge(acc_out, 4 * g + 4)
                for h in range(2):
                    mm = pe.matmul(W2[OWN[h], :], c["ones_w"][:, 0:DH], acc[:, h, :], start=True, stop=True)
                mm.then_inc(den_ps, 1)

            def values(b):
                for i in range(2 * NT):
                    kt, n = divmod(i, 2)
                    if i < 2:
                        maxima_read(PAIRS * b + 1, 3 + i)
                    else:
                        pe.wait_ge(v_out, 8 * b + i - 1)
                    split_matmul(pe, (W0, W1)[i % 2], [
                        (c_hi[:, k, kt * P:(kt + 1) * P], c_lo[:, k, kt * P:(kt + 1) * P],
                         c["wv_hi"][:, k, n * T:(n + 1) * T], c["wv_lo"][:, k, n * T:(n + 1) * T])
                        for k in range(DK)]).then_inc(v_ps, 1)

            def project(b, tail):
                pe.wait_ge(att_out, PAIRS * b + PAIRS)
                for m in range(DK):
                    if not tail:
                        pe.wait_ge(v_out, 8 * b + 15 + m)
                    full_matmul(pe, (W0, W1)[m], [(c["wo"][:, p, m * P:(m + 1) * P], att[:, p, :])
                                                  for p in range(PAIRS)]).then_inc(o_ps, 1)

            def batch(b, first, last):
                for p in range(PAIRS):
                    g = per_pair(b, p)
                    nxt = not (last and p == PAIRS - 1)
                    nxt2 = not (last and p >= PAIRS - 2)
                    pn = (p + 1) % PAIRS
                    head = first and p == 0
                    pe.wait_ge(row_out, 2 * g + 1)
                    pe.wait_ge(k_hi_out, 4 * g + 4)
                    pe.wait_ge(q_lo_out, 2 * g + 2)
                    if p < 2:
                        pe.wait_ge(k_mask, 4 * b + 2 * p + 2)
                    scores(g, p, 0, 0, head)
                    if nxt:
                        operands_ready(g + 1)
                        maxima_read(g, 7)
                        max_scores(g + 1, pn, 0, 0)
                    scores(g, p, 0, 1, head)
                    max_to_row(g, p, 1)
                    if nxt:
                        maxima_read(g, 8)
                        max_scores(g + 1, pn, 0, 1)
                        maxima_read(g + 1, 1)
                        max_scores(g + 1, pn, 0, 2)
                    pe.wait_ge(row_out, 2 * g + 2)
                    scores(g, p, 1, 0, head)
                    if nxt:
                        maxima_read(g + 1, 2)
                        max_scores(g + 1, pn, 0, 3)
                    if not head:
                        sums(g - 1)
                    scores(g, p, 1, 1, head)
                    if p == 0:
                        values(b)
                        if not first:
                            project(b - 1, False)
                    if nxt2:
                        if p == 0:
                            pe.wait_ge(v_out, 8 * b + 8)
                            if not first:
                                pe.wait_ge(o_out, 2 * b - 1)
                        else:
                            maxima_read(g + 1, 3)
                        queries(b if p < PAIRS - 2 else b + 1, g + 2, (p + 2) % PAIRS)
                        if p > 0:
                            maxima_read(g + 1, 4)
                        elif not first:
                            pe.wait_ge(o_out, 2 * b)
                        keys(g + 2, (p + 2) % PAIRS)
                    pe.wait_ge(exp_out, 4 * g + 3)
                    if not head:
                        pe.wait_ge(att_out, g)
                    weighted_values(p, 0)
                    if nxt:
                        if not head:
                            pe.wait_ge(newton, 2 * g - 1)
                        max_to_row(g + 1, pn, 0)
                    weighted_values(p, 1)
                    if nxt:
                        if nxt2:
                            pe.wait_ge(q_lo_out, 2 * g + 6)
                        max_scores(g + 1, pn, 1, 0)
                    pe.wait_ge(exp_out, 4 * g + 4)
                    weighted_values(p, 2)
                    if nxt:
                        if nxt2:
                            pe.wait_ge(k_lo_out, 2 * g + 6)
                        else:
                            maxima_read(g + 1, 4)
                        max_scores(g + 1, pn, 1, 1)
                    weighted_values(p, 3).then_inc(pv_ps, 1)
                    if nxt:
                        for t in (2, 3):
                            maxima_read(g + 1, NT + t - 1)
                            max_scores(g + 1, pn, 1, t)

            for m in range(DK):
                mm = full_matmul(pe, ps[:, m, 0:2], [(c["wo"][:, p, m * P:(m + 1) * P], c["bv"][:, :, p])
                                                     for p in range(PAIRS)])
            mm.then_inc(bias_ps, 1)
            for g in range(2):
                if g:
                    pe.wait_ge(q_lo_out, 2)
                    pe.wait_ge(k_lo_out, 2)
                queries(0, g, g)
                keys(g, g)
            pe.wait_ge(bias_out, 1)
            pe.wait_ge(q_hi_out, 4)
            pe.wait_ge(q_lo_out, 4)
            pe.wait_ge(k_lo_out, 4)
            for h in range(2):
                for t in range(NT):
                    if h or t > 1:
                        maxima_read(0, NT * h + t - 1)
                    max_scores(0, 0, h, t)
            max_to_row(0, 0, 0)
            batch(0, True, False)
            with pe.Fori(1, B - 1) as b:
                batch(b, False, False)
            batch(B - 1, False, True)
            sums(PAIRS * B - 1)
            project(B - 1, True)


def ffn_phase(nc, ctx, sb, a, c, ps, y2_dram, out):
    def sem(name):
        return ctx.enter_context(nc.semaphore("c_" + name))

    w_hi = sb(ctx, "wfc_hi", [P, DK, HID], F32R)
    w_lo = sb(ctx, "wfc_lo", [P, DK, HID], F32R)
    tern = sb(ctx, "tern", [P, HK, D], F32R)
    pscale = sb(ctx, "pscale", [P, DK], F32)
    ones2 = c["ones_w"][:, 0:2]

    def sems(*names):
        return [sem(n) for n in names]

    w_in, step, w_ps, ready = sems("w_in", "step", "w_ps", "ready")
    with ExitStack() as tmp:
        wfc = sb(tmp, "wfc_raw", [P, DK, HID], F32)
        wabs = sb(tmp, "wfc_abs", [P, DK, HID], F32)
        wpr = sb(tmp, "wpr_raw", [P, HK, D], F32)
        wpabs = sb(tmp, "wpr_abs", [P, HK, D], F32)
        bT = sb(tmp, "bT", [RANK, RANK], F32)
        vr = sb(tmp, "vr", [RANK, D], F32)
        uT = sb(tmp, "uT", [RANK, HID], F32)
        bv = sb(tmp, "bv_lr", [RANK, D], F32)
        gt = sb(tmp, "gt", [P, 1], F32)
        scale = sb(tmp, "scale", [P, HID], F32)
        up = sb(tmp, "up", [P, HID], F32)
        dn = sb(tmp, "dn", [P, HID], F32)
        full = sb(tmp, "wfull", [P, DK, HID], F32)
        pup = sb(tmp, "pup", [P, D], F32)
        pdn = sb(tmp, "pdn", [P, D], F32)
        psc = sb(tmp, "psc", [P, D], F32)
        with nc.Block() as block:
            @block.sync
            def _(sp):
                sp.dma_start(wfc[:], a["wfcT"].rearrange("(k p) n -> p k n", p=P)).then_inc(w_in, 16)
                sp.dma_start(wpr[:], a["wprojT"].rearrange("(k p) n -> p k n", p=P)).then_inc(w_in, 16)
                sp.dma_start(bT[:], a["fast_bT"]).then_inc(w_in, 16)
                sp.dma_start(vr[:], a["v"]).then_inc(w_in, 16)
                sp.dma_start(uT[:], a["uT"]).then_inc(w_in, 16)
                sp.dma_start(gt[:], a["gate"].partition_broadcast(P)).then_inc(w_in, 16)

            @block.scalar
            def _(act):
                act.wait_ge(w_in, 96)
                act.activation(wabs[:], wfc[:], ACT.Abs).then_inc(ready, 1)
                act.activation(wpabs[:], wpr[:], ACT.Abs).then_inc(ready, 1)

            @block.tensor
            def _(pe):
                pe.wait_ge(w_in, 96)
                pe.matmul(ps[0:RANK, 7, 0:D], bT[:], vr[:], start=True, stop=True).then_inc(w_ps, 1)
                pe.wait_ge(ready, 2)
                for n in range(2):
                    full_matmul(pe, ps[:, n, :], [(c["mean_w"][:], wabs[:, k, n * T:(n + 1) * T])
                                                  for k in range(DK)])
                full_matmul(pe, ps[:, 2, 0:D], [(c["ones_w"][:], wpabs[:, k, :]) for k in range(HK)])
                for m in range(DK):
                    mm = full_matmul(pe, ps[:, 2, D + 2 * m:D + 2 * m + 2],
                                     [(wpabs[:, k, m * P:(m + 1) * P], ones2) for k in range(HK)])
                mm.then_inc(w_ps, 1)
                pe.wait_ge(step, 1)
                for k in range(DK):
                    for n in range(2):
                        mm = pe.matmul(ps[:, 3 + 2 * k + n, :], bv[:, k * P:(k + 1) * P],
                                       uT[:, n * T:(n + 1) * T], start=True, stop=True)
                mm.then_inc(w_ps, 1)

            @block.vector
            def _(dve):
                done = [0]

                def then(ins):
                    done[0] += 1
                    ins.then_inc(step, 1)
                    dve.wait_ge(step, done[0])

                dve.wait_ge(w_ps, 1)
                then(dve.tensor_copy(bv[:], ps[0:RANK, 7, 0:D]))
                dve.wait_ge(w_ps, 2)
                then(dve.tensor_scalar(scale[:], ps[:, 0:2, :].rearrange("p a n -> p (a n)"), 1e-5, None, ALU.max))
                then(dve.tensor_scalar(psc[:], ps[:, 2, 0:D], 1.0 / HID, 1e-5, ALU.mult, ALU.max))
                then(dve.tensor_scalar(pscale[:], ps[:, 2, D:D + 2 * DK:2], 1.0 / HID, 1e-5, ALU.mult, ALU.max))
                dve.wait_ge(w_ps, 3)
                for k in range(DK):
                    then(dve.scalar_tensor_tensor(out=up[:], in0=scale[:], scalar=0.5, in1=wfc[:, k, :],
                                                  op0=ALU.mult, op1=ALU.is_lt))
                    then(dve.scalar_tensor_tensor(out=dn[:], in0=scale[:], scalar=-0.5, in1=wfc[:, k, :],
                                                  op0=ALU.mult, op1=ALU.is_gt))
                    then(dve.tensor_tensor(up[:], up[:], dn[:], ALU.subtract))
                    then(dve.tensor_tensor(up[:], up[:], scale[:], ALU.mult))
                    then(dve.scalar_tensor_tensor(
                        out=full[:, k, :], in0=ps[:, 3 + 2 * k:5 + 2 * k, :].rearrange("p a n -> p (a n)"),
                        scalar=gt[:, 0:1], in1=up[:], op0=ALU.mult, op1=ALU.add))
                then(dve.tensor_copy(w_hi[:], full[:]))
                then(dve.tensor_tensor(w_lo[:], full[:], f32(w_hi[:]), ALU.subtract))
                for k in range(HK):
                    then(dve.scalar_tensor_tensor(out=pup[:], in0=psc[:], scalar=0.5, in1=wpr[:, k, :],
                                                  op0=ALU.mult, op1=ALU.is_lt))
                    then(dve.scalar_tensor_tensor(out=pdn[:], in0=psc[:], scalar=-0.5, in1=wpr[:, k, :],
                                                  op0=ALU.mult, op1=ALU.is_gt))
                    then(dve.tensor_tensor(tern[:, k, :], pup[:], pdn[:], ALU.subtract))

    y2 = sb(ctx, "y2_c", [P, DK, T], F32)
    dev2, sq2 = (sb(ctx, n, [P, DK, T], F32) for n in ("dev2", "sq2"))
    var2, est2, inv2, rs2 = (sb(ctx, n + "2", [P, T], F32) for n in ("var", "est", "inv", "rs"))
    x2 = sb(ctx, "x2", [P, 2, DK, T], F32)
    x_hi, x_lo = (sb(ctx, "cx_" + n, [P, 2, DK, T], F32R) for n in ("hi", "lo"))
    RH = 4
    r = sb(ctx, "relu", [P, RH, T], F32)
    rr = sb(ctx, "relu2", [P, RH, T], F32)
    h_hi, h_lo = (sb(ctx, "h_" + n, [P, HK, T], F32R) for n in ("hi", "lo"))
    y3 = sb(ctx, "y3", [P, DK, T], F32)
    dev3, sq3, x3 = (sb(ctx, n, [P, DK, T], F32) for n in ("dev3", "sq3", "x3"))
    var3, est3, inv3, rs3 = (sb(ctx, n + "3", [P, T], F32) for n in ("var", "est", "inv", "rs"))

    y_in, stored = sems("y_in", "stored")
    mean2_ps, dev2_out, sq2_out, var2_ps, var2_out, est2_out, rs2_out, x2_out = sems(
        "mean2_ps", "dev2_out", "sq2_out", "var2_ps", "var2_out", "est2_out", "rs2_out", "x2_out")
    mean3_ps, dev3_out, sq3_out, var3_ps, var3_out, est3_out, rs3_out, x3_out = sems(
        "mean3_ps", "dev3_out", "sq3_out", "var3_ps", "var3_out", "est3_out", "rs3_out", "x3_out")
    x_split, h_ps, relu_out, hi_out, rr_out, lo_out, p_ps, y3_out = sems(
        "x_split", "h_ps", "relu_out", "hi_out", "rr_out", "lo_out", "p_ps", "y3_out")

    HIDDEN = [ps[:, i, :] for i in (0, 1, 2, 7)]
    STAT3, STAT2 = ps[:, 3, :], ps[:, 4, :]
    OUT = ps[:, 5:7, :]

    def both(tile):
        return tile[:].rearrange("p (o t) -> p o t", o=1).to_broadcast([P, DK, T])

    with nc.Block() as block:
        @block.sync
        def _(sp):
            def load(b):
                sp.dma_start(y2[:], batch_cols(y2_dram, b)).then_inc(y_in, 16)

            def store(b):
                sp.wait_ge(x3_out, b + 1)
                sp.dma_start(batch_cols(out, b), x3[:]).then_inc(stored, 16)

            load(0)
            sp.wait_ge(dev2_out, 1)
            load(1)
            sp.wait_ge(dev2_out, 2)
            load(2)
            with sp.Fori(3, B) as b:
                sp.wait_ge(dev2_out, b)
                load(b)
                store(b - 3)
            for b in (B - 3, B - 2, B - 1):
                store(b)
            sp.wait_ge(stored, 16 * B)

        @block.gpsimd
        def _(pool):
            def batch(b, first):
                for i in range(HK):
                    pool.wait_ge(relu_out, HK * b + i + 1)
                    if not (first and i < RH):
                        pool.wait_ge(lo_out, HK * b + i - RH + 1)
                    n = i % RH
                    pool.tensor_tensor(rr[:, n, :], r[:, n, :], r[:, n, :], ALU.mult).then_inc(rr_out, 1)

            batch(0, True)
            with pool.Fori(1, B) as b:
                batch(b, False)

        @block.scalar
        def _(act):
            def norm_square(dev, sq, dev_out, sq_out, b):
                act.wait_ge(dev_out, b + 1)
                act.activation(sq[:], dev[:], ACT.Square).then_inc(sq_out, 1)

            def norm_root(stat, norm, sems, b, first):
                var, est, inv = norm
                var_ps, var_out, est_out, rs_out = sems
                act.wait_ge(var_ps, b + 1)
                if not first:
                    act.wait_ge(rs_out, 2 * b)
                act.activation(var[:], stat, ACT.Identity, bias=c["eps"][:, 0:1]).then_inc(var_out, 1)
                act.wait_ge(var_out, b + 1)
                act.activation(inv[:], var[:], ACT.Ln).then_inc(est_out, 1)
                act.wait_ge(est_out, 3 * b + 1)
                act.activation(est[:], inv[:], ACT.Exp, scale=-0.5).then_inc(est_out, 1)
                act.wait_ge(est_out, 3 * b + 2)
                act.activation(inv[:], est[:], ACT.Square).then_inc(est_out, 1)

            def norm2_root(b, first):
                norm_root(STAT2, (var2, est2, inv2), (var2_ps, var2_out, est2_out, rs2_out), b, first)

            def norm3_root(b, first):
                norm_root(STAT3, (var3, est3, inv3), (var3_ps, var3_out, est3_out, rs3_out), b, first)

            def hidden(b, i, first):
                n = HK * b + i
                act.wait_ge(h_ps, n + 1)
                if not (first and i < RH):
                    act.wait_ge(rr_out, n - RH + 1)
                act.activation(r[:, i % RH, :], HIDDEN[i % RH], ACT.Relu).then_inc(relu_out, 1)
                act.wait_ge(relu_out, n + 1)
                if i == 0 and not first:
                    act.wait_ge(p_ps, 2 * b)
                act.activation(h_hi[:, i, :], r[:, i % RH, :], ACT.Square).then_inc(hi_out, 1)

            def batch(b, first, second, last):
                for i in (0, 1, 2):
                    hidden(b, i, first)
                if not last:
                    norm_square(dev2, sq2, dev2_out, sq2_out, b + 1)
                for i in (3, 4):
                    hidden(b, i, first)
                if not first:
                    norm_square(dev3, sq3, dev3_out, sq3_out, b - 1)
                hidden(b, 5, first)
                if not last:
                    norm2_root(b + 1, False)
                for i in (6, 7):
                    hidden(b, i, first)
                if not first:
                    norm3_root(b - 1, second)

            act.preload_act_table_set("natural_log_exp_and_others")
            norm_square(dev2, sq2, dev2_out, sq2_out, 0)
            norm2_root(0, True)
            batch(0, True, False, False)
            batch(1, False, True, False)
            with act.Fori(2, B - 1) as b:
                batch(b, False, False, False)
            batch(B - 1, False, False, True)
            norm_square(dev3, sq3, dev3_out, sq3_out, B - 1)
            norm3_root(B - 1, False)

        @block.vector
        def _(dve):
            def deviate2(b, first):
                dve.wait_ge(mean2_ps, b + 1)
                if not first:
                    dve.wait_ge(x2_out, b)
                dve.tensor_tensor(dev2[:], y2[:], both(STAT2_T), ALU.subtract).then_inc(dev2_out, 1)

            def inverse_root(norm, est_out, rs_out, b):
                var, est, inv, rs = norm
                dve.wait_ge(est_out, 3 * b + 3)
                dve.scalar_tensor_tensor(out=rs[:], in0=inv[:], scalar=-0.5, in1=var[:], op0=ALU.mult,
                                         op1=ALU.mult).then_inc(rs_out, 1)
                dve.wait_ge(rs_out, 2 * b + 1)
                dve.scalar_tensor_tensor(out=rs[:], in0=rs[:], scalar=1.5, in1=est[:], op0=ALU.add,
                                         op1=ALU.mult).then_inc(rs_out, 1)
                dve.wait_ge(rs_out, 2 * b + 2)

            def normalise2(b, par, first):
                inverse_root((var2, est2, inv2, rs2), est2_out, rs2_out, b)
                if not (isinstance(b, int) and b < 2):
                    dve.wait_ge(y3_out, 2 * b - 2)
                dve.tensor_tensor(x2[:, par], dev2[:], both(rs2), ALU.mult).then_inc(x2_out, 1)
                dve.wait_ge(x2_out, b + 1)
                if not (isinstance(b, int) and b < 2):
                    dve.wait_ge(h_ps, HK * b - HK)
                dve.tensor_copy(x_hi[:, par], x2[:, par]).then_inc(x_split, 1)
                dve.wait_ge(x_split, 2 * b + 1)
                dve.tensor_tensor(x_lo[:, par], x2[:, par], f32(x_hi[:, par]), ALU.subtract).then_inc(x_split, 1)

            def hidden_lo(b, i):
                n = HK * b + i
                dve.wait_ge(hi_out, n + 1)
                dve.wait_ge(rr_out, n + 1)
                dve.tensor_tensor(h_lo[:, i, :], rr[:, i % RH, :], f32(h_hi[:, i, :]), ALU.subtract).then_inc(lo_out, 1)

            def residual(b, par, first):
                for m in range(DK):
                    dve.wait_ge(p_ps, 2 * b + m + 1)
                    if m == 0 and not first:
                        dve.wait_ge(dev3_out, b)
                    dve.scalar_tensor_tensor(out=y3[:, m], in0=OUT[:, m], scalar=pscale[:, m:m + 1],
                                             in1=x2[:, par, m], op0=ALU.mult, op1=ALU.add).then_inc(y3_out, 1)

            def deviate3(b, first):
                dve.wait_ge(mean3_ps, b + 1)
                if not first:
                    dve.wait_ge(x3_out, b)
                dve.tensor_tensor(dev3[:], y3[:], both(STAT3_T), ALU.subtract).then_inc(dev3_out, 1)

            def normalise3(b, first):
                inverse_root((var3, est3, inv3, rs3), est3_out, rs3_out, b)
                if not first:
                    dve.wait_ge(stored, 16 * b)
                dve.tensor_tensor(x3[:], dev3[:], both(rs3), ALU.mult).then_inc(x3_out, 1)

            STAT2_T, STAT3_T = ps[:, 4, :], ps[:, 3, :]

            def batch(b, par, first, second, last):
                if not first:
                    residual(b - 1, 1 - par, second)
                hidden_lo(b, 0)
                hidden_lo(b, 1)
                if not last:
                    deviate2(b + 1, False)
                hidden_lo(b, 2)
                hidden_lo(b, 3)
                if not first:
                    deviate3(b - 1, second)
                for i in (4, 5, 6, 7):
                    hidden_lo(b, i)
                if not last:
                    normalise2(b + 1, 1 - par, False)
                if not first:
                    normalise3(b - 1, second)

            deviate2(0, True)
            normalise2(0, 0, True)
            batch(0, 0, True, False, False)
            batch(1, 1, False, True, False)
            with dve.Fori(2, B - 3, 2) as i:
                batch(i, 0, False, False, False)
                batch(i + 1, 1, False, False, False)
            batch(B - 2, 0, False, False, False)
            batch(B - 1, 1, False, False, True)
            residual(B - 1, 1, False)
            deviate3(B - 1, False)
            normalise3(B - 1, False)

        @block.tensor
        def _(pe):
            def mean2(b, first):
                pe.wait_ge(y_in, 16 * b + 16)
                if not first:
                    pe.wait_ge(var2_out, b)
                full_matmul(pe, STAT2, [(c["mean_w"][:], y2[:, k]) for k in range(DK)]).then_inc(mean2_ps, 1)

            def var2(b):
                pe.wait_ge(sq2_out, b + 1)
                full_matmul(pe, STAT2, [(c["mean_w"][:], sq2[:, k]) for k in range(DK)]).then_inc(var2_ps, 1)

            def mean3(b, first):
                pe.wait_ge(y3_out, 2 * b + 2)
                if not first:
                    pe.wait_ge(var3_out, b)
                full_matmul(pe, STAT3, [(c["mean_w"][:], y3[:, k]) for k in range(DK)]).then_inc(mean3_ps, 1)

            def var3(b):
                pe.wait_ge(sq3_out, b + 1)
                full_matmul(pe, STAT3, [(c["mean_w"][:], sq3[:, k]) for k in range(DK)]).then_inc(var3_ps, 1)

            def hidden(b, par, i, first):
                if i == 0:
                    pe.wait_ge(x_split, 2 * b + 2)
                if not (first and i < RH):
                    pe.wait_ge(relu_out, HK * b + i - RH + 1)
                cols = slice(i * P, (i + 1) * P)
                split_matmul(pe, HIDDEN[i % RH], [(w_hi[:, k, cols], w_lo[:, k, cols], x_hi[:, par, k],
                                                   x_lo[:, par, k]) for k in range(DK)]).then_inc(h_ps, 1)

            def project(b, m, tiles):
                for k in tiles:
                    pe.wait_ge(lo_out, HK * b + k + 1)
                    w = tern[:, k, m * P:(m + 1) * P]
                    pe.matmul(OUT[:, m], w, h_hi[:, k, :], start=(k == 0), stop=False)
                    mm = pe.matmul(OUT[:, m], w, h_lo[:, k, :], start=False, stop=(k == HK - 1))
                if tiles[-1] == HK - 1:
                    mm.then_inc(p_ps, 1)

            def batch(b, par, first, second, last):
                for i in (0, 1):
                    hidden(b, par, i, first)
                if not last:
                    mean2(b + 1, False)
                for i in (2, 3):
                    hidden(b, par, i, first)
                if not first:
                    mean3(b - 1, second)
                for i in (4, 5):
                    hidden(b, par, i, first)
                if not last:
                    var2(b + 1)
                for i in (6, 7):
                    hidden(b, par, i, first)
                if not first:
                    pe.wait_ge(y3_out, 2 * b)
                project(b, 0, range(0, 6))
                if not first:
                    var3(b - 1)
                project(b, 0, (6, 7))
                project(b, 1, range(HK))

            mean2(0, True)
            var2(0)
            batch(0, 0, True, False, False)
            batch(1, 1, False, True, False)
            with pe.Fori(2, B - 3, 2) as i:
                batch(i, 0, False, False, False)
                batch(i + 1, 1, False, False, False)
            batch(B - 2, 0, False, False, False)
            batch(B - 1, 1, False, False, True)
            mean3(B - 1, False)
            var3(B - 1)


def kernel(**inputs):
    import numpy as np
    import concourse.bacc as bacc
    from concourse.bass_utils import run_bass_kernel_spmd

    i = {k: np.asarray(v) for k, v in inputs.items()}

    def columns(v):
        return v.reshape(-1, P).T

    key, query = np.arange(P)[:, None], np.arange(P)[None, :]
    diff = query - key
    seen = (diff >= 0) & (key // CHUNK == query // CHUNK)
    bits = np.stack([((diff >> j) & 1) * seen for j in range(5)] + [seen], 1).astype(np.float32)
    arrays = {
        "xT": i["x"].reshape(B * T, D).T, "cT": i["ctx_1024"].reshape(B * T, D).T,
        "mask": i["mask_BxS2_bf1"].view(np.uint8),
        "l0_Wq": i["L0_attn_W_q"], "l0_Wk": i["L0_attn_W_k"], "l0_WvT": i["L0_attn_W_v"].T,
        "l0_WgT": i["L0_attn_W_g"].T, "l0_WoT": i["L0_attn_W_o"].T,
        "log_decay": i["L0_attn_log_decay"].reshape(1, D),
        "Wq": i["L0_xattn_Wq"], "Wk": i["L0_xattn_Wk"], "Wv": i["L0_xattn_Wv"], "Wo": i["L0_xattn_Wo"],
        "bq": columns(i["L0_xattn_bq"]), "bk": columns(i["L0_xattn_bk"]), "bo": columns(i["L0_xattn_bo"]),
        "bv": columns(i["L0_xattn_bv"]),
        "fast_bT": i["L0_ffn_fast_b"].T, "wfcT": i["L0_ffn_w_fc"].T, "wprojT": i["L0_ffn_w_proj"].T,
        "uT": i["L0_ffn_u"].T, "v": i["L0_ffn_v"], "gate": i["L0_ffn_gate"].reshape(1, 1),
        "ident": np.eye(P, dtype=np.float32), "bits": bits,
    }
    nc = bacc.Bacc("TRN2", target_bir_lowering=False, num_devices=1)
    sent, aps = {}, {}
    for name, v in arrays.items():
        v = np.ascontiguousarray(v)
        sent[f"in_{name}"] = v
        aps[name] = nc.dram_tensor(f"in_{name}", v.shape, mybir.dt.from_np(v.dtype), kind="ExternalInput").ap()
    out = nc.dram_tensor("outT", (D, B * T), F32, kind="ExternalOutput").ap()
    decoder_layer(nc, aps, out)
    got = run_bass_kernel_spmd(nc, [sent], core_ids=[0]).results[0]["outT"]
    return got.T.reshape(B, T, D)
```

```python
from contextlib import ExitStack

import concourse.bass as bass
from concourse import mybir

ACT = mybir.ActivationFunctionType
ALU = mybir.AluOpType
AX = mybir.AxisListType
F32 = mybir.dt.float32
F32R = mybir.dt.float32r
BF16 = mybir.dt.bfloat16
U8 = mybir.dt.uint8

P = 128
B, T, D = 8, 512, 256
DK = D // P
NT = T // P
CHUNK = 32
HEADS, DH = 16, 64
HD = HEADS * DH
PAIRS = HEADS // 2
HID = 1024
HK = HID // P
RANK = 16
EPS = 1e-5
MASKED = -1e30
LOWEST = -3e38
SCALE = DH ** -0.5


def split_matmul(pe, out, terms):
    n = len(terms)
    for i, (lh, ll, rh, rl) in enumerate(terms):
        pe.matmul(out, lh, rh, start=(i == 0), stop=False)
        pe.matmul(out, lh, rl, start=False, stop=False)
        mm = pe.matmul(out, ll, rh, start=False, stop=(i == n - 1))
    return mm


def full_matmul(pe, out, terms):
    for i, (l, r) in enumerate(terms):
        mm = pe.matmul(out, l, r, start=(i == 0), stop=(i == len(terms) - 1))
    return mm


def f32(ap):
    return ap.bitcast(F32)


def batch_cols(dram, b):
    v = dram.rearrange("(k p) (b t) -> b p k t", p=P, t=T)
    if isinstance(b, int):
        return v[b]
    return v[bass.ds(b, 1)].rearrange("b p k t -> (b p) k t")


def row_of(dram, b):
    return dram[b:b + 1, :] if isinstance(b, int) else dram[bass.ds(b, 1), :]


def decoder_layer(nc, a, out):
    x1_dram = nc.dram_tensor("x1_scratch", [D, B * T], F32, kind="Internal").ap()
    y2_dram = nc.dram_tensor("y2_scratch", [D, B * T], F32, kind="Internal").ap()
    with ExitStack() as whole:
        def sb(ctx, name, shape, dt):
            return ctx.enter_context(nc.sbuf_tensor(name, shape, dt))

        c = {}
        c["mean_w"] = sb(whole, "mean_w", [P, P], F32)
        c["ones_w"] = sb(whole, "ones_w", [P, P], F32)
        c["ident"] = sb(whole, "ident", [P, P], BF16)
        c["eps"] = sb(whole, "eps", [P, 1], F32)
        c["wfc"] = sb(whole, "wfc", [P, DK, HID], F32)
        c["tern"] = sb(whole, "tern", [P, HK, D], BF16)
        c["pscale"] = sb(whole, "pscale", [P, DK], F32)
        c["y2"] = sb(whole, "y2_c", [P, DK, T], F32)
        ps = whole.enter_context(nc.psum_tensor("ps", [P, 8, T], F32))
        with ExitStack() as attention:
            for w in ("wq", "wk", "wv"):
                c[w + "_hi"] = sb(attention, w + "_hi", [P, DK, HD], F32R)
                c[w + "_lo"] = sb(attention, w + "_lo", [P, DK, HD], F32R)
            c["raw"] = sb(attention, "raw", [P, 2, DK, T], F32)
            c["wo"] = sb(attention, "wo", [P, PAIRS, D], F32)
            c["bq"] = sb(attention, "bq", [P, PAIRS], F32)
            c["bk"] = sb(attention, "bk", [P, PAIRS], F32)
            c["bo"] = sb(attention, "bo", [P, DK], F32)
            c["bv"] = sb(attention, "bv", [P, 2, PAIRS], F32)
            with ExitStack() as ctx:
                linear_attention_phase(nc, ctx, sb, a, c, ps, x1_dram)
            with ExitStack() as ctx:
                cross_attention_phase(nc, ctx, sb, a, c, ps, x1_dram, y2_dram)
        with ExitStack() as ctx:
            ffn_phase(nc, ctx, sb, a, c, ps, y2_dram, out)


def linear_attention_phase(nc, ctx, sb, a, c, ps, x1_dram):
    def sem(name):
        return ctx.enter_context(nc.semaphore("a_" + name))

    ident_f = sb(ctx, "ident_f", [P, P], F32)
    bits = sb(ctx, "bits", [P, 6, P], F32)
    nbit = sb(ctx, "nbit", [P, P], F32)
    decay = sb(ctx, "decay", [P, 6], F32)
    factor = sb(ctx, "factor", [P, P], F32)
    dmask = sb(ctx, "dmask", [P, P], F32)
    raw = {w: sb(ctx, w + "_l0", [P, DK, D], F32) for w in ("Wq", "Wk", "WvT", "WgT", "WoT")}
    wv = raw["WvT"]
    w_hi = {w: sb(ctx, w + "_l0_hi", [P, DK, D], F32R) for w in ("M", "WgT", "WoT")}
    w_lo = {w: sb(ctx, w + "_l0_lo", [P, DK, D], F32R) for w in ("M", "WgT", "WoT")}
    stage = c["raw"][:].rearrange("p k i t -> p k (i t)")
    x = sb(ctx, "x_in", [P, 2, DK, T], F32)
    x_hi = sb(ctx, "x_hi", [P, 2, DK, T], F32R)
    x_lo = sb(ctx, "x_lo", [P, 2, DK, T], F32R)
    qm = sb(ctx, "qm", [P, DK, T], F32)
    gate = sb(ctx, "gate", [P, DK, T], F32)
    v = sb(ctx, "v_tok", [P, NT, D], F32)
    s = sb(ctx, "s_masked", [P, NT, P], F32)
    og_hi = sb(ctx, "og_hi", [P, DK, T], F32R)
    og_lo = sb(ctx, "og_lo", [P, DK, T], F32R)
    y = sb(ctx, "y_a", [P, DK, T], F32)
    dev = sb(ctx, "dev_a", [P, DK, T], F32)
    sq = sb(ctx, "sq_a", [P, DK, T], F32)
    og = sq
    tile_sum = sb(ctx, "tile_sum_a", [P, T], F32)
    rs = sb(ctx, "rs_a", [P, T], F32)
    x1 = sb(ctx, "x1_a", [P, DK, T], F32)
    wfc = sb(ctx, "wfc_raw", [P, DK, HID], F32)
    wpr = sb(ctx, "wpr_raw", [P, HK, D], F32)
    uT = sb(ctx, "uT", [RANK, HID], F32)
    bT = sb(ctx, "bT", [RANK, RANK], F32)
    vr = sb(ctx, "vr", [RANK, D], F32)
    mid = sb(ctx, "mid", [RANK, D], F32)
    gt = sb(ctx, "gt", [P, 1], F32)
    scale = sb(ctx, "scale", [P, HID], F32)
    psc = sb(ctx, "psc", [P, D], F32)
    above = sb(ctx, "above", [P, DK, HID], BF16)
    wabs = c["wfc"]

    qk_in, gate_w_in = sem("qk_in"), sem("gate_w_in")
    consts_in, w_in, vec_in, stage_in = sem("consts_in"), sem("w_in"), sem("vec_in"), sem("stage_in")
    setup, decay_in, sig_done = sem("setup"), sem("decay_in"), sem("sig_done")
    pow_step, m_ps, w_split = sem("pow_step"), sem("m_ps"), sem("w_split")
    stage_split, next_in = sem("stage_split"), sem("next_in")
    x_in, x_split = [sem("x_in_even"), sem("x_in_odd")], sem("x_split")
    qm_ps, qm_out, g_ps, g_out = sem("qm_ps"), sem("qm_out"), sem("g_ps"), sem("g_out")
    v_ps, v_out, s_ps, s_out = sem("v_ps"), sem("v_out"), sem("s_ps"), sem("s_out")
    o_ps, gate_used, og_split = sem("o_ps"), sem("gate_used"), sem("og_split")
    y_ps, y_out = sem("y_ps"), sem("y_out")
    y_sum_out, sq_sum_out = sem("y_sum_out"), sem("sq_sum_out")
    mean_ps, dev_out, sq_out, var_ps = sem("mean_ps"), sem("dev_out"), sem("sq_out"), sem("var_ps")
    sd_out, rs_out, x1_out, stored = sem("sd_out"), sem("rs_out"), sem("x1_out"), sem("stored")
    f_in, f_abs, f_sum = sem("f_in"), sem("f_abs"), sem("f_sum")
    f_mid_ps, f_mid = sem("f_mid_ps"), sem("f_mid")
    f_ps, f_scale, f_low_ps, f_low = sem("f_ps"), sem("f_scale"), sem("f_low_ps"), sem("f_low")
    f_above, f_below, f_step = sem("f_above"), sem("f_below"), sem("f_step")
    STAGED = ("Wq", "Wk", "Wv")

    QO, G, VY, S, ST = ps[:, 0:2, :], ps[:, 2:4, :], ps[:, 4:6, :], ps[:, 6, :], ps[:, 7, :]

    with nc.Block() as block:
        @block.sync
        def _(sp):
            def load_weight(w, done):
                sp.dma_start(raw[w][:], a["l0_" + w].rearrange("(k p) n -> p k n", p=P)).then_inc(done, 16)

            load_weight("Wq", qk_in)
            load_weight("Wk", qk_in)
            sp.dma_start(x[:, 0], batch_cols(a["xT"], 0)).then_inc(x_in[0], 16)
            load_weight("WgT", gate_w_in)
            sp.dma_start(decay[:, 5:6], a["log_decay"][:, 0:1].partition_broadcast(P)).then_inc(decay_in, 16)
            load_weight("WoT", w_in)
            load_weight("WvT", w_in)
            sp.dma_start(ident_f[:], a["ident"]).then_inc(consts_in, 16)
            sp.dma_start(bits[:], a["bits"]).then_inc(consts_in, 16)
            sp.dma_start(x[:, 1], batch_cols(a["xT"], 1)).then_inc(x_in[1], 16)
            sp.dma_start(wfc[:], a["wfcT"].rearrange("(k p) n -> p k n", p=P)).then_inc(f_in, 16)
            sp.dma_start(wpr[:], a["wprojT"].rearrange("(k p) n -> p k n", p=P)).then_inc(f_in, 16)
            sp.dma_start(bT[:], a["fast_bT"]).then_inc(f_in, 16)
            sp.dma_start(vr[:], a["v"]).then_inc(f_in, 16)
            sp.dma_start(uT[:], a["uT"]).then_inc(f_in, 16)
            sp.dma_start(gt[:], a["gate"].partition_broadcast(P)).then_inc(f_in, 16)
            sp.dma_start(c["wo"][:], a["Wo"].rearrange("(k p) n -> p k n", p=P)).then_inc(vec_in, 16)
            sp.dma_start(c["bq"][:], a["bq"]).then_inc(vec_in, 16)
            sp.dma_start(c["bk"][:], a["bk"]).then_inc(vec_in, 16)
            sp.dma_start(c["bo"][:], a["bo"]).then_inc(vec_in, 16)
            for i in range(2):
                sp.dma_start(c["bv"][:, i, :], a["bv"]).then_inc(vec_in, 16)

            def load_and_store(b, par):
                sp.wait_ge(y_out, 2 * b - 2)
                sp.dma_start(x[:, par], batch_cols(a["xT"], b)).then_inc(x_in[par], 16)
                sp.wait_ge(x1_out, b - 1)
                sp.dma_start(batch_cols(x1_dram, b - 2), x1[:]).then_inc(stored, 16)

            with sp.Fori(2, B - 1, 2) as b:
                load_and_store(b, 0)
                load_and_store(b + 1, 1)
            sp.wait_ge(stage_split, 2 * len(STAGED))
            sp.wait_ge(stored, 16 * (B - 2))
            sp.dma_start(c["raw"][:, 0], batch_cols(x1_dram, 0)).then_inc(next_in, 16)
            sp.dma_start(c["raw"][:, 1], batch_cols(a["cT"], 0)).then_inc(next_in, 16)
            for b in (B - 2, B - 1):
                sp.wait_ge(x1_out, b + 1)
                sp.dma_start(batch_cols(x1_dram, b), x1[:]).then_inc(stored, 16)
            sp.wait_ge(next_in, 32)
            sp.wait_ge(stored, 16 * B)
            sp.wait_ge(vec_in, 16 * 6)

        @block.gpsimd
        def _(pool):
            pool.wait_ge(x_in[1], 16)
            for i, w in enumerate(("wq", "wk", "wv")):
                if i:
                    pool.wait_ge(stage_split, 2 * i)
                pool.dma_start(stage, a[STAGED[i]].rearrange("(k p) n -> p k n", p=P)).then_inc(stage_in, 16)
                pool.wait_ge(stage_in, 16 * (i + 1))
                pool.tensor_copy(c[w + "_hi"][:], stage).then_inc(stage_split, 1)
                pool.wait_ge(stage_split, 2 * i + 1)
                pool.tensor_tensor(c[w + "_lo"][:], stage, f32(c[w + "_hi"][:]),
                                   ALU.subtract).then_inc(stage_split, 1)
            for k in range(DK):
                n = 3 * k
                pool.wait_ge(f_above, k + 1)
                pool.wait_ge(f_below, k + 1)
                pool.tensor_tensor(wfc[:, k], above[:, k], wfc[:, k], ALU.subtract).then_inc(f_step, 1)
                pool.wait_ge(f_step, n + 1)
                pool.tensor_tensor(wfc[:, k], wfc[:, k], scale[:], ALU.mult).then_inc(f_step, 1)
                pool.wait_ge(f_step, n + 2)
                pool.tensor_tensor(c["wfc"][:, k], c["wfc"][:, k], wfc[:, k], ALU.add).then_inc(f_step, 1)
            pool.wait_ge(f_above, DK + 1)
            pool.wait_ge(f_below, DK + 1)
            pool.tensor_tensor(c["tern"][:], c["tern"][:], wpr[:], ALU.subtract).then_inc(f_step, 1)

        @block.scalar
        def _(act):
            act.wait_ge(setup, 3)
            act.wait_ge(decay_in, 16)
            act.activation(decay[:, 0:1], decay[:, 5:6], ACT.Sigmoid).then_inc(sig_done, 1)

            def front(b):
                act.wait_ge(g_ps, b + 1)
                if not (isinstance(b, int) and b == 0):
                    act.wait_ge(gate_used, b)
                act.activation(gate[:], G, ACT.Sigmoid).then_inc(g_out, 1)
                for m in range(DK):
                    act.wait_ge(qm_ps, 2 * b + m + 1)
                    if m == 0 and not (isinstance(b, int) and b == 0):
                        act.wait_ge(s_ps, b)
                    act.activation(qm[:, m], QO[:, m], ACT.Copy).then_inc(qm_out, 1)

            def square(b):
                act.wait_ge(dev_out, b + 1)
                if not (isinstance(b, int) and b == 0):
                    act.wait_ge(sq_sum_out, b)
                act.activation(sq[:], dev[:], ACT.Square).then_inc(sq_out, 1)

            def values(b):
                for n in range(2):
                    act.wait_ge(v_ps, 2 * b + n + 1)
                    act.activation(v[:, 2 * n:2 * n + 2], VY[:, n].rearrange("p (t n) -> p t n", n=D),
                                   ACT.Copy).then_inc(v_out, 1)

            def deviation(b):
                act.wait_ge(var_ps, b + 1)
                act.activation(rs[:], ST, ACT.Sqrt, bias=c["eps"][:, 0:1]).then_inc(sd_out, 1)

            front(0)
            act.wait_ge(f_in, 96)
            act.activation(wabs[:], wfc[:], ACT.Abs).then_inc(f_abs, 1)
            values(0)
            act.wait_ge(f_sum, 1)
            act.activation(wabs[:].rearrange("p k (j n) -> p (k j) n", n=D), wpr[:], ACT.Abs).then_inc(f_abs, 1)
            front(1)
            square(0)
            values(1)
            deviation(0)
            with act.Fori(2, B - 1, 2) as i:
                for b in (i, i + 1):
                    front(b)
                    square(b - 1)
                    values(b)
                    deviation(b - 1)
            square(B - 1)
            deviation(B - 1)

        @block.vector
        def _(dve):
            dve.memset(c["mean_w"][:], 1.0 / D).then_inc(setup, 1)
            dve.memset(c["ones_w"][:], 1.0).then_inc(setup, 1)
            dve.memset(c["eps"][:], EPS).then_inc(setup, 1)

            def split_x(b, par):
                dve.wait_ge(x_in[par], 8 * (b - par) + 16)
                if not (isinstance(b, int) and b < 2):
                    dve.wait_ge(qm_ps, 2 * b - 2)
                dve.tensor_copy(x_hi[:, par], x[:, par]).then_inc(x_split, 1)
                dve.wait_ge(x_split, 2 * b + 1)
                dve.tensor_tensor(x_lo[:, par], x[:, par], f32(x_hi[:, par]), ALU.subtract).then_inc(x_split, 1)

            split_x(0, 0)
            for i, w in enumerate(("WgT", "M", "WoT")):
                if w == "M":
                    dve.wait_ge(m_ps, 1)
                    src = ps[:, 0, :].rearrange("p (k n) -> p k n", k=DK)
                elif w == "WgT":
                    dve.wait_ge(gate_w_in, 16)
                    src = raw[w][:]
                else:
                    dve.wait_ge(w_in, 32)
                    src = raw[w][:]
                dve.tensor_copy(w_hi[w][:], src).then_inc(w_split, 1)
                dve.wait_ge(w_split, 2 * i + 1)
                dve.tensor_tensor(w_lo[w][:], src, f32(w_hi[w][:]), ALU.subtract).then_inc(w_split, 1)
            dve.wait_ge(consts_in, 32)
            dve.wait_ge(sig_done, 1)
            dve.tensor_copy(c["ident"][:], ident_f[:]).then_inc(setup, 1)
            dve.tensor_copy(dmask[:], bits[:, 5, :]).then_inc(pow_step, 1)
            n = 1
            for j in range(5):
                dve.tensor_scalar(nbit[:], bits[:, j, :], -1.0, 1.0, ALU.mult, ALU.add).then_inc(pow_step, 1)
                n += 1
                dve.wait_ge(pow_step, n)
                dve.scalar_tensor_tensor(out=factor[:], in0=bits[:, j, :], scalar=decay[:, j:j + 1],
                                         in1=nbit[:], op0=ALU.mult, op1=ALU.add).then_inc(pow_step, 1)
                dve.wait_ge(pow_step, n + 1)
                dve.tensor_tensor(dmask[:], dmask[:], factor[:], ALU.mult).then_inc(pow_step, 1)
                n += 2
                if j < 4:
                    dve.tensor_tensor(decay[:, j + 1:j + 2], decay[:, j:j + 1], decay[:, j:j + 1],
                                      ALU.mult).then_inc(pow_step, 1)
                    n += 1
            dve.wait_ge(pow_step, n)

            def finish_y(b, par):
                for m in range(DK):
                    dve.wait_ge(y_ps, 2 * b + m + 1)
                    if m == 0 and not (isinstance(b, int) and b == 0):
                        dve.wait_ge(dev_out, b)
                    dve.scalar_tensor_tensor(out=y[:, m], in0=x[:, par, m], scalar=2.0, in1=VY[:, m],
                                             op0=ALU.mult, op1=ALU.add).then_inc(y_out, 1)
                dve.wait_ge(y_out, 2 * b + 2)
                if not (isinstance(b, int) and b == 0):
                    dve.wait_ge(var_ps, b)
                dve.tensor_tensor(tile_sum[:], y[:, 0], y[:, 1], ALU.add).then_inc(y_sum_out, 1)

            def sum_squares(b):
                dve.wait_ge(sq_out, b + 1)
                dve.wait_ge(mean_ps, b + 1)
                dve.tensor_tensor(tile_sum[:], sq[:, 0], sq[:, 1], ALU.add).then_inc(sq_sum_out, 1)

            def subtract_mean(b):
                dve.wait_ge(mean_ps, b + 1)
                dve.wait_ge(y_out, 2 * b + 2)
                if not (isinstance(b, int) and b == 0):
                    dve.wait_ge(x1_out, b)
                mean = ST.rearrange("p (o t) -> p o t", o=1).to_broadcast([P, DK, T])
                dve.tensor_tensor(dev[:], y[:], mean, ALU.subtract).then_inc(dev_out, 1)

            def mask_scores(b):
                dve.wait_ge(s_ps, b + 1)
                if not (isinstance(b, int) and b == 0):
                    dve.wait_ge(o_ps, 2 * b)
                dve.tensor_tensor(s[:], S.rearrange("p (t n) -> p t n", n=P),
                                  dmask[:].rearrange("p (o n) -> p o n", o=1).to_broadcast([P, NT, P]),
                                  ALU.mult).then_inc(s_out, 1)

            def normalise(b):
                dve.wait_ge(sd_out, b + 1)
                dve.reciprocal(rs[:], rs[:]).then_inc(rs_out, 1)
                dve.wait_ge(rs_out, b + 1)
                if not (isinstance(b, int) and b == 0):
                    dve.wait_ge(stored, 16 * b)
                dve.tensor_tensor(x1[:], dev[:], rs[:].rearrange("p (o t) -> p o t", o=1).to_broadcast([P, DK, T]),
                                  ALU.mult).then_inc(x1_out, 1)

            def gated(b):
                dve.wait_ge(o_ps, 2 * b + 2)
                dve.wait_ge(g_out, b + 1)
                if not (isinstance(b, int) and b == 0):
                    dve.wait_ge(y_ps, 2 * b)
                if not (isinstance(b, int) and b == 0):
                    dve.wait_ge(sq_sum_out, b)
                dve.tensor_tensor(og[:], QO, gate[:], ALU.mult).then_inc(gate_used, 1)
                dve.wait_ge(gate_used, b + 1)
                dve.tensor_copy(og_hi[:], og[:]).then_inc(og_split, 1)
                dve.wait_ge(og_split, 2 * b + 1)
                dve.tensor_tensor(og_lo[:], og[:], f32(og_hi[:]), ALU.subtract).then_inc(og_split, 1)

            def ffn_scales():
                dve.wait_ge(f_mid_ps, 1)
                dve.tensor_copy(mid[:], VY[0:RANK, 1, 0:D]).then_inc(f_mid, 1)
                dve.wait_ge(f_ps, 1)
                dve.tensor_scalar(scale[:], G.rearrange("p a n -> p (a n)"), 1e-5, None, ALU.max).then_inc(f_scale, 1)
                dve.tensor_scalar(psc[:], S[:, 0:D], 1.0 / HID, 1e-5, ALU.mult, ALU.max).then_inc(f_scale, 1)
                dve.tensor_scalar(c["pscale"][:], S[:, D:D + 2 * DK:2], 1.0 / HID, 1e-5, ALU.mult,
                                  ALU.max).then_inc(f_scale, 1)
                for k, banks in enumerate((QO, VY)):
                    dve.wait_ge(f_low_ps, k + 1)
                    dve.tensor_scalar(c["wfc"][:, k, :], banks.rearrange("p a n -> p (a n)"), gt[:, 0:1], None,
                                      ALU.mult).then_inc(f_low, 1)

            def step(b, par, last):
                finish_y(b - 1, 1 - par)
                mask_scores(b)
                subtract_mean(b - 1)
                sum_squares(b - 1)
                if not last:
                    split_x(b + 1, 1 - par)
                gated(b)
                if isinstance(b, int) and b == 1:
                    ffn_scales()
                normalise(b - 1)

            mask_scores(0)
            split_x(1, 1)
            dve.wait_ge(f_abs, 1)
            dve.tensor_tensor(scale[:], wabs[:, 0], wabs[:, 1], ALU.add).then_inc(f_sum, 1)
            gated(0)
            dve.wait_ge(f_abs, 2)
            dve.tensor_reduce(psc[:], wabs[:].rearrange("p k (j n) -> p n (k j)", n=D), AX.X, ALU.add).then_inc(f_sum, 1)
            step(1, 1, False)
            dve.wait_ge(f_scale, 3)
            dve.wait_ge(f_low, 2)
            for k in range(DK):
                dve.scalar_tensor_tensor(out=above[:, k], in0=scale[:], scalar=0.5, in1=wfc[:, k],
                                         op0=ALU.mult, op1=ALU.is_lt).then_inc(f_above, 1)
                dve.wait_ge(f_above, k + 1)
                dve.scalar_tensor_tensor(out=wfc[:, k], in0=scale[:], scalar=-0.5, in1=wfc[:, k],
                                         op0=ALU.mult, op1=ALU.is_gt).then_inc(f_below, 1)
            with dve.Fori(2, B - 3, 2) as i:
                step(i, 0, False)
                step(i + 1, 1, False)
            scales = psc[:].rearrange("p (o n) -> p o n", o=1).to_broadcast([P, HK, D])
            dve.scalar_tensor_tensor(out=c["tern"][:], in0=scales, scalar=0.5, in1=wpr[:],
                                     op0=ALU.mult, op1=ALU.is_lt).then_inc(f_above, 1)
            dve.wait_ge(f_above, DK + 1)
            dve.scalar_tensor_tensor(out=wpr[:], in0=scales, scalar=-0.5, in1=wpr[:],
                                     op0=ALU.mult, op1=ALU.is_gt).then_inc(f_below, 1)
            step(B - 2, 0, False)
            step(B - 1, 1, True)
            finish_y(B - 1, 1)
            subtract_mean(B - 1)
            sum_squares(B - 1)
            normalise(B - 1)

        @block.tensor
        def _(pe):
            pe.wait_ge(setup, 2)
            pe.wait_ge(qk_in, 32)
            for m in range(DK):
                mm = full_matmul(pe, ps[:, 0, m * D:(m + 1) * D],
                                 [(raw["Wq"][:, k, m * P:(m + 1) * P], raw["Wk"][:, k, :]) for k in range(DK)])
            mm.then_inc(m_ps, 1)

            def project(bank, w, r_hi, r_lo, m):
                return split_matmul(pe, bank, [(w_hi[w][:, k, m * P:(m + 1) * P], w_lo[w][:, k, m * P:(m + 1) * P],
                                                r_hi[:, k], r_lo[:, k]) for k in range(DK)])

            def queries(b, par):
                if not (isinstance(b, int) and b == 0):
                    pe.wait_ge(gate_used, b)
                for m in range(DK):
                    project(QO[:, m], "M", x_hi[:, par], x_lo[:, par], m).then_inc(qm_ps, 1)

            def outputs(b):
                pe.wait_ge(og_split, 2 * b + 2)
                pe.wait_ge(v_out, 2 * b + 2)
                for m in range(DK):
                    project(VY[:, m], "WoT", og_hi, og_lo, m).then_inc(y_ps, 1)

            def gates(b, par):
                pe.wait_ge(x_split, 2 * b + 2)
                if not (isinstance(b, int) and b == 0):
                    pe.wait_ge(g_out, b)
                for m in range(DK):
                    mm = project(G[:, m], "WgT", x_hi[:, par], x_lo[:, par], m)
                mm.then_inc(g_ps, 1)

            def mean(b):
                pe.wait_ge(y_sum_out, b + 1)
                if not (isinstance(b, int) and b == 0):
                    pe.wait_ge(sd_out, b)
                pe.matmul(ST, c["mean_w"][:], tile_sum[:], start=True, stop=True).then_inc(mean_ps, 1)

            def variance(b):
                pe.wait_ge(sq_sum_out, b + 1)
                pe.matmul(ST, c["mean_w"][:], tile_sum[:], start=True, stop=True).then_inc(var_ps, 1)

            def values(b, par, tiles):
                if not (isinstance(b, int) and b == 0):
                    pe.wait_ge(y_out, 2 * b)
                vb = VY.rearrange("p a (t n) -> p (a t) n", n=D)
                for t in tiles:
                    mm = full_matmul(pe, vb[:, t], [(x[:, par, k, t * P:(t + 1) * P], wv[:, k, :]) for k in range(DK)])
                    if t % 2:
                        mm.then_inc(v_ps, 1)

            def scores(b, par):
                pe.wait_ge(qm_out, 2 * b + 2)
                if not (isinstance(b, int) and b == 0):
                    pe.wait_ge(s_out, b)
                for t in range(NT):
                    tok = slice(t * P, (t + 1) * P)
                    mm = full_matmul(pe, S[:, tok], [(x[:, par, k, tok], qm[:, k, tok]) for k in range(DK)])
                mm.then_inc(s_ps, 1)

            def attend(b):
                pe.wait_ge(s_out, b + 1)
                pe.wait_ge(v_out, 2 * b + 2)
                for m in range(DK):
                    for t in range(NT):
                        mm = pe.matmul(QO[:, m, t * P:(t + 1) * P], v[:, t, m * P:(m + 1) * P], s[:, t],
                                       start=True, stop=True)
                    mm.then_inc(o_ps, 1)

            pe.wait_ge(w_split, 2)
            gates(0, 0)
            pe.wait_ge(w_split, 4)
            queries(0, 0)
            scores(0, 0)
            pe.wait_ge(w_in, 32)
            values(0, 0, range(NT))
            attend(0)

            def step(b, par):
                gates(b, par)
                queries(b, par)
                outputs(b - 1)
                scores(b, par)
                values(b, par, (0,))
                mean(b - 1)
                values(b, par, range(1, NT))
                attend(b)
                variance(b - 1)

            pe.wait_ge(w_split, 6)
            step(1, 1)
            pe.wait_ge(v_out, 4)
            pe.matmul(VY[0:RANK, 1, 0:D], bT[:], vr[:], start=True, stop=True).then_inc(f_mid_ps, 1)
            pe.wait_ge(f_sum, 2)
            pe.wait_ge(g_out, 2)
            pe.wait_ge(s_out, 2)
            for n in range(2):
                pe.matmul(G[:, n], c["mean_w"][:], scale[:, n * T:(n + 1) * T], start=True, stop=True)
            pe.matmul(S[:, 0:D], c["ones_w"][:], psc[:], start=True, stop=True)
            for m in range(DK):
                mm = pe.matmul(S[:, D + 2 * m:D + 2 * m + 2], psc[:, m * P:(m + 1) * P], c["ones_w"][:, 0:2],
                               start=True, stop=True)
            mm.then_inc(f_ps, 1)
            pe.wait_ge(f_mid, 1)
            pe.wait_ge(gate_used, 2)
            for k, banks in enumerate((QO, VY)):
                for n in range(2):
                    mm = pe.matmul(banks[:, n], mid[:, k * P:(k + 1) * P], uT[:, n * T:(n + 1) * T],
                                   start=True, stop=True)
                mm.then_inc(f_low_ps, 1)
            pe.wait_ge(f_scale, 3)
            pe.wait_ge(f_low, 2)
            with pe.Fori(2, B - 1, 2) as i:
                step(i, 0)
                step(i + 1, 1)
            outputs(B - 1)
            mean(B - 1)
            variance(B - 1)


def cross_attention_phase(nc, ctx, sb, a, c, ps, x1_dram, y2_dram):
    def sem(name):
        return ctx.enter_context(nc.semaphore("b_" + name))

    raw_x, raw_c = c["raw"][:, 0], c["raw"][:, 1]
    x_res = sb(ctx, "x_res", [P, DK, T], F32)
    x_hi, x_lo = (sb(ctx, "bx_" + n, [P, DK, T], F32R) for n in ("hi", "lo"))
    c_hi, c_lo = (sb(ctx, "bc_" + n, [P, DK, T], F32R) for n in ("hi", "lo"))
    mask_u8 = sb(ctx, "mask_u8", [P, T], U8)
    mask = sb(ctx, "mask", [P, T], F32)
    q1, q2, k1, k2 = (sb(ctx, n, [P, 2, 2, T], F32R) for n in ("q1", "q2", "k1", "k2"))
    v = sb(ctx, "v_b", [P, NT, HD], F32)
    prob = sb(ctx, "prob", [P, 2, NT * T], F32)
    half = sb(ctx, "half", [P, 2 * T], F32)
    acc = sb(ctx, "acc", [P, 2, T], F32)
    log_den = sb(ctx, "log_den", [P, T], F32)
    recip0 = sb(ctx, "recip0", [P, T], F32)
    recip = sb(ctx, "recip", [P, T], F32)
    att = sb(ctx, "att", [P, PAIRS, T], F32)
    y2 = sb(ctx, "y2", [P, DK, T], F32)
    out_bias = sb(ctx, "out_bias", [P, DK], F32)
    junk = sb(ctx, "junk", [P, NT, T], BF16)
    mx = sb(ctx, "mx", [P, 2, 2, NT], F32)
    nm_hi, nm_lo = (sb(ctx, "nm_" + n, [P, 2, 2, NT], BF16) for n in ("hi", "lo"))

    x_in, ctx_in, mask_in, res_in = sem("x_in"), sem("ctx_in"), sem("mask_in"), sem("res_in")
    consts, mask_done = sem("consts"), sem("mask_done")
    x_rounded, x_split = sem("x_rounded"), sem("x_split")
    q_ps, q_hi_out, q_lo_out = sem("q_ps"), sem("q_hi_out"), sem("q_lo_out")
    k_ps, k_hi_out, k_lo_out, k_mask = sem("k_ps"), sem("k_hi_out"), sem("k_lo_out"), sem("k_mask")
    smax_ps, smax_out, nm_out = sem("smax_ps"), sem("smax_out"), sem("nm_out")
    row_ps, row_out = sem("row_ps"), sem("row_out")
    st_ps, exp_out, pv_ps, acc_out = sem("st_ps"), sem("exp_out"), sem("pv_ps"), sem("acc_out")
    den_ps, log_out, recip0_out = sem("den_ps"), sem("log_out"), sem("recip0_out")
    bias_ps, bias_out, next_in = sem("bias_ps"), sem("bias_out"), sem("next_in")
    newton, att_out = sem("newton"), sem("att_out")
    v_ps, v_out, o_ps, o_out, stored = sem("v_ps"), sem("v_out"), sem("o_ps"), sem("o_out"), sem("stored")

    PV = ps[:, 4, :]
    W0, W1, W2 = ps[:, 5, :], ps[:, 6, :], ps[:, 7, :]
    OWN = (slice(0, DH), slice(DH, P))
    OTHER = (OWN[1], OWN[0])
    MAX_ROW, MASK_ROW = (DH, 0), (DH + 32, 32)

    def per_pair(b, p):
        return b * PAIRS + p

    with nc.Block() as block:
        @block.sync
        def _(sp):
            def load(b):
                if not (isinstance(b, int) and b == 0):
                    sp.dma_start(raw_x, batch_cols(x1_dram, b)).then_inc(x_in, 16)
                    sp.dma_start(raw_c, batch_cols(a["cT"], b)).then_inc(ctx_in, 16)
                sp.dma_start(mask_u8[:], row_of(a["mask"], b).partition_broadcast(P)).then_inc(mask_in, 16)

            def store(b):
                sp.wait_ge(o_out, 2 * b + 2)
                sp.dma_start(batch_cols(y2_dram, b), y2[:]).then_inc(stored, 16)

            def load_residual(b):
                sp.dma_start(x_res[:], batch_cols(x1_dram, b)).then_inc(res_in, 16)

            load(0)
            load_residual(0)
            sp.wait_ge(x_split, 2)
            sp.wait_ge(mask_done, 1)
            load(1)
            with sp.Fori(1, B - 1) as b:
                store(b - 1)
                load_residual(b)
                sp.wait_ge(mask_done, b + 1)
                load(b + 1)
            store(B - 2)
            load_residual(B - 1)
            sp.wait_ge(stored, 16 * (B - 2))
            sp.dma_start(c["y2"][:], batch_cols(y2_dram, 0)).then_inc(next_in, 16)
            sp.wait_ge(next_in, 16)
            store(B - 1)
            sp.wait_ge(stored, 16 * B)

        @block.gpsimd
        def _(pool):
            def add_key_tiles(g, h, first):
                n = 4 * g + 2 * h
                pool.wait_ge(exp_out, n + 2)
                pool.tensor_tensor(half[:], prob[:, h, 0:2 * T], prob[:, h, 2 * T:4 * T],
                                   ALU.add).then_inc(acc_out, 1)
                pool.wait_ge(acc_out, n + 1)
                if not first:
                    pool.wait_ge(den_ps, g)
                pool.tensor_tensor(acc[:, h, :], half[:, 0:T], half[:, T:2 * T], ALU.add).then_inc(acc_out, 1)
                pool.wait_ge(acc_out, n + 2)

            def split_inputs(b):
                pool.wait_ge(x_rounded, 2 * b + 1)
                pool.tensor_tensor(x_lo[:], raw_x, f32(x_hi[:]), ALU.subtract).then_inc(x_split, 1)
                pool.wait_ge(x_rounded, 2 * b + 2)
                pool.tensor_tensor(c_lo[:], raw_c, f32(c_hi[:]), ALU.subtract).then_inc(x_split, 1)

            def batch(b, first, last):
                for p in range(PAIRS):
                    for h in range(2):
                        add_key_tiles(per_pair(b, p), h, first and p == 0)
                    if p == PAIRS - 3 and not last:
                        split_inputs(b + 1)

            pool.memset(f32(q2[:]), 0.0).then_inc(consts, 1)
            pool.memset(f32(k2[:]), 0.0).then_inc(consts, 1)
            pool.wait_ge(consts, 2)
            for h in range(2):
                pool.memset(f32(q2[MASK_ROW[h]:MASK_ROW[h] + 1, :, h, :]), 1.0).then_inc(consts, 1)
                pool.memset(f32(k2[MAX_ROW[h]:MAX_ROW[h] + 1, :, h, :]), 1.0).then_inc(consts, 1)
            batch(0, True, False)
            with pool.Fori(1, B - 1) as b:
                batch(b, False, False)
            batch(B - 1, False, True)

        @block.scalar
        def _(act):
            act.preload_act_table_set("natural_log_exp_and_others")

            def exps(g, h, s, first):
                act.wait_ge(st_ps, 4 * g + 2 * h + s + 1)
                if not first and s == 0:
                    act.wait_ge(pv_ps, g)
                    act.wait_ge(acc_out, 4 * g - 2 + 2 * h)
                act.activation(prob[:, h, s * 2 * T:(s + 1) * 2 * T], ps[:, 2 * s:2 * s + 2, :], ACT.Exp,
                               scale=SCALE).then_inc(exp_out, 1)

            def reciprocal_estimate(g, first):
                act.wait_ge(den_ps, g + 1)
                if not first:
                    act.wait_ge(newton, 2 * g)
                act.activation(log_den[:], W2, ACT.Ln).then_inc(log_out, 1)
                act.wait_ge(log_out, g + 1)
                act.activation(recip0[:], log_den[:], ACT.Exp, scale=-1.0).then_inc(recip0_out, 1)

            def queries_hi(g, p):
                par = p % 2
                act.wait_ge(q_ps, g + 1)
                for h in range(2):
                    act.activation(q1[OWN[h], par, h, :], W0[OWN[h], :], ACT.Identity,
                                   bias=c["bq"][OWN[h], p:p + 1]).then_inc(q_hi_out, 1)

            def queries_twice(g, p):
                par = p % 2
                act.wait_ge(q_hi_out, 4 * g + 2)
                for h in range(2):
                    act.activation(q1[OTHER[h], par, h, :], f32(q1[OWN[h], par, h, :]), ACT.Copy).then_inc(q_hi_out, 1)

            def keys_hi(g, p):
                par = p % 2
                act.wait_ge(k_ps, g + 1)
                for h in range(2):
                    act.activation(k1[OWN[h], par, h, :], W1[OWN[h], :], ACT.Identity,
                                   bias=c["bk"][OWN[h], p:p + 1]).then_inc(k_hi_out, 1)

            def keys_twice(g, p):
                par = p % 2
                act.wait_ge(k_hi_out, 4 * g + 2)
                for h in range(2):
                    act.activation(k2[OWN[h], par, h, :], f32(k1[OWN[h], par, h, :]), ACT.Copy).then_inc(k_hi_out, 1)

            def values_out(b, first):
                if not first:
                    act.wait_ge(pv_ps, PAIRS * b)
                for i in range(2 * NT):
                    kt, n = divmod(i, 2)
                    act.wait_ge(v_ps, 8 * b + i + 1)
                    act.activation(v[:, kt, n * T:(n + 1) * T], (W0, W1)[i % 2], ACT.Copy).then_inc(v_out, 1)

            def round_inputs(b, first):
                if not first:
                    act.wait_ge(x_in, 16 * b)
                    act.wait_ge(k_ps, PAIRS * b)
                act.activation(x_hi[:], raw_x, ACT.Copy).then_inc(x_rounded, 1)
                if not first:
                    act.wait_ge(ctx_in, 16 * b)
                act.activation(c_hi[:], raw_c, ACT.Copy).then_inc(x_rounded, 1)

            def mask_rows(b, par):
                act.wait_ge(mask_done, b + 1)
                for h in range(2):
                    r = slice(MASK_ROW[h], MASK_ROW[h] + 1)
                    act.activation(k2[r, par, h, :], mask[r, :], ACT.Copy).then_inc(k_mask, 1)

            def max_row(g, p, h):
                r = slice(MAX_ROW[h], MAX_ROW[h] + 1)
                act.wait_ge(row_ps, 2 * g + h + 1)
                act.activation(q2[r, p % 2, h, :], W2[r, :], ACT.Copy).then_inc(row_out, 1)

            def project_pair(g, p):
                queries_hi(g, p)
                keys_hi(g, p)
                queries_twice(g, p)
                keys_twice(g, p)

            def batch(b, first, last):
                for p in range(PAIRS):
                    g = per_pair(b, p)
                    head = first and p == 0
                    nxt = not (last and p == PAIRS - 1)
                    nxt2 = not (last and p >= PAIRS - 2)
                    exps(g, 0, 0, head)
                    max_row(g, p, 1)
                    exps(g, 0, 1, head)
                    exps(g, 1, 0, head)
                    if not head:
                        reciprocal_estimate(g - 1, first and p == 1)
                    exps(g, 1, 1, head)
                    if p == 0:
                        values_out(b, first)
                        mask_rows(b, 1)
                    if nxt2:
                        project_pair(g + 2, (p + 2) % PAIRS)
                    if nxt:
                        max_row(g + 1, (p + 1) % PAIRS, 0)
                    if p == PAIRS - 3 and not last:
                        round_inputs(b + 1, False)
                    if p == PAIRS - 1 and not last:
                        mask_rows(b + 1, 0)

            round_inputs(0, True)
            act.wait_ge(consts, 6)
            project_pair(0, 0)
            project_pair(1, 1)
            mask_rows(0, 0)
            max_row(0, 0, 0)
            batch(0, True, False)
            with act.Fori(1, B - 1) as b:
                batch(b, False, False)
            batch(B - 1, False, True)
            reciprocal_estimate(PAIRS * B - 1, False)

        @block.vector
        def _(dve):
            scores_number = dve.alloc_register("scores_number")

            def first_split():
                dve.wait_ge(x_rounded, 1)
                dve.tensor_tensor(x_lo[:], raw_x, f32(x_hi[:]), ALU.subtract).then_inc(x_split, 1)
                dve.wait_ge(x_rounded, 2)
                dve.tensor_tensor(c_lo[:], raw_c, f32(c_hi[:]), ALU.subtract).then_inc(x_split, 1)

            def prepare_mask(b, first):
                dve.wait_ge(mask_in, 16 * b + 16)
                if not first:
                    dve.wait_ge(k_mask, 4 * b)
                dve.tensor_scalar(mask[:], mask_u8[:], 1.0, -MASKED, ALU.subtract, ALU.mult).then_inc(mask_done, 1)
                dve.wait_ge(mask_done, b + 1)

            def queries_lo(g, p):
                par = p % 2
                for h in range(2):
                    dve.wait_ge(q_hi_out, 4 * g + 2)
                    dve.scalar_tensor_tensor(out=q2[OWN[h], par, h, :], in0=W0[OWN[h], :],
                                             scalar=c["bq"][OWN[h], p:p + 1], in1=f32(q1[OWN[h], par, h, :]),
                                             op0=ALU.add, op1=ALU.subtract).then_inc(q_lo_out, 1)

            def keys_lo(g, p):
                par = p % 2
                for h in range(2):
                    dve.wait_ge(k_hi_out, 4 * g + 2)
                    dve.scalar_tensor_tensor(out=k1[OTHER[h], par, h, :], in0=W1[OWN[h], :],
                                             scalar=c["bk"][OWN[h], p:p + 1], in1=f32(k1[OWN[h], par, h, :]),
                                             op0=ALU.add, op1=ALU.subtract).then_inc(k_lo_out, 1)

            def maxima(b, g, p, h, tiles):
                for t in tiles:
                    if isinstance(b, int):
                        dve.wait_ge(smax_ps, 8 * g + NT * h + t + 1)
                    else:
                        dve.wait_ge(smax_ps, scores_number)
                        dve.reg_add(scores_number, scores_number, 1)
                    dve.tensor_tensor_reduce(junk[:, t, :], (W0, W1)[t % 2], mask[:], 1.0, LOWEST, ALU.add, ALU.max,
                                             mx[:, p % 2, h, t:t + 1]).then_inc(smax_out, 1)

            def negate_maxima(g, p, h):
                par = p % 2
                dve.wait_ge(smax_out, 8 * g + NT * (h + 1))
                dve.tensor_scalar(nm_hi[:, par, h, :], mx[:, par, h, :], -1.0, None, ALU.mult).then_inc(nm_out, 1)
                dve.wait_ge(nm_out, 4 * g + 2 * h + 1)
                dve.scalar_tensor_tensor(out=nm_lo[:, par, h, :], in0=mx[:, par, h, :], scalar=-1.0,
                                         in1=nm_hi[:, par, h, :], op0=ALU.mult,
                                         op1=ALU.subtract).then_inc(nm_out, 1)

            def normalise(b, g, p, first):
                dve.wait_ge(recip0_out, g + 1)
                dve.tensor_tensor(log_den[:], W2, recip0[:], ALU.mult).then_inc(newton, 1)
                dve.wait_ge(newton, 2 * g + 1)
                dve.scalar_tensor_tensor(out=recip[:], in0=log_den[:], scalar=2.0, in1=recip0[:],
                                         op0=ALU.subtract, op1=ALU.mult).then_inc(newton, 1)
                dve.wait_ge(newton, 2 * g + 2)
                dve.wait_ge(pv_ps, g + 1)
                if p == 0 and not first:
                    dve.wait_ge(o_ps, 2 * b)
                dve.scalar_tensor_tensor(out=att[:, p, :], in0=PV, scalar=-1.0, in1=recip[:], op0=ALU.mult,
                                         op1=ALU.mult).then_inc(att_out, 1)

            def projected_out(b, first):
                if first:
                    dve.wait_ge(bias_out, 1)
                dve.wait_ge(res_in, 16 * b + 16)
                if not first:
                    dve.wait_ge(stored, 16 * b)
                for m in range(DK):
                    dve.wait_ge(o_ps, 2 * b + m + 1)
                    dve.scalar_tensor_tensor(out=y2[:, m], in0=(W0, W1)[m], scalar=out_bias[:, m:m + 1],
                                             in1=x_res[:, m], op0=ALU.add, op1=ALU.add).then_inc(o_out, 1)

            def batch(b, first, last):
                for p in range(PAIRS):
                    g = per_pair(b, p)
                    nxt = not (last and p == PAIRS - 1)
                    nxt2 = not (last and p >= PAIRS - 2)
                    pn, bn = (p + 1, b) if p < PAIRS - 1 else (0, b + 1)
                    if p == PAIRS - 1 and not last:
                        prepare_mask(b + 1, False)
                    if nxt:
                        maxima(bn, g + 1, pn, 0, range(NT))
                        negate_maxima(g + 1, pn, 0)
                    if p > 0:
                        normalise(b, g - 1, p - 1, first)
                    elif not first:
                        normalise(b - 1, g - 1, PAIRS - 1, False)
                        projected_out(b - 1, isinstance(b, int) and b == 1)
                    if nxt2:
                        queries_lo(g + 2, (p + 2) % PAIRS)
                        keys_lo(g + 2, (p + 2) % PAIRS)
                    if nxt:
                        maxima(bn, g + 1, pn, 1, range(NT))
                        negate_maxima(g + 1, pn, 1)

            first_split()
            prepare_mask(0, True)
            dve.wait_ge(consts, 6)
            dve.wait_ge(bias_ps, 1)
            dve.tensor_tensor(out_bias[:], ps[:, 0:DK, 0:1].rearrange("p m o -> p (m o)"), c["bo"][:],
                              ALU.add).then_inc(bias_out, 1)
            for g in range(2):
                queries_lo(g, g)
                keys_lo(g, g)
            for h in range(2):
                maxima(0, 0, 0, h, range(NT))
                negate_maxima(0, 0, h)
            batch(0, True, False)
            batch(1, False, False)
            dve.reg_mov(scores_number, 8 * (per_pair(2, 0) + 1) + 1)
            with dve.Fori(2, B - 1) as b:
                batch(b, False, False)
            batch(B - 1, False, True)
            normalise(B - 1, PAIRS * B - 1, PAIRS - 1, False)
            projected_out(B - 1, False)

        @block.tensor
        def _(pe):
            def heads(bank, w, r_hi, r_lo, p):
                cols = slice(p * P, (p + 1) * P)
                return split_matmul(pe, bank, [(c[w + "_hi"][:, k, cols], c[w + "_lo"][:, k, cols],
                                                r_hi[:, k], r_lo[:, k]) for k in range(DK)])

            def queries(b, g, p):
                if p == 0:
                    pe.wait_ge(x_split, 2 * b + 2)
                heads(W0, "wq", x_hi, x_lo, p).then_inc(q_ps, 1)

            def keys(g, p):
                heads(W1, "wk", c_hi, c_lo, p).then_inc(k_ps, 1)

            def max_scores(g, p, h, t):
                par = p % 2
                pe.matmul((W0, W1)[t % 2], q1[:, par, h, t * P:(t + 1) * P], k1[:, par, h, :],
                          start=True, stop=True).then_inc(smax_ps, 1)

            def maxima_read(g, n):
                pe.wait_ge(smax_out, 8 * g + n)

            def operands_ready(g):
                pe.wait_ge(q_hi_out, 4 * g + 4)
                pe.wait_ge(k_lo_out, 2 * g + 2)

            def max_to_row(g, p, h):
                par, r = p % 2, slice(MAX_ROW[h], MAX_ROW[h] + 1)
                pe.wait_ge(nm_out, 4 * g + 2 * h + 2)
                for t in range(NT):
                    o = W2[r, t * P:(t + 1) * P]
                    pe.matmul(o, nm_hi[:, par, h, t:t + 1], c["ident"][:], start=True, stop=False)
                    mm = pe.matmul(o, nm_lo[:, par, h, t:t + 1], c["ident"][:], start=False, stop=True)
                mm.then_inc(row_ps, 1)

            def tile_scores(p, h, kt):
                par = p % 2
                cols = slice(kt * P, (kt + 1) * P)
                pe.matmul(ps[:, kt, :], k1[:, par, h, cols], q1[:, par, h, :], start=True, stop=False)
                return pe.matmul(ps[:, kt, :], k2[:, par, h, cols], q2[:, par, h, :], start=False, stop=True)

            def banks_free(g, h, s, first):
                if not (first and h == 0):
                    pe.wait_ge(exp_out, 4 * g + 2 * h + s - 1)

            def scores(g, p, h, s, first):
                banks_free(g, h, s, first)
                tile_scores(p, h, 2 * s)
                tile_scores(p, h, 2 * s + 1).then_inc(st_ps, 1)

            def weighted_values(p, kt):
                for h in range(2):
                    cols = slice((2 * p + h) * DH, (2 * p + h + 1) * DH)
                    mm = pe.matmul(PV[OWN[h], :], v[:, kt, cols], prob[:, h, kt * T:(kt + 1) * T],
                                   start=(kt == 0), stop=(kt == NT - 1))
                return mm

            def sums(g):
                pe.wait_ge(acc_out, 4 * g + 4)
                for h in range(2):
                    mm = pe.matmul(W2[OWN[h], :], c["ones_w"][:, 0:DH], acc[:, h, :], start=True, stop=True)
                mm.then_inc(den_ps, 1)

            def values(b):
                for i in range(2 * NT):
                    kt, n = divmod(i, 2)
                    if i < 2:
                        maxima_read(PAIRS * b + 1, 3 + i)
                    else:
                        pe.wait_ge(v_out, 8 * b + i - 1)
                    split_matmul(pe, (W0, W1)[i % 2], [
                        (c_hi[:, k, kt * P:(kt + 1) * P], c_lo[:, k, kt * P:(kt + 1) * P],
                         c["wv_hi"][:, k, n * T:(n + 1) * T], c["wv_lo"][:, k, n * T:(n + 1) * T])
                        for k in range(DK)]).then_inc(v_ps, 1)

            def project(b, tail):
                pe.wait_ge(att_out, PAIRS * b + PAIRS)
                for m in range(DK):
                    if not tail:
                        pe.wait_ge(v_out, 8 * b + 15 + m)
                    full_matmul(pe, (W0, W1)[m], [(c["wo"][:, p, m * P:(m + 1) * P], att[:, p, :])
                                                  for p in range(PAIRS)]).then_inc(o_ps, 1)

            def batch(b, first, last):
                for p in range(PAIRS):
                    g = per_pair(b, p)
                    nxt = not (last and p == PAIRS - 1)
                    nxt2 = not (last and p >= PAIRS - 2)
                    pn = (p + 1) % PAIRS
                    head = first and p == 0
                    pe.wait_ge(row_out, 2 * g + 1)
                    pe.wait_ge(k_hi_out, 4 * g + 4)
                    pe.wait_ge(q_lo_out, 2 * g + 2)
                    if p < 2:
                        pe.wait_ge(k_mask, 4 * b + 2 * p + 2)
                    scores(g, p, 0, 0, head)
                    if nxt:
                        operands_ready(g + 1)
                        maxima_read(g, 7)
                        max_scores(g + 1, pn, 0, 0)
                    banks_free(g, 0, 1, head)
                    tile_scores(p, 0, 2)
                    max_to_row(g, p, 1)
                    tile_scores(p, 0, 3).then_inc(st_ps, 1)
                    if nxt:
                        maxima_read(g, 8)
                        max_scores(g + 1, pn, 0, 1)
                        maxima_read(g + 1, 1)
                        max_scores(g + 1, pn, 0, 2)
                    pe.wait_ge(row_out, 2 * g + 2)
                    scores(g, p, 1, 0, head)
                    if not head:
                        sums(g - 1)
                    if nxt:
                        maxima_read(g + 1, 2)
                        max_scores(g + 1, pn, 0, 3)
                    scores(g, p, 1, 1, head)
                    if p == 0:
                        values(b)
                        if not first:
                            project(b - 1, False)
                    if nxt2:
                        if p == 0:
                            pe.wait_ge(v_out, 8 * b + 8)
                            if not first:
                                pe.wait_ge(o_out, 2 * b - 1)
                        else:
                            maxima_read(g + 1, 3)
                        queries(b if p < PAIRS - 2 else b + 1, g + 2, (p + 2) % PAIRS)
                        if p > 0:
                            maxima_read(g + 1, 4)
                        elif not first:
                            pe.wait_ge(o_out, 2 * b)
                        keys(g + 2, (p + 2) % PAIRS)
                    pe.wait_ge(exp_out, 4 * g + 3)
                    if not head:
                        pe.wait_ge(att_out, g)
                    weighted_values(p, 0)
                    if nxt:
                        if not head:
                            pe.wait_ge(newton, 2 * g - 1)
                        max_to_row(g + 1, pn, 0)
                    weighted_values(p, 1)
                    if nxt:
                        if nxt2:
                            pe.wait_ge(q_lo_out, 2 * g + 6)
                        max_scores(g + 1, pn, 1, 0)
                    pe.wait_ge(exp_out, 4 * g + 4)
                    weighted_values(p, 2)
                    if nxt:
                        if nxt2:
                            pe.wait_ge(k_lo_out, 2 * g + 6)
                        else:
                            maxima_read(g + 1, 4)
                        max_scores(g + 1, pn, 1, 1)
                    if nxt:
                        maxima_read(g + 1, NT + 1)
                        max_scores(g + 1, pn, 1, 2)
                    weighted_values(p, 3).then_inc(pv_ps, 1)
                    if nxt:
                        maxima_read(g + 1, NT + 2)
                        max_scores(g + 1, pn, 1, 3)

            for m in range(DK):
                mm = full_matmul(pe, ps[:, m, 0:2], [(c["wo"][:, p, m * P:(m + 1) * P], c["bv"][:, :, p])
                                                     for p in range(PAIRS)])
            mm.then_inc(bias_ps, 1)
            for g in range(2):
                if g:
                    pe.wait_ge(q_lo_out, 2)
                    pe.wait_ge(k_lo_out, 2)
                queries(0, g, g)
                keys(g, g)
            pe.wait_ge(bias_out, 1)
            pe.wait_ge(q_hi_out, 4)
            pe.wait_ge(q_lo_out, 4)
            pe.wait_ge(k_lo_out, 4)
            for h in range(2):
                for t in range(NT):
                    if h or t > 1:
                        maxima_read(0, NT * h + t - 1)
                    max_scores(0, 0, h, t)
            max_to_row(0, 0, 0)
            batch(0, True, False)
            with pe.Fori(1, B - 1) as b:
                batch(b, False, False)
            batch(B - 1, False, True)
            sums(PAIRS * B - 1)
            project(B - 1, True)


def ffn_phase(nc, ctx, sb, a, c, ps, y2_dram, out):
    def sem(name):
        return ctx.enter_context(nc.semaphore("c_" + name))

    w_hi = sb(ctx, "wfc_hi", [P, DK, HID], F32R)
    w_lo = sb(ctx, "wfc_lo", [P, DK, HID], F32R)
    tern = sb(ctx, "tern_r", [P, HK, D], F32R)
    pscale = c["pscale"]

    def sems(*names):
        return [sem(n) for n in names]

    y2 = c["y2"]
    dev2, sq2 = (sb(ctx, n, [P, DK, T], F32) for n in ("dev2", "sq2"))
    est2, inv2, rs2 = (sb(ctx, n + "2", [P, T], F32) for n in ("est", "inv", "rs"))
    y2_sum, sq2_sum, y3_sum, sq3_sum = (sb(ctx, n, [P, T], F32) for n in ("y2_sum", "sq2_sum", "y3_sum", "sq3_sum"))
    x2 = sb(ctx, "x2", [P, 2, DK, T], F32)
    x_hi, x_lo = (sb(ctx, "cx_" + n, [P, 2, DK, T], F32R) for n in ("hi", "lo"))
    RH = 4
    r = sb(ctx, "relu", [P, RH, T], F32)
    rr = sb(ctx, "relu2", [P, RH, T], F32)
    h_hi, h_lo = (sb(ctx, "h_" + n, [P, HK, T], F32R) for n in ("hi", "lo"))
    y3 = sb(ctx, "y3", [P, DK, T], F32)
    dev3, sq3, x3 = (sb(ctx, n, [P, DK, T], F32) for n in ("dev3", "sq3", "x3"))
    est3, inv3, rs3 = (sb(ctx, n + "3", [P, T], F32) for n in ("est", "inv", "rs"))

    y_in, stored, w_round, w_split, tern_out = sems("y_in", "stored", "w_round", "w_split", "tern_out")
    mean2_ps, dev2_out, sq2_out, var2_ps, est2_out, rs2_out, x2_out = sems(
        "mean2_ps", "dev2_out", "sq2_out", "var2_ps", "est2_out", "rs2_out", "x2_out")
    mean3_ps, dev3_out, sq3_out, var3_ps, est3_out, rs3_out, x3_out = sems(
        "mean3_ps", "dev3_out", "sq3_out", "var3_ps", "est3_out", "rs3_out", "x3_out")
    y2_sum_out, sq2_sum_out, y3_sum_out, sq3_sum_out = sems(
        "y2_sum_out", "sq2_sum_out", "y3_sum_out", "sq3_sum_out")
    x_split, h_ps, relu_out, hi_out, rr_out, lo_out, p_ps, y3_out = sems(
        "x_split", "h_ps", "relu_out", "hi_out", "rr_out", "lo_out", "p_ps", "y3_out")

    HIDDEN = [ps[:, i, :] for i in (0, 1, 2, 7)]
    STAT3, STAT2 = ps[:, 3, :], ps[:, 4, :]
    OUT = ps[:, 5:7, :]

    def both(tile):
        return tile[:].rearrange("p (o t) -> p o t", o=1).to_broadcast([P, DK, T])

    with nc.Block() as block:
        @block.sync
        def _(sp):
            def load(b):
                sp.dma_start(y2[:], batch_cols(y2_dram, b)).then_inc(y_in, 16)

            def store(b):
                sp.wait_ge(x3_out, b + 1)
                sp.dma_start(batch_cols(out, b), x3[:]).then_inc(stored, 16)

            sp.wait_ge(dev2_out, 1)
            load(1)
            sp.wait_ge(dev2_out, 2)
            load(2)
            with sp.Fori(3, B) as b:
                sp.wait_ge(dev2_out, b)
                load(b)
                store(b - 3)
            for b in (B - 3, B - 2, B - 1):
                store(b)
            sp.wait_ge(stored, 16 * B)

        @block.gpsimd
        def _(pool):
            pool.tensor_copy(tern[:], c["tern"][:]).then_inc(tern_out, 1)

            def batch(b, first):
                for i in range(HK):
                    pool.wait_ge(relu_out, HK * b + i + 1)
                    if not (first and i < RH):
                        pool.wait_ge(lo_out, HK * b + i - RH + 1)
                    n = i % RH
                    pool.tensor_tensor(rr[:, n, :], r[:, n, :], r[:, n, :], ALU.mult).then_inc(rr_out, 1)

            batch(0, True)
            with pool.Fori(1, B) as b:
                batch(b, False)

        @block.scalar
        def _(act):
            def norm_square(dev, sq, dev_out, sq_out, sum_out, b, first):
                act.wait_ge(dev_out, b + 1)
                if not first:
                    act.wait_ge(sum_out, b)
                act.activation(sq[:], dev[:], ACT.Square).then_inc(sq_out, 1)

            def norm_root(stat, norm, sems, b, first):
                est, inv = norm
                var_ps, est_out, rs_out = sems
                act.wait_ge(var_ps, b + 1)
                if not first:
                    act.wait_ge(rs_out, 2 * b)
                act.activation(inv[:], stat, ACT.Ln, bias=c["eps"][:, 0:1]).then_inc(est_out, 1)
                act.wait_ge(est_out, 3 * b + 1)
                act.activation(est[:], inv[:], ACT.Exp, scale=-0.5).then_inc(est_out, 1)
                act.wait_ge(est_out, 3 * b + 2)
                act.activation(inv[:], est[:], ACT.Square).then_inc(est_out, 1)

            def norm2_root(b, first):
                norm_root(STAT2, (est2, inv2), (var2_ps, est2_out, rs2_out), b, first)

            def norm3_root(b, first):
                norm_root(STAT3, (est3, inv3), (var3_ps, est3_out, rs3_out), b, first)

            def hidden(b, i, first):
                n = HK * b + i
                act.wait_ge(h_ps, n + 1)
                if not (first and i < RH):
                    act.wait_ge(rr_out, n - RH + 1)
                act.activation(r[:, i % RH, :], HIDDEN[i % RH], ACT.Relu).then_inc(relu_out, 1)
                act.wait_ge(relu_out, n + 1)
                if i == 0 and not first:
                    act.wait_ge(p_ps, 2 * b)
                act.activation(h_hi[:, i, :], r[:, i % RH, :], ACT.Square).then_inc(hi_out, 1)

            def batch(b, first, second, last):
                for i in (0, 1, 2):
                    hidden(b, i, first)
                if not last:
                    norm_square(dev2, sq2, dev2_out, sq2_out, sq2_sum_out, b + 1, False)
                for i in (3, 4):
                    hidden(b, i, first)
                for i in (5, 6, 7):
                    hidden(b, i, first)
                if not last:
                    norm2_root(b + 1, False)
                if not first:
                    norm3_root(b - 1, second)

            act.preload_act_table_set("natural_log_exp_and_others")
            for k in range(DK):
                act.activation(w_hi[:, k], c["wfc"][:, k], ACT.Copy).then_inc(w_round, 1)
            norm_square(dev2, sq2, dev2_out, sq2_out, sq2_sum_out, 0, True)
            norm2_root(0, True)
            batch(0, True, False, False)
            batch(1, False, True, False)
            with act.Fori(2, B - 1) as b:
                batch(b, False, False, False)
            batch(B - 1, False, False, True)
            norm3_root(B - 1, False)

        @block.vector
        def _(dve):
            def add_tiles(total, tiles, total_out, read, b, first):
                if not first:
                    dve.wait_ge(read, b)
                dve.tensor_tensor(total[:], tiles[:, 0], tiles[:, 1], ALU.add).then_inc(total_out, 1)

            def sum_y2(b, first):
                if not first:
                    dve.wait_ge(y_in, 16 * b)
                add_tiles(y2_sum, y2, y2_sum_out, mean2_ps, b, first)

            def sum_y3(b, first):
                dve.wait_ge(y3_out, 2 * b + 2)
                add_tiles(y3_sum, y3, y3_sum_out, mean3_ps, b, first)

            def sum_squares2(b, first):
                dve.wait_ge(sq2_out, b + 1)
                add_tiles(sq2_sum, sq2, sq2_sum_out, var2_ps, b, first)

            def sum_squares3(b, first):
                dve.wait_ge(dev3_out, b + 1)
                dve.tensor_tensor(sq3[:], dev3[:], dev3[:], ALU.mult).then_inc(sq3_out, 1)
                dve.wait_ge(sq3_out, b + 1)
                add_tiles(sq3_sum, sq3, sq3_sum_out, var3_ps, b, first)

            def deviate2(b, first):
                dve.wait_ge(mean2_ps, b + 1)
                if not first:
                    dve.wait_ge(x2_out, b)
                dve.tensor_tensor(dev2[:], y2[:], both(STAT2_T), ALU.subtract).then_inc(dev2_out, 1)

            def inverse_root(norm, est_out, rs_out, b):
                stat, est, inv, rs = norm
                dve.wait_ge(est_out, 3 * b + 3)
                dve.scalar_tensor_tensor(out=rs[:], in0=stat, scalar=c["eps"][:, 0:1], in1=inv[:], op0=ALU.add,
                                         op1=ALU.mult).then_inc(rs_out, 1)
                dve.wait_ge(rs_out, 2 * b + 1)
                dve.scalar_tensor_tensor(out=rs[:], in0=rs[:], scalar=-3.0, in1=est[:], op0=ALU.add,
                                         op1=ALU.mult).then_inc(rs_out, 1)
                dve.wait_ge(rs_out, 2 * b + 2)

            def normalise2(b, par, first):
                inverse_root((STAT2, est2, inv2, rs2), est2_out, rs2_out, b)
                if not (isinstance(b, int) and b < 2):
                    dve.wait_ge(y3_out, 2 * b - 2)
                dve.scalar_tensor_tensor(out=x2[:, par], in0=dev2[:], scalar=-0.5, in1=both(rs2), op0=ALU.mult,
                                         op1=ALU.mult).then_inc(x2_out, 1)
                dve.wait_ge(x2_out, b + 1)
                if not (isinstance(b, int) and b < 2):
                    dve.wait_ge(h_ps, HK * b - HK)
                dve.tensor_copy(x_hi[:, par], x2[:, par]).then_inc(x_split, 1)
                dve.wait_ge(x_split, 2 * b + 1)
                dve.tensor_tensor(x_lo[:, par], x2[:, par], f32(x_hi[:, par]), ALU.subtract).then_inc(x_split, 1)

            def hidden_lo(b, i):
                n = HK * b + i
                dve.wait_ge(hi_out, n + 1)
                dve.wait_ge(rr_out, n + 1)
                dve.tensor_tensor(h_lo[:, i, :], rr[:, i % RH, :], f32(h_hi[:, i, :]), ALU.subtract).then_inc(lo_out, 1)

            def residual(b, par, first):
                for m in range(DK):
                    dve.wait_ge(p_ps, 2 * b + m + 1)
                    if m == 0 and not first:
                        dve.wait_ge(dev3_out, b)
                    dve.scalar_tensor_tensor(out=y3[:, m], in0=OUT[:, m], scalar=pscale[:, m:m + 1],
                                             in1=x2[:, par, m], op0=ALU.mult, op1=ALU.add).then_inc(y3_out, 1)

            def deviate3(b, first):
                dve.wait_ge(mean3_ps, b + 1)
                if not first:
                    dve.wait_ge(x3_out, b)
                dve.tensor_tensor(dev3[:], y3[:], both(STAT3_T), ALU.subtract).then_inc(dev3_out, 1)

            def normalise3(b, first):
                inverse_root((STAT3, est3, inv3, rs3), est3_out, rs3_out, b)
                if not first:
                    dve.wait_ge(stored, 16 * b)
                dve.scalar_tensor_tensor(out=x3[:], in0=dev3[:], scalar=-0.5, in1=both(rs3), op0=ALU.mult,
                                         op1=ALU.mult).then_inc(x3_out, 1)

            STAT2_T, STAT3_T = ps[:, 4, :], ps[:, 3, :]

            def batch(b, par, first, second, last, next_last=False):
                if not first:
                    residual(b - 1, 1 - par, second)
                    sum_y3(b - 1, second)
                hidden_lo(b, 0)
                hidden_lo(b, 1)
                if not last:
                    deviate2(b + 1, False)
                hidden_lo(b, 2)
                if not last:
                    sum_squares2(b + 1, False)
                hidden_lo(b, 3)
                if not first:
                    deviate3(b - 1, second)
                for i in (4, 5):
                    hidden_lo(b, i)
                if not first:
                    sum_squares3(b - 1, second)
                for i in (6, 7):
                    hidden_lo(b, i)
                if not last:
                    normalise2(b + 1, 1 - par, False)
                if not (last or next_last):
                    sum_y2(b + 2, False)
                if not first:
                    normalise3(b - 1, second)

            def weights_lo(k):
                dve.wait_ge(w_round, k + 1)
                dve.tensor_tensor(w_lo[:, k], c["wfc"][:, k], f32(w_hi[:, k]), ALU.subtract).then_inc(w_split, 1)

            sum_y2(0, True)
            deviate2(0, True)
            weights_lo(0)
            sum_squares2(0, True)
            weights_lo(1)
            normalise2(0, 0, True)
            sum_y2(1, False)
            batch(0, 0, True, False, False)
            batch(1, 1, False, True, False)
            with dve.Fori(2, B - 3, 2) as i:
                batch(i, 0, False, False, False)
                batch(i + 1, 1, False, False, False)
            batch(B - 2, 0, False, False, False, next_last=True)
            batch(B - 1, 1, False, False, True)
            residual(B - 1, 1, False)
            sum_y3(B - 1, False)
            deviate3(B - 1, False)
            sum_squares3(B - 1, False)
            normalise3(B - 1, False)

        @block.tensor
        def _(pe):
            def mean2(b, first):
                pe.wait_ge(y2_sum_out, b + 1)
                if not first:
                    pe.wait_ge(rs2_out, 2 * b)
                pe.matmul(STAT2, c["mean_w"][:], y2_sum[:], start=True, stop=True).then_inc(mean2_ps, 1)

            def var2(b):
                pe.wait_ge(sq2_sum_out, b + 1)
                pe.matmul(STAT2, c["mean_w"][:], sq2_sum[:], start=True, stop=True).then_inc(var2_ps, 1)

            def mean3(b, first):
                pe.wait_ge(y3_sum_out, b + 1)
                if not first:
                    pe.wait_ge(rs3_out, 2 * b)
                pe.matmul(STAT3, c["mean_w"][:], y3_sum[:], start=True, stop=True).then_inc(mean3_ps, 1)

            def var3(b):
                pe.wait_ge(sq3_sum_out, b + 1)
                pe.matmul(STAT3, c["mean_w"][:], sq3_sum[:], start=True, stop=True).then_inc(var3_ps, 1)

            def hidden(b, par, i, first):
                if i == 0:
                    pe.wait_ge(x_split, 2 * b + 2)
                if not (first and i < RH):
                    pe.wait_ge(relu_out, HK * b + i - RH + 1)
                cols = slice(i * P, (i + 1) * P)
                split_matmul(pe, HIDDEN[i % RH], [(w_hi[:, k, cols], w_lo[:, k, cols], x_hi[:, par, k],
                                                   x_lo[:, par, k]) for k in range(DK)]).then_inc(h_ps, 1)

            def project(b, m, tiles):
                for k in tiles:
                    pe.wait_ge(lo_out, HK * b + k + 1)
                    w = tern[:, k, m * P:(m + 1) * P]
                    pe.matmul(OUT[:, m], w, h_hi[:, k, :], start=(k == 0), stop=False)
                    mm = pe.matmul(OUT[:, m], w, h_lo[:, k, :], start=False, stop=(k == HK - 1))
                if tiles[-1] == HK - 1:
                    mm.then_inc(p_ps, 1)

            def batch(b, par, first, second, last):
                for i in (0, 1):
                    hidden(b, par, i, first)
                if not last:
                    mean2(b + 1, False)
                for i in (2, 3):
                    hidden(b, par, i, first)
                if not first:
                    mean3(b - 1, second)
                for i in (4, 5):
                    hidden(b, par, i, first)
                if not last:
                    var2(b + 1)
                for i in (6, 7):
                    hidden(b, par, i, first)
                if not first:
                    pe.wait_ge(y3_out, 2 * b)
                project(b, 0, range(0, 6))
                if not first:
                    var3(b - 1)
                project(b, 0, (6, 7))
                project(b, 1, range(HK))

            mean2(0, True)
            var2(0)
            pe.wait_ge(w_split, DK)
            pe.wait_ge(tern_out, 1)
            batch(0, 0, True, False, False)
            batch(1, 1, False, True, False)
            with pe.Fori(2, B - 3, 2) as i:
                batch(i, 0, False, False, False)
                batch(i + 1, 1, False, False, False)
            batch(B - 2, 0, False, False, False)
            batch(B - 1, 1, False, False, True)
            mean3(B - 1, False)
            var3(B - 1)


def kernel(**inputs):
    import numpy as np
    import concourse.bacc as bacc
    from concourse.bass_utils import run_bass_kernel_spmd

    i = {k: np.asarray(v) for k, v in inputs.items()}

    def columns(v):
        return v.reshape(-1, P).T

    key, query = np.arange(P)[:, None], np.arange(P)[None, :]
    diff = query - key
    seen = (diff >= 0) & (key // CHUNK == query // CHUNK)
    bits = np.stack([((diff >> j) & 1) * seen for j in range(5)] + [seen], 1).astype(np.float32)
    arrays = {
        "xT": i["x"].reshape(B * T, D).T, "cT": i["ctx_1024"].reshape(B * T, D).T,
        "mask": i["mask_BxS2_bf1"].view(np.uint8),
        "l0_Wq": i["L0_attn_W_q"], "l0_Wk": i["L0_attn_W_k"], "l0_WvT": i["L0_attn_W_v"].T,
        "l0_WgT": i["L0_attn_W_g"].T, "l0_WoT": i["L0_attn_W_o"].T,
        "log_decay": i["L0_attn_log_decay"].reshape(1, D),
        "Wq": i["L0_xattn_Wq"], "Wk": i["L0_xattn_Wk"], "Wv": i["L0_xattn_Wv"], "Wo": i["L0_xattn_Wo"],
        "bq": columns(i["L0_xattn_bq"]), "bk": columns(i["L0_xattn_bk"]), "bo": columns(i["L0_xattn_bo"]),
        "bv": columns(i["L0_xattn_bv"]),
        "fast_bT": i["L0_ffn_fast_b"].T, "wfcT": i["L0_ffn_w_fc"].T, "wprojT": i["L0_ffn_w_proj"].T,
        "uT": i["L0_ffn_u"].T, "v": i["L0_ffn_v"], "gate": i["L0_ffn_gate"].reshape(1, 1),
        "ident": np.eye(P, dtype=np.float32), "bits": bits,
    }
    nc = bacc.Bacc("TRN2", target_bir_lowering=False, num_devices=1)
    sent, aps = {}, {}
    for name, v in arrays.items():
        v = np.ascontiguousarray(v)
        sent[f"in_{name}"] = v
        aps[name] = nc.dram_tensor(f"in_{name}", v.shape, mybir.dt.from_np(v.dtype), kind="ExternalInput").ap()
    out = nc.dram_tensor("outT", (D, B * T), F32, kind="ExternalOutput").ap()
    decoder_layer(nc, aps, out)
    got = run_bass_kernel_spmd(nc, [sent], core_ids=[0]).results[0]["outT"]
    return got.T.reshape(B, T, D)
```
